# Optimizing a Trainium2 kernel written in Bass

```python
import numpy as np
import jax
import jax.numpy as jnp

def _softmax(x, axis=-1):
    return jax.nn.softmax(x, axis=axis)

def _gelu(x):
    return jax.nn.gelu(x, approximate=True)

def _silu(x):
    return jax.nn.silu(x)

def _sigmoid(x):
    return jax.nn.sigmoid(x)

def _layernorm(x, axis=-1, eps=1e-05):
    m = jnp.mean(x, axis=axis, keepdims=True)
    v = jnp.var(x, axis=axis, keepdims=True)
    return (x - m) / jnp.sqrt(v + eps)

def _scatter_add(tgt, idx, src, axis=0):
    return tgt.at[idx].add(src)

def _segment_sum(src, seg, n):
    return jax.ops.segment_sum(src, seg, n)
kernel_name = 'mk_gps_d1_gnn_r32_cb02fb'

def setup_inputs(seed: int=0):
    np.random.seed(seed)
    _w = jnp.asarray

    def _rec_inputs():
        import jax
        import jax.numpy as jnp
        _gk = jax.random.key(seed)
        x = -0.0003713 + 1 * jax.random.normal(jax.random.fold_in(_gk, 1), (3125, 256), jnp.float32)
        _s = jax.random.randint(jax.random.fold_in(_gk, 2), (25000,), 0, 3125, jnp.int32)
        _d = jax.random.randint(jax.random.fold_in(_gk, 3), (25000,), 0, 3125, jnp.int32)
        _loop = jnp.arange(3125, dtype=jnp.int32)
        src = jnp.concatenate([_s, _d, _loop])
        dst = jnp.concatenate([_d, _s, _loop])
        _o = jnp.argsort(dst, stable=True)
        src = src[_o]
        dst = dst[_o]
        return (x, src, dst)
    x, src, dst = _rec_inputs()

    def _L0_gnn_setup():
        import jax, jax.numpy as jnp
        import numpy as np
        N_NODES = 50000
        N_EDGES = 25000
        D = 256

        def _gcn_conv(x, edge_index, W, b):
            N = x.shape[0]
            loop = jnp.arange(N, dtype=edge_index.dtype)
            src = jnp.concatenate([edge_index[0], loop])
            dst = jnp.concatenate([edge_index[1], loop])
            deg = jax.ops.segment_sum(jnp.ones(src.shape, dtype=x.dtype), dst, num_segments=N)
            dinv = jnp.where(deg > 0, jax.lax.rsqrt(jnp.maximum(deg, 1.0)), 0.0)
            norm = dinv[src] * dinv[dst]
            h = x @ W.T
            msg = h[src] * norm[:, None]
            out = jax.ops.segment_sum(msg, dst, num_segments=N)
            return out + b
        key = jax.random.key(seed)
        k1, k2, k3 = jax.random.split(key, 3)
        node_features = jax.random.normal(k1, (N_NODES, D), dtype=jnp.float32)
        edge_index = jax.random.randint(k2, (2, N_EDGES), 0, N_NODES, dtype=jnp.int64)
        W = jax.random.normal(k3, (D, D), dtype=jnp.float32) * (1.0 / np.sqrt(D))
        b = jnp.zeros((D,), dtype=jnp.float32)
        alpha = jnp.full((1,), 0.5, dtype=jnp.float32)
        return {'node_features': node_features, 'edge_index': edge_index, 'W': W, 'b': b, 'alpha': alpha}
    _L0_gnn_all = _L0_gnn_setup()
    _L0_gnn_in = {k: v for k, v in _L0_gnn_all.items() if k in ('W', 'b', 'alpha')}
    del _L0_gnn_all

    def _L0_mix_setup():
        import jax, jax.numpy as jnp
        import numpy as np
        MIDC = 256
        HEADS = 8
        HEADC = MIDC // HEADS
        EPS = 1e-05

        def _ln(x, gamma, beta):
            mu = jnp.mean(x, axis=-1, keepdims=True)
            var = jnp.var(x, axis=-1, keepdims=True)
            return (x - mu) * jax.lax.rsqrt(var + EPS) * gamma + beta
        key = jax.random.key(seed)
        ks = jax.random.split(key, 8)
        B, HW, C = (8, 128, MIDC)
        s = 1.0 / np.sqrt(C)
        return {'x': jax.random.normal(ks[0], (B, HW, C), jnp.float32), 'w_qkv': jax.random.normal(ks[1], (C, 3 * C), jnp.float32) * s, 'b_qkv': jnp.zeros((3 * C,), jnp.float32), 'kln_g': jnp.ones((HEADC,), jnp.float32), 'kln_b': jnp.zeros((HEADC,), jnp.float32), 'vln_g': jnp.ones((HEADC,), jnp.float32), 'vln_b': jnp.zeros((HEADC,), jnp.float32), 'w1': jax.random.normal(ks[2], (C, C), jnp.float32) * s, 'b1': jnp.zeros((C,), jnp.float32), 'w2': jax.random.normal(ks[3], (C, C), jnp.float32) * s, 'b2': jnp.zeros((C,), jnp.float32)}
    _L0_mix_all = _L0_mix_setup()
    _L0_mix_in = {k: v for k, v in _L0_mix_all.items() if k in ('w_qkv', 'b_qkv', 'kln_g', 'kln_b', 'vln_g', 'vln_b', 'w1', 'b1', 'w2', 'b2')}
    del _L0_mix_all

    def _L0_ffn_setup():
        import jax, jax.numpy as jnp
        import numpy as np
        BN_EPS = 0.001

        def _bn(h, g, b, m, v):
            return g * (h - m) * jax.lax.rsqrt(v + BN_EPS) + b
        key = jax.random.key(seed)
        ks = jax.random.split(key, 8)
        B, F, Df = (256, 64, 256)
        E, H, D = (8, 256, 256)
        s1 = 1.0 / np.sqrt(Df)
        s2 = 1.0 / np.sqrt(H)
        return {'x': jax.random.normal(ks[0], (B, F, Df), jnp.float32), 'Wr': jax.random.normal(ks[1], (Df, E), jnp.float32) * s1, 'br': jnp.zeros((E,), jnp.float32), 'W1': jax.random.normal(ks[2], (E, Df, H), jnp.float32) * s1, 'b1': jnp.zeros((E, H), jnp.float32), 'g1': jnp.ones((E, H), jnp.float32), 'be1': jnp.zeros((E, H), jnp.float32), 'm1': jnp.zeros((E, H), jnp.float32), 'v1': jnp.ones((E, H), jnp.float32), 'W2': jax.random.normal(ks[3], (E, H, H), jnp.float32) * s2, 'b2': jnp.zeros((E, H), jnp.float32), 'g2': jnp.ones((E, H), jnp.float32), 'be2': jnp.zeros((E, H), jnp.float32), 'm2': jnp.zeros((E, H), jnp.float32), 'v2': jnp.ones((E, H), jnp.float32), 'Wo': jax.random.normal(ks[4], (E, H, D), jnp.float32) * s2, 'bo': jnp.zeros((E, D), jnp.float32)}
    _L0_ffn_all = _L0_ffn_setup()
    _L0_ffn_in = {k: v for k, v in _L0_ffn_all.items() if k in ('Wr', 'br', 'W1', 'b1', 'g1', 'be1', 'm1', 'v1', 'W2', 'b2', 'g2', 'be2', 'm2', 'v2', 'Wo', 'bo')}
    del _L0_ffn_all
    return {'x': x, 'src': src, 'dst': dst, 'L0_gnn_W': _L0_gnn_in['W'], 'L0_gnn_b': _L0_gnn_in['b'], 'L0_gnn_alpha': _L0_gnn_in['alpha'], 'L0_mix_w_qkv': _L0_mix_in['w_qkv'], 'L0_mix_b_qkv': _L0_mix_in['b_qkv'], 'L0_mix_kln_g': _L0_mix_in['kln_g'], 'L0_mix_kln_b': _L0_mix_in['kln_b'], 'L0_mix_vln_g': _L0_mix_in['vln_g'], 'L0_mix_vln_b': _L0_mix_in['vln_b'], 'L0_mix_w1': _L0_mix_in['w1'], 'L0_mix_b1': _L0_mix_in['b1'], 'L0_mix_w2': _L0_mix_in['w2'], 'L0_mix_b2': _L0_mix_in['b2'], 'L0_ffn_Wr': _L0_ffn_in['Wr'], 'L0_ffn_br': _L0_ffn_in['br'], 'L0_ffn_W1': _L0_ffn_in['W1'], 'L0_ffn_b1': _L0_ffn_in['b1'], 'L0_ffn_g1': _L0_ffn_in['g1'], 'L0_ffn_be1': _L0_ffn_in['be1'], 'L0_ffn_m1': _L0_ffn_in['m1'], 'L0_ffn_v1': _L0_ffn_in['v1'], 'L0_ffn_W2': _L0_ffn_in['W2'], 'L0_ffn_b2': _L0_ffn_in['b2'], 'L0_ffn_g2': _L0_ffn_in['g2'], 'L0_ffn_be2': _L0_ffn_in['be2'], 'L0_ffn_m2': _L0_ffn_in['m2'], 'L0_ffn_v2': _L0_ffn_in['v2'], 'L0_ffn_Wo': _L0_ffn_in['Wo'], 'L0_ffn_bo': _L0_ffn_in['bo']}

def reference(x, src, dst, L0_gnn_W, L0_gnn_b, L0_gnn_alpha, L0_mix_w_qkv, L0_mix_b_qkv, L0_mix_kln_g, L0_mix_kln_b, L0_mix_vln_g, L0_mix_vln_b, L0_mix_w1, L0_mix_b1, L0_mix_w2, L0_mix_b2, L0_ffn_Wr, L0_ffn_br, L0_ffn_W1, L0_ffn_b1, L0_ffn_g1, L0_ffn_be1, L0_ffn_m1, L0_ffn_v1, L0_ffn_W2, L0_ffn_b2, L0_ffn_g2, L0_ffn_be2, L0_ffn_m2, L0_ffn_v2, L0_ffn_Wo, L0_ffn_bo):
    import jax
    import jax.numpy as jnp

    def _L0_gnn_ref(node_features, edge_index, W, b, alpha):
        import jax, jax.numpy as jnp
        import numpy as np
        N_NODES = 50000
        N_EDGES = 25000
        D = 256

        def _gcn_conv(x, edge_index, W, b):
            N = x.shape[0]
            loop = jnp.arange(N, dtype=edge_index.dtype)
            src = jnp.concatenate([edge_index[0], loop])
            dst = jnp.concatenate([edge_index[1], loop])
            deg = jax.ops.segment_sum(jnp.ones(src.shape, dtype=x.dtype), dst, num_segments=N)
            dinv = jnp.where(deg > 0, jax.lax.rsqrt(jnp.maximum(deg, 1.0)), 0.0)
            norm = dinv[src] * dinv[dst]
            h = x @ W.T
            msg = h[src] * norm[:, None]
            out = jax.ops.segment_sum(msg, dst, num_segments=N)
            return out + b
        updated = _gcn_conv(node_features, edge_index, W, b)
        a = alpha[0]
        return a * node_features + (1.0 - a) * updated

    def _L0_mix_ref(x, w_qkv, b_qkv, kln_g, kln_b, vln_g, vln_b, w1, b1, w2, b2):
        import jax, jax.numpy as jnp
        import numpy as np
        MIDC = 256
        HEADS = 8
        HEADC = MIDC // HEADS
        EPS = 1e-05

        def _ln(x, gamma, beta):
            mu = jnp.mean(x, axis=-1, keepdims=True)
            var = jnp.var(x, axis=-1, keepdims=True)
            return (x - mu) * jax.lax.rsqrt(var + EPS) * gamma + beta
        B, HW, C = x.shape
        bias = x
        qkv = (x @ w_qkv + b_qkv).reshape(B, HW, HEADS, 3 * HEADC)
        qkv = qkv.transpose(0, 2, 1, 3)
        q, k, v = jnp.split(qkv, 3, axis=-1)
        k = _ln(k, kln_g, kln_b)
        v = _ln(v, vln_g, vln_b)
        kv = jnp.einsum('bhnd,bhne->bhde', k, v) / HW
        out = jnp.einsum('bhnd,bhde->bhne', q, kv)
        out = out.transpose(0, 2, 1, 3).reshape(B, HW, C)
        ret = out + bias
        h = jax.nn.gelu(ret @ w1 + b1, approximate=False)
        return h @ w2 + b2 + bias

    def _L0_ffn_ref(x, Wr, br, W1, b1, g1, be1, m1, v1, W2, b2, g2, be2, m2, v2, Wo, bo):
        import jax, jax.numpy as jnp
        import numpy as np
        BN_EPS = 0.001

        def _bn(h, g, b, m, v):
            return g * (h - m) * jax.lax.rsqrt(v + BN_EPS) + b
        feat = jnp.mean(x, axis=0)
        w = jax.nn.softmax(feat @ Wr + br, axis=-1)
        h = jnp.einsum('bfd,edh->bfeh', x, W1) + b1
        h = jax.nn.relu(_bn(h, g1, be1, m1, v1))
        h = jnp.einsum('bfeh,ehk->bfek', h, W2) + b2
        h = jax.nn.relu(_bn(h, g2, be2, m2, v2))
        y = jnp.einsum('bfeh,ehd->bfed', h, Wo) + bo
        return jnp.einsum('bfed,fe->bfd', y, w)
    edge_index = jnp.stack([src, dst])
    xn = _layernorm(x, axis=-1)
    x = x + _L0_gnn_ref(xn, edge_index, L0_gnn_W, L0_gnn_b, L0_gnn_alpha) + _L0_mix_ref(xn[None], L0_mix_w_qkv, L0_mix_b_qkv, L0_mix_kln_g, L0_mix_kln_b, L0_mix_vln_g, L0_mix_vln_b, L0_mix_w1, L0_mix_b1, L0_mix_w2, L0_mix_b2)[0]
    x = x + _L0_ffn_ref(_layernorm(x, axis=-1)[None], L0_ffn_Wr, L0_ffn_br, L0_ffn_W1, L0_ffn_b1, L0_ffn_g1, L0_ffn_be1, L0_ffn_m1, L0_ffn_v1, L0_ffn_W2, L0_ffn_b2, L0_ffn_g2, L0_ffn_be2, L0_ffn_m2, L0_ffn_v2, L0_ffn_Wo, L0_ffn_bo)[0]
    return x

_drawn_inputs = setup_inputs


def setup_inputs(seed=0):
    import zlib

    import numpy as np

    out = dict(_drawn_inputs(seed))
    spreads = {'L0_gnn_b': (0.0, 0.41),
     'L0_mix_b_qkv': (0.0, 0.318),
     'L0_mix_kln_g': (1.0, 0.6),
     'L0_mix_kln_b': (0.0, 0.544),
     'L0_mix_vln_g': (1.0, 0.6),
     'L0_mix_vln_b': (0.0, 0.481),
     'L0_mix_b1': (0.0, 0.315),
     'L0_mix_b2': (0.0, 0.1),
     'L0_ffn_br': (0.0, 0.586),
     'L0_ffn_b1': (0.0, 0.8),
     'L0_ffn_g1': (1.0, 0.6),
     'L0_ffn_be1': (0.0, 0.8),
     'L0_ffn_m1': (0.0, 0.8),
     'L0_ffn_v1': (1.0, 0.6),
     'L0_ffn_b2': (0.0, 0.577),
     'L0_ffn_g2': (1.0, 0.6),
     'L0_ffn_be2': (0.0, 0.61),
     'L0_ffn_m2': (0.0, 0.602),
     'L0_ffn_v2': (1.0, 0.6),
     'L0_ffn_bo': (0.0, 0.435)}
    factors = {}
    for name, (base, spread) in spreads.items():
        noise = np.random.default_rng([zlib.crc32(name.encode()), seed]).standard_normal(out[name].shape)
        drawn = base * np.exp(spread * noise) if base else spread * noise
        out[name] = jnp.asarray(drawn.astype(out[name].dtype))
    for name, factor in factors.items():
        out[name] = (out[name] * factor).astype(out[name].dtype)
    return out
```

```python
import numpy as np
import concourse.bass as bass
from concourse import mybir
from contextlib import ExitStack

N, D, E = 3125, 256, 53125
P = 112
NT = 28
NP = P * NT
TG = 4
NG = NT // TG
GN = TG * P
LAST = N - (NT - 1) * P
EXP = 8
HC = 32
NH2 = 2 * D // HC
EP, EC = 125, 425
CH = 25
NCH = EC // CH
CA, CB = NP // 64, 64
WIN = 2048
WS = WIN // 128
US = 8
SCALE = 2048.0
LN_EPS, BN_EPS = 1e-5, 1e-3
O_WT, O_KV, O_W1, O_W2, O_WR, O_WQ = 0, 256, 768, 1024, 1280, 1288
SW = 1544
R_VG, R_VB, R_BG, R_B2, R_BR, R_A, R_BKV = 0, 128, 256, 512, 768, 776, 777
RW = R_BKV + 512
M_ST, M_BC, M_FL, M_CM = 0, 64, 100, 128
DVE_LINKS = 4 * 4 + 4


def build(nc, x_d, edges_d, wffn_d, bn_d, wsm_d, col_d, row_d, bo_d, out_d):
    f32, f32r, f16, i32 = mybir.dt.float32, mybir.dt.float32r, mybir.dt.float16, mybir.dt.int32
    ACT = mybir.ActivationFunctionType
    ALU = mybir.AluOpType
    AX = mybir.AxisListType.X
    ds = bass.ds

    table_d = nc.dram_tensor("table_d", [NP, 2 * D], f16).ap()
    base_d = nc.dram_tensor("base_d", [NP, D], f32).ap()
    self_d = nc.dram_tensor("self_d", [NP, D], f32).ap()
    xnT_d = nc.dram_tensor("xnT_d", [NT, 128, 4 * P], f32).ap()
    cnt_d = nc.dram_tensor("cnt_d", [NP], f32).ap()

    ctx = ExitStack()
    with ctx:
        def sb(name, shape, dt, where=ctx):
            return where.enter_context(nc.sbuf_tensor(name, shape, dt))

        def sem(name):
            return ctx.enter_context(nc.semaphore(name))

        G = sb("G", [128, 2, US, 2 * D], f16)
        idx = sb("idx", [128, 2, WS], i32)
        win = sb("win", [128, NT, WS, 2], i32)
        oh = sb("oh", [128, 2, P, US], f16)
        dl = sb("dl", [128, WS], f16)
        iota_rep = sb("iota_rep", [128, P, US], f16)
        ident = sb("ident", [128, 128], f32)
        tbase = sb("tbase", [128, NT], f32)
        wgT = sb("wgT", [128, 2, 2, D], f32r)
        w2s = sb("w2s", [128, 2, 2, D], f32r)
        wms = sb("wms", [128, 2, 2, D], f32r)
        wrs = sb("wrs", [128, 2, 2, EXP], f32r)
        bnsc = sb("bnsc", [128, 2, EXP, 2], f32)
        bnbi = sb("bnbi", [128, 2, EXP, 2], f32)
        cm = sb("cm", [128, 2], f32)
        bo4 = sb("bo4", [32, TG, D], f32)
        rd = sb("rd", [P, NT], f32)
        br_b = sb("br_b", [P, EXP], f32)
        epsc = sb("epsc", [128, 1], f32)
        flag = sb("flag", [1, 1], i32)
        starts = sb("starts", [1, NT], i32)
        stbc = sb("stbc", [128, NT], f32)
        iotaP = sb("iotaP", [128, P], f32)

        pro = ExitStack()
        x_all = sb("x_all", [P, NT, D], f32, pro)
        edg = sb("edg", [EP, EC, 2], i32, pro)
        oneA = sb("oneA", [EP, 2, CA, CH], f16, pro)
        oneB = sb("oneB", [EP, 2, CB, CH], f16, pro)
        xn = sb("xn", [P, NT, D], f32, pro)
        iotaA = sb("iotaA", [EP, CA, CH], f16, pro)
        iotaB = sb("iotaB", [EP, CB, CH], f16, pro)
        ab_i = sb("ab_i", [EP, 2, EC], i32, pro)
        ab_f = sb("ab_f", [EP, 2, EC], f16, pro)
        posn = sb("posn", [EP, EC], f32, pro)
        viol = sb("viol", [EP, EC], f32, pro)
        wsm = sb("wsm", [128, 2, SW], f32, pro)
        pro_small = dict(
            col=[128, 6], rowv=[128, RW], bn=[128, 2, 5, EXP, 2], bntmp=[128, 2, EXP, 2],
            nxt=[EP, 2], vs=[EP, 2], cnt_ab=[CA, CB], cnt_t=[NT, P], tot=[NT, 2], ltri=[NT, NT],
            ones=[128, 128], stf=[1, NT], deg=[P, NT], dinv=[P, NT], dS=[P, NT], sd=[P, NT],
            bst=[P, 7, 6], mv=[P, NT, 2], rstd=[P, NT], nmr=[P, NT], a1=[P, 2], brow=[P, D],
            gm=[128, 2, NH2], gb=[1, NH2], bkv=[1, 512],
            sq=[P, 512], s2=[P, 2, NH2], kn=[P, 2, D], vn=[P, 2, 2, 130], xc=[P, 2, D],
            kvs=[128, 2, 128], kvt=[128, 2, 128], rT=[128, 2, D], rb=[128, 2],
        )
        T = {}
        for k, s in pro_small.items():
            T[k] = sb("p_" + k, s, i32 if k == "nxt" else f32, pro)
        wkv = sb("wkv", [128, 2, 2, 512], f32r, pro)
        bkvs = sb("bkvs", [1, 2, 512], f32r, pro)
        onesr = sb("onesr", [1, P], f32r, pro)
        xT = sb("xT", [128, 2, 2, 2, P], f32r, pro)
        xs32 = sb("xs32", [P, 2, 2, D], f32, pro)
        tb16 = sb("tb16", [P, 2, 2, 2, D], f16, pro)
        sf32 = sb("sf32", [P, 2, 2, D], f32, pro)
        fb_e = sb("fb_e", [EP, 2], i32, pro)
        fb_g = sb("fb_g", [EP, 2 * D], f16, pro)
        fb_o = sb("fb_o", [EP, P], f16, pro)
        fb_s = sb("fb_s", [EP, 8], f32, pro)
        fb_a = sb("fb_a", [P, D], f32, pro)
        fb_z = sb("fb_z", [EP, 512], f16, pro)
        wst = sb("wst", [128, 2, 3, 2, D], f32, pro)
        pro.close()

        whi = sb("whi", [128, EXP, 3, 2, D], f32r)
        wlo = sb("wlo", [128, EXP, 3, 2, D], f32r)
        h1 = sb("h1", [128, 2, 2, GN], f32r)
        h2 = sb("h2", [128, 2, 2, GN], f32r)
        t1 = sb("t1", [128, 2, GN], f32)
        t2 = sb("t2", [128, 2, GN], f32)
        x2T = sb("x2T", [128, 2, 2, GN], f32r)
        gT = sb("gT", [128, 2, 2, GN], f32r)
        xg = sb("xg", [128, TG, 2, 2, P], f32r)
        x1 = sb("x1", [P, TG, D], f32)
        acc = sb("acc", [P, TG, D], f32)
        bs = sb("bs", [P, 2, 2, D], f32)
        alo = sb("alo", [P, D], f32)
        ag1 = sb("ag1", [P, D], f32)
        ag2 = sb("ag2", [P, D], f32)
        aT = sb("aT", [128, 2, 2, P], f32r)
        bst2 = sb("bst2", [P, 6], f32)
        mv2 = sb("mv2", [P, TG, 2], f32)
        sd2 = sb("sd2", [P, TG], f32)
        rs2 = sb("rs2", [P, TG], f32)
        nm2 = sb("nm2", [P, TG], f32)
        xn2 = sb("xn2", [P, TG, D], f32)
        lg = sb("lg", [P, TG, EXP], f32)
        lg2 = sb("lg2", [P, TG, EXP], f32)
        mx = sb("mx", [P, TG], f32)
        sm = sb("sm", [P, TG], f32)
        wn = sb("wn", [P, TG, EXP], f32)
        wT = sb("wT", [TG * EXP, P], f32)

        B = [ctx.enter_context(nc.psum_tensor(f"bank{i}", [128, 512], f32)) for i in range(8)]
        TRP = [B[0], B[1]]
        KVP = [B[2], B[3]]
        KA, KS, CNT, MSC = B[4], B[5], B[6], B[7]
        H1P, H2P = [B[0], B[1]], [B[2], B[3]]
        YP = [B[4][:P, 0:D], B[4][:P, D:2 * D], B[5][:P, 0:D], B[5][:P, D:2 * D]]
        AGG = B[6]
        MP = B[7][:P, 0:D]
        MT = B[7][:, D:D + 2 * P]
        ML = B[7][:P, D + 2 * P:D + 2 * P + TG * EXP]

        S = {n: sem(n) for n in (
            "edges_in nxt_in x_in0 x_in1 x_in2 x_in3 wsm_in col_in row_in bn_in bo_in wst_in0 wst_in1 wst_free "
            "settled consts pool_link dve_link dve_loop_link "
            "ln_var ln_std ln_ready xn_ready one_ready one_free cnt_ps cnt_sb cnt_out cnt_in tot_sb cntT_ps "
            "start_ps starts_sb stf_sb flag_ps flag_sb deg_sb deg_sqrt dinv_sb base_ready base_out "
            "xs_ready xs_hi tb_ready tb_out0 tb_out1 sf_ready sf_out0 sf_out1 win_in idx_ready "
            "wkv_ready wrest_hi wrest_lo w_hi w_lo bn_v bn_sd bn_ready rT_ps rT_sb wm_ps wm_hi wm_lo pro_over "
            "xc_ready tr_ps xT_hi xT_lo xT_out0 xT_out1 kv_ps sq_ready s2_ready sd_ready kn_ready kv_sum kvs_sb "
            "fb_link fb_link2 fb_idx fb_gath fb_oh fb_mm fb_sum fb_res fb_add fb_over "
            "gath0 gath1 dl_ready unit_done oh_ready agg_evac alo_ready ag_ready "
            "mt_ps mt_hi mt_lo mp_ps mp_free st_ready var_ready std_ready rs_ready nmr_ready xn2_ready "
            "g_ps g_act g_hi g_lo r_ps r_lg r_max r_sub r_exp r_sum w_ready xg_in bs_in0 bs_in1 "
            "l1_ps l1_act l1_hi l1_lo l2_ps l2_act l2_hi l2_lo y_ps y_used out_sent"
        ).split()}

        block = ctx.enter_context(nc.Block())

        def after(eng, name, value):
            if not isinstance(value, int) or value > 0:
                eng.wait_ge(S[name], value)

        def settle(eng):
            eng.sem_inc(S["settled"], 1)

        def bc_out(ap, n):
            return ap.rearrange("p (o m) -> p o m", o=1).to_broadcast([ap.shape[0], n, ap.shape[1]])

        def bc_in(ap, m):
            return ap.rearrange("p (n o) -> p n o", o=1).to_broadcast([ap.shape[0], ap.shape[1], m])

        T_AT, X_AT = (0, 1, 2, 5), (3, 4, 6, 7)
        MP_BEFORE = (0, 1, 2, 3, 3, 3, 3, 4)
        MT_BEFORE = (1, 2, 3, 7)

        @block.sync
        def _(sp):
            e3 = edges_d.rearrange("(p j) two -> p j two", p=EP)
            sp.dma_start(edg[:, :, :], e3).then_inc(S["edges_in"], 16)
            xv = x_d.rearrange("(t p) d -> p t d", p=P)
            for i in range(4):
                sp.dma_start(x_all[:, 7 * i:7 * i + 7, :], xv[:, 7 * i:7 * i + 7, :]).then_inc(S[f"x_in{i}"], 16)
            sp.dma_start(T["nxt"][0:EP - 1, :], e3[1:EP, 0, :]).then_inc(S["nxt_in"], 16)
            sp.dma_start(T["rowv"][:, :], row_d.to_broadcast([128, RW])).then_inc(S["row_in"], 16)
            sp.dma_start(T["bn"][:, :, :, :, :], bn_d).then_inc(S["bn_in"], 16)
            sp.dma_start(T["col"][:, :], col_d).then_inc(S["col_in"], 16)
            sp.dma_start(wsm[:, :, :], wsm_d).then_inc(S["wsm_in"], 16)
            sp.wait_ge(S["consts"], 1)
            for t in range(TG):
                sp.dma_start(bo4[EXP * t:EXP * t + EXP, t, :], bo_d).then_inc(S["bo_in"], 16)
            for e in range(2):
                sp.dma_start(wst[:, e, :, :, :], wffn_d[:, e, :, :, :]).then_inc(S[f"wst_in{e}"], 16)
            sp.wait_ge(S["cnt_sb"], 1)
            sp.dma_start(cnt_d.rearrange("(a b) -> a b", b=CB), T["cnt_ab"][:, :]).then_inc(S["cnt_out"], 16)
            sp.wait_ge(S["cnt_out"], 16)
            sp.dma_start(T["cnt_t"][:, :], cnt_d.rearrange("(t p) -> t p", p=P)).then_inc(S["cnt_in"], 16)
            ef = edges_d.rearrange("e two -> (e two)")
            sp.wait_ge(S["starts_sb"], 1)
            with sp.Fori(0, NT) as t:
                v = sp.value_load(starts[0:1, ds(t, 1)], min_val=0, max_val=E - WIN)
                sp.dma_start(win[:, ds(t, 1), :, :].rearrange("p o s two -> p o (s two)"),
                             ef[ds(v * 2, 2 * WIN)].rearrange("(p o k) -> p o k", p=128, o=1))\
                    .then_inc(S["win_in"], 16)
                sp.wait_ge(S["win_in"], (t + 1) * 16)
                settle(sp)
            for e in range(2, EXP):
                sp.wait_ge(S["wst_free"], e - 1)
                sp.dma_start(wst[:, e % 2, :, :, :], wffn_d[:, e, :, :, :]).then_inc(S[f"wst_in{e % 2}"], 16)

            def load_base(t, k):
                settle(sp)
                sp.dma_start(bs[:, k, 0, :], base_d[ds(t * P, P), :]).then_inc(S[f"bs_in{k}"], 16)
                sp.dma_start(bs[:, k, 1, :], self_d[ds(t * P, P), :]).then_inc(S[f"bs_in{k}"], 16)

            def load_xg(q):
                settle(sp)
                sp.dma_start(xg[:, :, :, :, :].rearrange("p t h c n -> p t (h c n)").bitcast(f32),
                             xnT_d[ds(q * TG, TG), :, :].rearrange("t p n -> p t n")).then_inc(S["xg_in"], 16)

            sp.wait_ge(S["fb_over"], 1)
            sp.wait_ge(S["pro_over"], 3)
            for k in range(2):
                sp.wait_ge(S[f"xT_out{k}"], 16 * (NT // 2))
            load_xg(0)
            for t in range(2):
                load_base(t, t % 2)

            def group_loads(q, tiles):
                for t in range(tiles):
                    sp.wait_ge(S["mp_free"], q * 8 + (t + 1))
                    load_base(q * TG + (t + 2), t % 2)

            sp.wait_ge(S["g_ps"], 2)
            load_xg(1)
            group_loads(0, TG)
            ov = out_d.rearrange("(g t p) d -> g p t d", t=TG, p=P)

            def store(g):
                sp.wait_ge(S["y_used"], (g + 1) * (EXP * TG))
                settle(sp)
                sp.dma_start(ov[ds(g, 1)].rearrange("g p t d -> p (g t) d"), acc[:, :, :]).then_inc(S["out_sent"], 16)

            with sp.Fori(0, NG - 2) as g:
                sp.wait_ge(S["g_ps"], g * 2 + 4)
                load_xg(g + 2)
                group_loads(g + 1, TG)
                store(g)
            group_loads(NG - 1, 2)
            store(NG - 2)
            store(NG - 1)
            sp.wait_ge(S["out_sent"], NG * 16)

        @block.gpsimd
        def _(pool):
            n = [0]

            def link(ins):
                n[0] += 1
                ins.then_inc(S["pool_link"], 1)
                pool.wait_ge(S["pool_link"], n[0])

            pool.memset(bo4[:, :, :], 0.0).then_inc(S["consts"], 1)
            for dst, m in ((iotaA, CA), (iotaB, CB), (iota_rep, P)):
                pool.iota(dst[:, :, :], [[1, m], [0, dst.shape[2]]], base=0, channel_multiplier=0,
                          allow_small_or_imprecise_dtypes=True).then_inc(S["consts"], 1)
            pool.iota(tbase[:, :], [[P, NT]], base=0, channel_multiplier=0,
                      allow_small_or_imprecise_dtypes=True).then_inc(S["consts"], 1)
            pool.iota(iotaP[:, :], [[1, P]], base=0, channel_multiplier=0,
                      allow_small_or_imprecise_dtypes=True).then_inc(S["consts"], 1)
            link(pool.memset(ident[:, :], 0.0))
            pool.affine_select(out=ident[:, :], in_=ident[:, :], compare_op=ALU.not_equal, fill=1.0, base=0,
                               pattern=[[-1, 128]], channel_multiplier=1).then_inc(S["consts"], 1)
            link(pool.memset(T["ltri"][:, :], 1.0))
            pool.affine_select(out=T["ltri"][:, :], in_=T["ltri"][:, :], compare_op=ALU.is_gt, fill=0.0, base=0,
                               pattern=[[1, NT]], channel_multiplier=-1).then_inc(S["consts"], 1)
            pool.memset(T["ones"][:, :], 1.0).then_inc(S["consts"], 1)
            pool.memset(T["vn"][:, :, :, :], 1.0).then_inc(S["consts"], 1)
            pool.memset(fb_z[:, :], 0.0).then_inc(S["consts"], 1)
            pool.memset(epsc[:, :], LN_EPS).then_inc(S["consts"], 1)
            pool.memset(T["kvs"][:, :, :], 0.0).then_inc(S["consts"], 1)
            pool.iota(posn[:, :], [[1, EC]], base=0, channel_multiplier=EC,
                      allow_small_or_imprecise_dtypes=True).then_inc(S["consts"], 1)
            pool.wait_ge(S["row_in"], 16)
            link(pool.tensor_scalar(T["a1"][:, 0:1], T["rowv"][:P, R_A:R_A + 1], 1.0, None, ALU.add))
            link(pool.tensor_scalar(T["a1"][:, 1:2], T["rowv"][:P, R_A:R_A + 1], -1.0, 1.0, ALU.mult, ALU.add))
            link(pool.tensor_scalar(T["brow"][:, :], T["rowv"][:P, R_BG:R_BG + D], T["a1"][:, 1:2], None, ALU.mult))
            link(pool.tensor_tensor(T["brow"][:, :], T["brow"][:, :], T["rowv"][:P, R_B2:R_B2 + D], ALU.add))
            pool.tensor_copy(br_b[:, :], T["rowv"][:P, R_BR:R_BR + EXP]).then_inc(S["consts"], 1)
            bv = base_d.rearrange("(t p) d -> p t d", p=P)
            for i in range(4):
                pool.wait_ge(S["xn_ready"], 7 * i + 7)
                q = x_all[:, 7 * i:7 * i + 7, :]
                link(pool.tensor_tensor(q, q, bc_out(T["brow"][:, :], 7), ALU.add))
                for t in range(7 * i, 7 * i + 7):
                    link(pool.tensor_scalar(sf32[:, t % 2, 0, :], xn[:, t, :], T["a1"][:, 0:1], None, ALU.mult))
                    link(pool.tensor_tensor(x_all[:, t, :], x_all[:, t, :], sf32[:, t % 2, 0, :], ALU.add))
                pool.dma_start(bv[:, 7 * i:7 * i + 7, :], q).then_inc(S["base_out"], 16)
            pool.sem_inc(S["base_ready"], 1)

            def gather_unit(u, k):
                settle(pool)
                for s in range(US):
                    pool.indirect_dma_start(
                        G[:, u, s, :], None, table_d,
                        bass.IndirectOffsetOnAxis(ap=idx[:, k, u * US + s:u * US + s + 1], axis=0),
                    ).then_inc(S[f"gath{u}"], 16)

            def tile_index(t, k):
                pool.wait_ge(S["win_in"], (t + 1) * 16)
                pool.tensor_copy(idx[:, k:k + 1, :], win[:, ds(t, 1), :, 0]).then_inc(S["idx_ready"], 1)

            tile_index(0, 0)
            pool.wait_ge(S["tb_out0"], 16 * (NT // 4))
            pool.wait_ge(S["tb_out1"], 16 * (NT // 4))
            pool.wait_ge(S["idx_ready"], 1)
            gather_unit(0, 0)
            tile_index(1, 1)
            gather_unit(1, 0)

            pool.wait_ge(S["sf_out0"], 16 * (NT // 4))
            pool.wait_ge(S["sf_out1"], 16 * (NT // 4))
            pool.wait_ge(S["base_out"], 64)
            pool.wait_ge(S["flag_sb"], 1)
            needed = pool.value_load(flag[0:1, 0:1], min_val=0, max_val=1)
            with pool.If(needed > 0):
                with pool.Fori(0, NT) as t:
                    with pool.Fori(0, EC) as j:
                        pool.wait_ge(S["fb_mm"], t * EC + j)
                        pool.tensor_copy(fb_e[:, :], edg[:, ds(j, 1), :].rearrange("p o two -> p (o two)"))\
                            .then_inc(S["fb_idx"], 1)
                        pool.wait_ge(S["fb_idx"], t * EC + (j + 1))
                        settle(pool)
                        pool.indirect_dma_start(fb_g[:, :], None, table_d,
                                                bass.IndirectOffsetOnAxis(ap=fb_e[:, 0:1], axis=0))\
                            .then_inc(S["fb_gath"], 16)
                    pool.wait_ge(S["fb_res"], t + 1)
                    pool.dma_start(self_d[ds(t * P, P), :], fb_a[:, :], accum_op=ALU.add).then_inc(S["fb_add"], 16)
                    pool.wait_ge(S["fb_add"], (t + 1) * 16)
            pool.sem_inc(S["fb_over"], 1)

            def tile_gathers(t, k, more):
                pool.wait_ge(S["idx_ready"], t + 1)
                pool.wait_ge(S["unit_done"], t * 2 - 1)
                gather_unit(0, k)
                pool.wait_ge(S["unit_done"], t * 2)
                if more:
                    tile_index(t + 1, 1 - k)
                gather_unit(1, k)

            with pool.Fori(0, NT // 2 - 1) as i:
                tile_gathers(i * 2 + 1, 1, True)
                tile_gathers(i * 2 + 2, 0, True)
            tile_gathers(NT - 1, 1, False)

        @block.scalar
        def _(act):
            act.wait_ge(S["consts"], 12)
            for i in range(4):
                act.wait_ge(S["ln_var"], 7 * i + 7)
                act.activation(T["rstd"][:, 7 * i:7 * i + 7], T["mv"][:, 7 * i:7 * i + 7, 1], ACT.Sqrt,
                               bias=epsc[:P, :]).then_inc(S["ln_std"], 1)
                act.wait_ge(S["ln_ready"], i + 1)
                with act.Fori(7 * i, 7 * i + 7) as t:
                    act.activation(xn[:, ds(t, 1), :], x_all[:, ds(t, 1), :], ACT.Identity,
                                   bias=T["nmr"][:, ds(t, 1)], scale=T["rstd"][:, ds(t, 1)])\
                        .then_inc(S["xn_ready"], 1)
            act.wait_ge(S["bn_v"], 1)
            act.activation(T["bntmp"][:, :, :, :], T["bntmp"][:, :, :, :], ACT.Sqrt).then_inc(S["bn_sd"], 1)
            act.wait_ge(S["wkv_ready"], 2)
            act.activation(wkv[:, 0, :, :], wsm[:, :, O_KV:O_KV + 512], ACT.Copy).then_inc(S["wrest_hi"], 1)
            act.activation(bkvs[:, 0, :], T["bkv"][:, :], ACT.Copy).then_inc(S["wrest_hi"], 1)
            act.activation(onesr[:, :], T["ones"][0:1, 0:P], ACT.Copy).then_inc(S["wrest_hi"], 1)
            for w, o, m in ((wgT, O_WT, D), (w2s, O_W2, D), (wrs, O_WR, EXP)):
                act.activation(w[:, 0, :, :], wsm[:, :, o:o + m], ACT.Copy).then_inc(S["wrest_hi"], 1)
            act.wait_ge(S["cnt_ps"], 1)
            act.activation(T["cnt_ab"][:, :], CNT[:CA, 0:CB], ACT.Copy).then_inc(S["cnt_sb"], 1)
            act.wait_ge(S["deg_sb"], 1)
            act.activation(T["deg"][:, :], T["deg"][:, :], ACT.Sqrt).then_inc(S["deg_sqrt"], 1)
            act.wait_ge(S["dinv_sb"], 1)
            act.wait_ge(S["base_ready"], 1)

            def table_pair(i, k):
                act.wait_ge(S["xs_ready"], i * 2 + (k + 1))
                after(act, f"tb_out{k}", i * 16)
                act.activation(tb16[:, k, :, 0, :], xs32[:, k, :, :], ACT.Copy).then_inc(S["xs_hi"], 1)
                after(act, f"sf_out{k}", i * 16)
                for m in range(2):
                    t = i * 4 + (2 * k + m)
                    act.activation(sf32[:, k, m:m + 1, :], xn[:, ds(t, 1), :],
                                   ACT.Copy, scale=T["sd"][:, ds(t, 1)]).then_inc(S["sf_ready"], 1)
                act.wait_ge(S["tb_ready"], i * 2 + (k + 1))
                rows = ds(i * (4 * P) + 2 * k * P, 2 * P)
                act.dma_start(table_d[rows, :].rearrange("(m p) d -> p m d", p=P),
                              tb16[:, k, :, :, :].rearrange("p m h d -> p m (h d)")).then_inc(S[f"tb_out{k}"], 16)
                act.wait_ge(S["sf_ready"], i * 4 + (2 * k + 2))
                act.dma_start(self_d[rows, :].rearrange("(m p) d -> p m d", p=P),
                              sf32[:, k, :, :]).then_inc(S[f"sf_out{k}"], 16)

            with act.Fori(0, NT // 4) as i:
                for k in range(2):
                    table_pair(i, k)

            def kv_copy(t, k):
                after(act, "tr_ps", t - 1)
                act.activation(T["xc"][:, k:k + 1, :], xn[:, ds(t, 1), :], ACT.Copy).then_inc(S["xc_ready"], 1)

            def kv_high(t, k, i):
                act.wait_ge(S["tr_ps"], t + 1)
                after(act, "kv_ps", t - 1)
                after(act, f"xT_out{k}", i * 16)
                act.activation(xT[:, k, 0, :, :], TRP[k][:, 0:2 * P].rearrange("p (c n) -> p c n", c=2), ACT.Copy)\
                    .then_inc(S["xT_hi"], 1)

            def kv_square(t, k):
                act.wait_ge(S["kv_ps"], t + 1)
                after(act, "s2_ready", t)
                act.activation(T["sq"][:, :], KVP[k][:P, :], ACT.Square).then_inc(S["sq_ready"], 1)
                act.wait_ge(S["xT_lo"], t + 1)
                act.dma_start(xnT_d[ds(t, 1), :, :].rearrange("o p n -> p o n"),
                              xT[:, k, :, :, :].rearrange("p (o h) c n -> p o (h c n)", o=1).bitcast(f32))\
                    .then_inc(S[f"xT_out{k}"], 16)
                act.wait_ge(S["s2_ready"], t + 1)
                after(act, "kn_ready", 2 * t)
                act.activation(T["s2"][:, 1, :], T["s2"][:, 0, :], ACT.Sqrt, bias=epsc[:P, :], scale=1.0 / HC)\
                    .then_inc(S["sd_ready"], 1)

            def kv_turn(t, k, i):
                if not isinstance(t, int) or t + 1 < NT:
                    kv_copy(t + 1, 1 - k)
                if not isinstance(t, int) or t < NT:
                    kv_high(t, k, i)
                if not isinstance(t, int) or t >= 1:
                    kv_square(t - 1, 1 - k)

            kv_copy(0, 0)
            kv_turn(0, 0, 0)
            kv_turn(1, 1, 0)
            with act.Fori(1, NT // 2 - 1) as i:
                kv_turn(i * 2, 0, i)
                kv_turn(i * 2 + 1, 1, i)
            for t in range(NT - 2, NT + 1):
                kv_turn(t, t % 2, t // 2)
            act.wait_ge(S["wm_ps"], 1)
            for c in range(2):
                act.activation(wms[:, 0, c, :], KVP[c][:, 0:D], ACT.Copy).then_inc(S["wm_hi"], 1)
            act.sem_inc(S["pro_over"], 1)
            act.wait_ge(S["pro_over"], 3)
            act.wait_ge(S["fb_over"], 1)
            for k in range(2):
                act.wait_ge(S[f"xT_out{k}"], 16 * (NT // 2))
            for e in range(EXP):
                act.wait_ge(S[f"wst_in{e % 2}"], 16 * (e // 2 + 1))
                act.activation(whi[:, e, :, :, :], wst[:, e % 2, :, :, :], ACT.Copy).then_inc(S["w_hi"], 1)

            def expert_relu(l, g, e, mlp_before=False):
                name, buf, banks = (("l1", t1, H1P), ("l2", t2, H2P))[l]
                m = g * EXP + e
                after(act, name + "_lo", m)
                if mlp_before:
                    act.wait_ge(S["g_lo"], g + 2 if e else g + 1)
                for c in range(2):
                    act.wait_ge(S[name + "_ps"], m * 2 + (c + 1))
                    act.activation(buf[:, c, :], banks[c][:, 0:GN], ACT.Relu, bias=bnbi[:, l, e, c:c + 1],
                                   scale=bnsc[:, l, e, c:c + 1]).then_inc(S[name + "_act"], 1)

            def expert_high(l, g, e):
                name, buf, hi = (("l1", t1, h1), ("l2", t2, h2))[l]
                m = g * EXP + e
                act.wait_ge(S[name + "_act"], m * 2 + 2)
                if l:
                    after(act, "y_ps", m * TG)
                act.activation(hi[:, 0, :, :], buf[:, :, :], ACT.Copy).then_inc(S[name + "_hi"], 1)

            def mlp(q):
                after(act, "l1_lo", (q - 1) * EXP + 1)
                for c in range(2):
                    act.wait_ge(S["g_ps"], q * 2 + (c + 1))
                    act.activation(t1[:, c, :], H1P[c][:, 0:GN], ACT.Gelu, bias=cm[:, c:c + 1]).then_inc(S["g_act"], 1)
                act.wait_ge(S["g_act"], q * 2 + 2)
                after(act, "mp_ps", q * 8 - 4)
                act.activation(gT[:, 0, :, :], t1[:, :, :], ACT.Copy).then_inc(S["g_hi"], 1)

            def agg_low(q, t):
                act.wait_ge(S["unit_done"], q * 8 + (2 * t + 2))
                after(act, "agg_evac", q * TG + t)
                act.activation(alo[:, :], AGG[:P, D:2 * D], ACT.Copy,
                               scale=rd[:, ds(q * TG + t, 1)]).then_inc(S["alo_ready"], 1)

            def mt_high(q, at, dst):
                act.wait_ge(S["mt_ps"], q * 9 + (at + 1))
                act.activation(dst, MT[:, :].rearrange("p (c n) -> p c n", c=2), ACT.Copy).then_inc(S["mt_hi"], 1)

            def agg_high(q, t):
                after(act, "mp_ps", q * 8 + t if t else q * 8 - 4)
                mt_high(q, T_AT[t], aT[:, 0, :, :])

            def x2_high(q, t):
                after(act, "l1_ps", q * 16)
                mt_high(q, X_AT[t], x2T[:, 0, :, t * P:t * P + P])

            def norm(q, t):
                act.wait_ge(S["var_ready"], q * TG + (t + 1))
                act.activation(sd2[:, t:t + 1], mv2[:, t, 1:2], ACT.Sqrt, bias=epsc[:P, :]).then_inc(S["std_ready"], 1)
                act.wait_ge(S["nmr_ready"], q * TG + (t + 1))
                act.activation(xn2[:, t, :], x1[:, t, :], ACT.Identity, bias=nm2[:, t:t + 1],
                               scale=rs2[:, t:t + 1]).then_inc(S["xn2_ready"], 1)

            def softmax(q):
                act.wait_ge(S["r_sub"], q + 1)
                act.activation(lg2[:, :, :], lg[:, :, :], ACT.Exp).then_inc(S["r_exp"], 1)

            mlp(0)
            agg_low(0, 0)
            agg_high(0, 0)
            agg_low(0, 1)
            agg_high(0, 1)
            norm(0, 0)
            agg_low(0, 2)
            agg_high(0, 2)
            norm(0, 1)
            agg_low(0, 3)
            norm(0, 2)
            x2_high(0, 0)
            x2_high(0, 1)
            agg_high(0, 3)
            x2_high(0, 2)
            norm(0, 3)
            x2_high(0, 3)
            softmax(0)

            def group(g, prepare):
                q = g + 1
                expert_relu(0, g, 0, True)
                expert_high(0, g, 0)
                if prepare:
                    mlp(q)
                expert_relu(0, g, 1, prepare)
                expert_relu(1, g, 0)
                expert_high(0, g, 1)
                expert_high(1, g, 0)
                for e in range(1, EXP):
                    if prepare and e % 2:
                        agg_low(q, e // 2)
                    if e < EXP - 1:
                        expert_relu(0, g, e + 1)
                    elif prepare:
                        x2_high(q, 1)
                    expert_relu(1, g, e)
                    if e < EXP - 1:
                        expert_high(0, g, e + 1)
                    elif prepare:
                        agg_high(q, 3)
                    expert_high(1, g, e)
                    if prepare:
                        if e in (1, 3, 5):
                            agg_high(q, e // 2)
                        if e in (2, 4):
                            norm(q, e // 2 - 1)
                        if e == 6:
                            x2_high(q, 0)
                            norm(q, 2)
                        if e == 7:
                            x2_high(q, 2)
                            norm(q, 3)
                if prepare:
                    x2_high(q, 3)
                    softmax(q)

            with act.Fori(0, NG - 1) as g:
                group(g, True)
            group(NG - 1, False)

        @block.vector
        def _(dve):
            n = [0]

            def link(ins):
                n[0] += 1
                ins.then_inc(S["dve_link"], 1)
                dve.wait_ge(S["dve_link"], n[0])

            dve.wait_ge(S["edges_in"], 16)
            dve.wait_ge(S["nxt_in"], 16)
            dst = edg[:, :, 1]
            dve.tensor_scalar(ab_i[:, 0, :], dst, 6, None, ALU.logical_shift_right)
            link(dve.tensor_scalar(ab_i[:, 1, :], dst, 63, None, ALU.bitwise_and))
            dve.tensor_copy(ab_f[:, :, :], ab_i[:, :, :])
            link(dve.memset(viol[:, :], 0.0))
            dve.tensor_tensor(viol[:, 0:EC - 1], edg[:, 0:EC - 1, 1], edg[:, 1:EC, 1], ALU.is_gt)
            link(dve.tensor_tensor(viol[0:EP - 1, EC - 1:EC], edg[0:EP - 1, EC - 1, 1:2], T["nxt"][0:EP - 1, 1:2],
                                   ALU.is_gt))
            link(dve.reduce_sum(T["vs"][:, 0:1], viol[:, :], axis=AX))
            for i in range(4):
                dve.wait_ge(S[f"x_in{i}"], 16)
                after(dve, "ln_var", 7 * i)
                for t in range(7):
                    ins = dve.bn_stats(T["bst"][:, t, :], x_all[:, 7 * i + t, :])
                link(ins)
                for t in range(7):
                    dve.bn_aggr(T["mv"][:, 7 * i + t, :], T["bst"][:, t, :]).then_inc(S["ln_var"], 1)
            for i in range(4):
                w = slice(7 * i, 7 * i + 7)
                dve.wait_ge(S["ln_std"], i + 1)
                link(dve.reciprocal(T["rstd"][:, w], T["rstd"][:, w]))
                dve.scalar_tensor_tensor(out=T["nmr"][:, w], in0=T["mv"][:, w, 0], scalar=-1.0, in1=T["rstd"][:, w],
                                         op0=ALU.mult, op1=ALU.mult).then_inc(S["ln_ready"], 1)
            dve.wait_ge(S["bn_in"], 16)
            bnv = T["bn"]
            dve.tensor_scalar(T["bntmp"][:, :, :, :], bnv[:, :, 4, :, :], BN_EPS, None, ALU.add).then_inc(S["bn_v"], 1)

            def one_hots(c, k):
                after(dve, "one_free", c - 1)
                dve.tensor_tensor(oneA[:, k, :, :], iotaA[:, :, :],
                                  ab_f[:, 0, ds(c * CH, CH)].rearrange("p (o m) -> p o m", o=1)
                                  .to_broadcast([EP, CA, CH]), ALU.is_equal).then_inc(S["one_ready"], 1)
                dve.tensor_tensor(oneB[:, k, :, :], iotaB[:, :, :],
                                  ab_f[:, 1, ds(c * CH, CH)].rearrange("p (o m) -> p o m", o=1)
                                  .to_broadcast([EP, CB, CH]), ALU.is_equal).then_inc(S["one_ready"], 1)

            dve.wait_ge(S["consts"], 15)
            one_hots(0, 0)
            with dve.Fori(0, NCH // 2) as i:
                one_hots(i * 2 + 1, 1)
                one_hots(i * 2 + 2, 0)

            dve.wait_ge(S["bn_sd"], 1)
            link(dve.reciprocal(T["bntmp"][:, :, :, :], T["bntmp"][:, :, :, :]))
            link(dve.tensor_tensor(bnsc[:, :, :, :], T["bntmp"][:, :, :, :], bnv[:, :, 1, :, :], ALU.mult))
            link(dve.tensor_tensor(T["bntmp"][:, :, :, :], bnv[:, :, 0, :, :], bnv[:, :, 3, :, :], ALU.subtract))
            link(dve.tensor_tensor(T["bntmp"][:, :, :, :], T["bntmp"][:, :, :, :], bnsc[:, :, :, :], ALU.mult))
            dve.tensor_tensor(bnbi[:, :, :, :], T["bntmp"][:, :, :, :], bnv[:, :, 2, :, :], ALU.add)\
                .then_inc(S["bn_ready"], 1)
            dve.wait_ge(S["wsm_in"], 16)
            for c in range(2):
                wv = wsm[:, c, O_KV:O_KV + 512].rearrange("p (h d) -> p h d", d=HC)
                link(dve.reduce_sum(T["gm"][:, c, :], wv, axis=AX))
                link(dve.tensor_scalar(T["gm"][:, c, :], T["gm"][:, c, :], -1.0 / HC, None, ALU.mult))
                ins = dve.tensor_tensor(wv, wv, bc_in(T["gm"][:, c, :], HC), ALU.add)
                if c == 0:
                    link(ins)
                else:
                    ins.then_inc(S["wkv_ready"], 1)
            brow_v = T["rowv"][0:1, R_BKV:R_BKV + 512].rearrange("p (h d) -> p h d", d=HC)
            link(dve.reduce_sum(T["gb"][:, :], brow_v, axis=AX))
            link(dve.tensor_scalar(T["gb"][:, :], T["gb"][:, :], -1.0 / HC, None, ALU.mult))
            dve.tensor_tensor(T["bkv"][:, :].rearrange("p (h d) -> p h d", d=HC), brow_v, bc_in(T["gb"][:, :], HC),
                              ALU.add).then_inc(S["wkv_ready"], 1)

            dve.wait_ge(S["cnt_in"], 16)
            link(dve.reduce_sum(T["tot"][:, 0:1], T["cnt_t"][:, :], axis=AX))
            dve.tensor_scalar(T["tot"][:, 1:2], T["tot"][:, 0:1], float(WIN), None, ALU.is_gt).then_inc(S["tot_sb"], 1)
            dve.wait_ge(S["cntT_ps"], 1)
            link(dve.tensor_scalar(T["deg"][:, :], CNT[:P, 128:128 + NT], 1.0, None, ALU.add))
            dve.tensor_scalar(T["deg"][:, :], T["deg"][:, :], 1.0, None, ALU.max).then_inc(S["deg_sb"], 1)
            dve.wait_ge(S["start_ps"], 1)
            dve.tensor_scalar(starts[:, :], MSC[0:1, M_ST:M_ST + NT], float(E - WIN), None, ALU.min)\
                .then_inc(S["starts_sb"], 1)
            dve.tensor_scalar(T["stf"][:, :], MSC[0:1, M_ST:M_ST + NT], float(E - WIN), None, ALU.min)\
                .then_inc(S["stf_sb"], 1)
            dve.wait_ge(S["deg_sqrt"], 1)
            link(dve.reciprocal(T["dinv"][:, :], T["deg"][:, :]))
            link(dve.tensor_scalar(T["dS"][:, :], T["dinv"][:, :], SCALE, None, ALU.mult))
            link(dve.tensor_scalar(T["rstd"][:, :], T["dinv"][:, :], T["a1"][:, 1:2], None, ALU.mult))
            link(dve.tensor_scalar(rd[:, :], T["rstd"][:, :], 1.0 / SCALE, None, ALU.mult))
            dve.tensor_tensor(T["sd"][:, :], T["dinv"][:, :], T["rstd"][:, :], ALU.mult).then_inc(S["dinv_sb"], 1)

            with dve.Fori(0, NT // 4) as i:
                dve.wait_ge(S["tb_ready"], i * 2)
                for k in range(2):
                    for m in range(2):
                        t = i * 4 + (2 * k + m)
                        ins = dve.tensor_scalar(xs32[:, k, m:m + 1, :], xn[:, ds(t, 1), :], T["dS"][:, ds(t, 1)],
                                                None, ALU.mult)
                    ins.then_inc(S["xs_ready"], 1)
                for k in range(2):
                    dve.wait_ge(S["xs_hi"], i * 2 + (k + 1))
                    dve.tensor_tensor(tb16[:, k, :, 1, :], xs32[:, k, :, :], tb16[:, k, :, 0, :], ALU.subtract)\
                        .then_inc(S["tb_ready"], 1)
            dve.wait_ge(S["flag_ps"], 1)
            dve.tensor_copy(stbc[:, :], MSC[:, M_BC:M_BC + NT])
            dve.tensor_scalar(flag[:, :], MSC[0:1, M_FL:M_FL + 1], 0.5, None, ALU.is_gt).then_inc(S["flag_sb"], 1)

            dve.wait_ge(S["wrest_hi"], 6)
            for w, o, m in ((wkv, O_KV, 512), (wgT, O_WT, D), (w2s, O_W2, D), (wrs, O_WR, EXP)):
                dve.tensor_tensor(w[:, 1, :, :], wsm[:, :, o:o + m], w[:, 0, :, :].bitcast(f32), ALU.subtract)\
                    .then_inc(S["wrest_lo"], 1)
            dve.tensor_tensor(bkvs[:, 1, :], T["bkv"][:, :], bkvs[:, 0, :].bitcast(f32), ALU.subtract)\
                .then_inc(S["wrest_lo"], 1)

            def kv_low(t, k):
                dve.wait_ge(S["xT_hi"], t + 1)
                dve.tensor_tensor(xT[:, k, 1, :, :], TRP[k][:, 0:2 * P].rearrange("p (c n) -> p c n", c=2),
                                  xT[:, k, 0, :, :].bitcast(f32), ALU.subtract).then_inc(S["xT_lo"], 1)

            def kv_norm(t, k):
                dve.wait_ge(S["sq_ready"], t + 1)
                dve.reduce_sum(T["s2"][:, 0, :], T["sq"][:, :].rearrange("p (h d) -> p h d", d=HC), axis=AX)\
                    .then_inc(S["s2_ready"], 1)
                dve.wait_ge(S["sd_ready"], t + 1)
                dve.reciprocal(T["s2"][:, 1, :], T["s2"][:, 1, :]).then_inc(S["dve_loop_link"], 1)
                after(dve, "kv_sum", t - 1)
                dve.wait_ge(S["dve_loop_link"], t + 1)
                dve.tensor_tensor(T["kn"][:, k, :].rearrange("p (h d) -> p h d", d=HC),
                                  KVP[k][:P, 0:D].rearrange("p (h d) -> p h d", d=HC),
                                  bc_in(T["s2"][:, 1, 0:8], HC), ALU.mult).then_inc(S["kn_ready"], 1)
                for h in range(2):
                    ins = dve.tensor_tensor(T["vn"][:, k, h, 0:128].rearrange("p (h d) -> p h d", d=HC),
                                            KVP[k][:P, D + 128 * h:D + 128 * h + 128].rearrange("p (h d) -> p h d", d=HC),
                                            bc_in(T["s2"][:, 1, 8 + 4 * h:12 + 4 * h], HC), ALU.mult)
                ins.then_inc(S["kn_ready"], 1)

            def kv_turn(t, k):
                if not isinstance(t, int) or t < NT:
                    kv_low(t, k)
                if not isinstance(t, int) or t >= 1:
                    kv_norm(t - 1, 1 - k)

            kv_turn(0, 0)
            kv_turn(1, 1)
            with dve.Fori(1, NT // 2 - 1) as i:
                kv_turn(i * 2, 0)
                kv_turn(i * 2 + 1, 1)
            for t in range(NT - 2, NT + 1):
                kv_turn(t, t % 2)

            dve.wait_ge(S["flag_sb"], 1)
            needed = dve.value_load(flag[0:1, 0:1], min_val=0, max_val=1)
            with dve.If(needed > 0):
                with dve.Fori(0, NT) as t:
                    with dve.Fori(0, EC) as j:
                        q = t * EC + j
                        rel, lt, off = fb_s[:, 0:1], fb_s[:, 1:2], fb_s[:, 2:3]
                        dve.tensor_scalar(rel, posn[:, ds(j, 1)], stbc[:EP, ds(t, 1)], 0.0, ALU.subtract, ALU.is_ge)
                        dve.tensor_scalar(lt, posn[:, ds(j, 1)], stbc[:EP, ds(t, 1)], float(WIN), ALU.subtract,
                                          ALU.is_lt)
                        dve.tensor_scalar(off, edg[:, ds(j, 1), 1], tbase[:EP, ds(t, 1)], None, ALU.subtract)\
                            .then_inc(S["fb_link"], 1)
                        dve.wait_ge(S["fb_link"], q * 3 + 1)
                        dve.tensor_tensor(rel, rel, lt, ALU.mult).then_inc(S["fb_link"], 1)
                        dve.wait_ge(S["fb_link"], q * 3 + 2)
                        dve.tensor_scalar(lt, rel, -1.0, 1.0, ALU.mult, ALU.add).then_inc(S["fb_link"], 1)
                        dve.wait_ge(S["fb_link"], q * 3 + 3)
                        dve.wait_ge(S["fb_mm"], q)
                        dve.tensor_scalar(fb_o[:, :], iotaP[:EP, :], off, lt, ALU.is_equal, ALU.mult)\
                            .then_inc(S["fb_oh"], 1)
                    dve.wait_ge(S["fb_sum"], t + 1)
                    dve.wait_ge(S["fb_add"], t * 16)
                    dve.tensor_scalar(fb_a[:, :], CNT[:P, D:2 * D], rd[:, ds(t, 1)], None, ALU.mult)\
                        .then_inc(S["fb_link2"], 1)
                    dve.wait_ge(S["fb_link2"], t + 1)
                    dve.scalar_tensor_tensor(out=fb_a[:, :], in0=CNT[:P, 0:D], scalar=rd[:, ds(t, 1)], in1=fb_a[:, :],
                                             op0=ALU.mult, op1=ALU.add).then_inc(S["fb_res"], 1)

            dve.wait_ge(S["kv_sum"], NT)
            vg, vb = T["rowv"][:, R_VG:R_VG + 128], T["rowv"][:, R_VB:R_VB + 128]
            kg, kb = T["col"][:, 4:5], T["col"][:, 5:6]
            for h in range(2):
                A, sk, sv = KA[:, 129 * h:129 * h + 128], KA[:, 129 * h + 128:129 * h + 129], KS[:, 128 * h:128 * h + 128]
                u, v = T["kvt"][:, 0, :], T["kvt"][:, 1, :]
                link(dve.tensor_tensor(u, A, vg, ALU.mult))
                link(dve.tensor_copy(T["rb"][:, 0:1], sk))
                link(dve.scalar_tensor_tensor(out=u, in0=vb, scalar=T["rb"][:, 0:1], in1=u, op0=ALU.mult, op1=ALU.add))
                link(dve.tensor_tensor(v, sv, vg, ALU.mult))
                link(dve.scalar_tensor_tensor(out=v, in0=vb, scalar=float(N), in1=v, op0=ALU.mult, op1=ALU.add))
                link(dve.tensor_scalar(v, v, kb, 1.0 / N, ALU.mult, ALU.mult))
                link(dve.tensor_scalar(u, u, kg, 1.0 / N, ALU.mult, ALU.mult))
                for b in range(4):
                    w = slice(32 * b, 32 * b + 32)
                    ins = dve.tensor_tensor(T["kvs"][w, h, w], T["kvt"][w, 0, w], T["kvt"][w, 1, w], ALU.add)
                if h == 0:
                    link(ins)
                else:
                    ins.then_inc(S["kvs_sb"], 1)
            dve.wait_ge(S["rT_ps"], 1)
            for h in range(2):
                link(dve.tensor_copy(T["rT"][:, h, :], TRP[h][:, 0:D]))
                c = slice(128 * h, 128 * h + 128)
                dve.tensor_tensor(T["rT"][:, h, c], T["rT"][:, h, c], ident[:, :], ALU.add).then_inc(S["rT_sb"], 1)
            dve.tensor_copy(T["rb"][:, :], MSC[:, M_CM:M_CM + 2]).then_inc(S["rT_sb"], 1)
            dve.wait_ge(S["wm_ps"], 1)
            dve.wait_ge(S["wm_hi"], 2)
            for c in range(2):
                dve.tensor_tensor(wms[:, 1, c, :], KVP[c][:, 0:D], wms[:, 0, c, :].bitcast(f32), ALU.subtract)\
                    .then_inc(S["wm_lo"], 1)
            dve.tensor_tensor(cm[:, :], MSC[:, M_CM + 2:M_CM + 4], T["col"][:, 2:4], ALU.add).then_inc(S["wm_lo"], 1)

            dve.sem_inc(S["pro_over"], 1)
            dve.wait_ge(S["pro_over"], 3)
            dve.wait_ge(S["fb_over"], 1)
            for k in range(2):
                dve.wait_ge(S[f"xT_out{k}"], 16 * (NT // 2))

            for e in range(EXP):
                dve.wait_ge(S["w_hi"], e + 1)
                dve.tensor_tensor(wlo[:, e, :, :, :], wst[:, e % 2, :, :, :], whi[:, e, :, :, :].bitcast(f32),
                                  ALU.subtract).then_inc(S["wst_free"], 1)

            def one_hot(q, u):
                t = q * TG + u // 2
                if u % 2 == 0:
                    dve.wait_ge(S["win_in"], t * 16 + 16)
                    after(dve, "oh_ready", q * 8 + u)
                    dve.tensor_scalar(dl[:, :], win[:, ds(t, 1), :, 1].rearrange("p o s -> p (o s)"),
                                      tbase[:, ds(t, 1)], None, ALU.subtract).then_inc(S["dl_ready"], 1)
                    dve.wait_ge(S["dl_ready"], t + 1)
                after(dve, "unit_done", q * 8 + (u - 1))
                k = u % 2
                dve.tensor_tensor(oh[:, k, :, :], iota_rep[:, :, :], bc_out(dl[:, k * US:k * US + US], P),
                                  ALU.is_equal).then_inc(S["oh_ready"], 1)

            def cut_low(name, g, e):
                buf, hi = ((t1, h1), (t2, h2))[name == "l2"]
                dve.wait_ge(S[name + "_hi"], g * EXP + (e + 1))
                dve.tensor_tensor(hi[:, 1, :, :], buf[:, :, :], hi[:, 0, :, :].bitcast(f32), ALU.subtract)\
                    .then_inc(S[name + "_lo"], 1)

            def mlp(q):
                dve.wait_ge(S["g_hi"], q + 1)
                dve.tensor_tensor(gT[:, 1, :, :], t1[:, :, :], gT[:, 0, :, :].bitcast(f32), ALU.subtract)\
                    .then_inc(S["g_lo"], 1)

            def agg_add(q, t):
                i = q * TG + t
                after(dve, "mt_ps", q * 9 + (T_AT[t - 1] + 1) if t else q * 9 - 3)
                dve.wait_ge(S["alo_ready"], i + 1)
                dve.scalar_tensor_tensor(out=ag1[:, :], in0=AGG[:P, 0:D], scalar=rd[:, ds(i, 1)], in1=alo[:, :],
                                         op0=ALU.mult, op1=ALU.add).then_inc(S["agg_evac"], 1)
                dve.wait_ge(S["agg_evac"], i + 1)
                dve.wait_ge(S[f"bs_in{t % 2}"], q * 64 + (t // 2 * 32 + 32))
                dve.tensor_tensor(ag2[:, :], ag1[:, :], bs[:, t % 2, 1, :], ALU.add).then_inc(S["ag_ready"], 1)

            def mt_low(q, at, dst, hi):
                dve.wait_ge(S["mt_hi"], q * 8 + (at + 1))
                dve.tensor_tensor(dst, MT[:, :].rearrange("p (c n) -> p c n", c=2), hi.bitcast(f32), ALU.subtract)\
                    .then_inc(S["mt_lo"], 1)

            def agg_cut(q, t):
                mt_low(q, T_AT[t], aT[:, 1, :, :], aT[:, 0, :, :])

            def x2_cut(q, t):
                w = slice(t * P, t * P + P)
                mt_low(q, X_AT[t], x2T[:, 1, :, w], x2T[:, 0, :, w])

            def residual(q, t):
                dve.wait_ge(S["mp_ps"], q * 8 + (t + 1))
                after(dve, "y_used", (q - 1) * (EXP * TG) + (t + 1))
                dve.tensor_tensor(x1[:, t, :], MP, bs[:, t % 2, 0, :], ALU.add).then_inc(S["mp_free"], 1)
                dve.wait_ge(S["mp_free"], q * 8 + (t + 1))
                dve.bn_stats(bst2[:, :], x1[:, t, :]).then_inc(S["st_ready"], 1)
                dve.wait_ge(S["st_ready"], q * TG + (t + 1))
                settle(dve)
                dve.bn_aggr(mv2[:, t, :], bst2[:, :]).then_inc(S["var_ready"], 1)

            def scales(q, t):
                dve.wait_ge(S["std_ready"], q * TG + (t + 1))
                dve.reciprocal(rs2[:, t:t + 1], sd2[:, t:t + 1]).then_inc(S["rs_ready"], 1)
                dve.wait_ge(S["rs_ready"], q * TG + (t + 1))
                dve.scalar_tensor_tensor(out=nm2[:, t:t + 1], in0=mv2[:, t, 0:1], scalar=-1.0, in1=rs2[:, t:t + 1],
                                         op0=ALU.mult, op1=ALU.mult).then_inc(S["nmr_ready"], 1)

            def softmax(q):
                dve.wait_ge(S["r_ps"], q + 1)
                dve.tensor_tensor(lg[:, :, :], ML.rearrange("p (t e) -> p t e", t=TG), bc_out(br_b[:, :], TG), ALU.add)\
                    .then_inc(S["r_lg"], 1)
                dve.wait_ge(S["r_lg"], q + 1)
                dve.reduce_max(mx[:, :], lg[:, :, :], axis=AX).then_inc(S["r_max"], 1)
                dve.wait_ge(S["r_max"], q + 1)
                dve.tensor_tensor(lg[:, :, :], lg[:, :, :], bc_in(mx[:, :], EXP), ALU.subtract)\
                    .then_inc(S["r_sub"], 1)
                dve.wait_ge(S["r_exp"], q + 1)
                dve.reduce_sum(sm[:, :], lg2[:, :, :], axis=AX).then_inc(S["r_sum"], 1)
                dve.wait_ge(S["r_sum"], q * 2 + 1)
                dve.reciprocal(sm[:, :], sm[:, :]).then_inc(S["r_sum"], 1)
                dve.wait_ge(S["r_sum"], q * 2 + 2)
                after(dve, "y_used", q * (EXP * TG))
                dve.tensor_tensor(wn[:, :, :], lg2[:, :, :], bc_in(sm[:, :], EXP), ALU.mult).then_inc(S["w_ready"], 1)

            def w_transposed(g):
                dve.wait_ge(S["mt_ps"], g * 9 + 9)
                dve.tensor_copy(wT[:, :], MT[0:TG * EXP, 0:P]).then_inc(S["mt_lo"], 1)

            def add_bias(g, t):
                dve.wait_ge(S["mp_ps"], g * 8 + (t + 5))
                dve.tensor_tensor(x1[:, t, :], MP, x1[:, t, :], ALU.add).then_inc(S["mp_free"], 1)

            def add_expert(g, e):
                for t in range(TG):
                    i = g * (EXP * TG) + (e * TG + t)
                    if t % 2 == 0:
                        dve.wait_ge(S["y_ps"], i + 2)
                    if e == 0:
                        dve.wait_ge(S["mp_free"], g * 8 + (t + 5))
                        dve.wait_ge(S["w_ready"], g + 1)
                        after(dve, "out_sent", g * 16)
                    else:
                        dve.wait_ge(S["y_used"], i - 3)
                    dve.scalar_tensor_tensor(out=acc[:, t, :], in0=YP[t], scalar=wn[:, t, e:e + 1],
                                             in1=x1[:, t, :] if e == 0 else acc[:, t, :],
                                             op0=ALU.mult, op1=ALU.add).then_inc(S["y_used"], 1)

            one_hot(0, 0)
            one_hot(0, 1)
            mlp(0)
            agg_add(0, 0)
            one_hot(0, 2)
            one_hot(0, 3)
            agg_cut(0, 0)
            agg_add(0, 1)
            one_hot(0, 4)
            residual(0, 0)
            agg_cut(0, 1)
            one_hot(0, 5)
            scales(0, 0)
            agg_add(0, 2)
            one_hot(0, 6)
            residual(0, 1)
            agg_cut(0, 2)
            one_hot(0, 7)
            scales(0, 1)
            agg_add(0, 3)
            residual(0, 2)
            scales(0, 2)
            x2_cut(0, 0)
            x2_cut(0, 1)
            agg_cut(0, 3)
            x2_cut(0, 2)
            residual(0, 3)
            scales(0, 3)
            x2_cut(0, 3)
            softmax(0)

            def group(g, prepare):
                q = g + 1
                if prepare:
                    one_hot(q, 0)
                cut_low("l1", g, 0)
                w_transposed(g)
                if prepare:
                    mlp(q)
                add_bias(g, 0)
                add_bias(g, 1)
                cut_low("l1", g, 1)
                add_bias(g, 2)
                cut_low("l2", g, 0)
                add_bias(g, 3)
                if prepare:
                    one_hot(q, 1)
                for e in range(1, EXP):
                    if prepare and e < EXP - 1:
                        one_hot(q, e + 1)
                    if prepare and e % 2:
                        agg_add(q, e // 2)
                    if prepare and e == 7:
                        x2_cut(q, 1)
                    if prepare and e in (2, 4, 6):
                        residual(q, e // 2 - 1)
                    if e < EXP - 1:
                        cut_low("l1", g, e + 1)
                    elif prepare:
                        agg_cut(q, 3)
                    cut_low("l2", g, e)
                    add_expert(g, e - 1)
                    if prepare:
                        if e in (1, 3, 5):
                            agg_cut(q, e // 2)
                        if e in (2, 4):
                            scales(q, e // 2 - 1)
                        if e == 6:
                            x2_cut(q, 0)
                            scales(q, 2)
                        if e == 7:
                            x2_cut(q, 2)
                            residual(q, 3)
                            scales(q, 3)
                add_expert(g, EXP - 1)
                if prepare:
                    x2_cut(q, 3)
                    softmax(q)

            with dve.Fori(0, NG - 1) as g:
                group(g, True)
            group(NG - 1, False)

        @block.tensor
        def _(pe):
            def count(c, k, first=False, last=False):
                pe.wait_ge(S["one_ready"], c * 2 + 2)
                for j in range(CH):
                    ins = pe.matmul(CNT[:CA, 0:CB], oneA[:, k, :, j], oneB[:, k, :, j],
                                    start=first and j == 0, stop=last and j == CH - 1, skip_group_check=True)
                ins.then_inc(S["one_free"], 1)

            count(0, 0, first=True)
            with pe.Fori(0, NCH // 2 - 1) as i:
                count(i * 2 + 1, 1)
                count(i * 2 + 2, 0)
            count(NCH - 2, 1)
            count(NCH - 1, 0, last=True)
            pe.wait_ge(S["one_free"], NCH)
            pe.sem_inc(S["cnt_ps"], 1)

            ones = T["ones"]
            pe.wait_ge(S["consts"], 15)
            pe.wait_ge(S["cnt_in"], 16)
            pe.transpose(CNT[:P, 128:128 + NT], T["cnt_t"][:, :], ident[:NT, :NT]).then_inc(S["cntT_ps"], 1)
            pe.wait_ge(S["tot_sb"], 1)
            pe.matmul(MSC[0:1, M_ST:M_ST + NT], T["tot"][:, 0:1], T["ltri"][:, :], start=True, stop=True)\
                .then_inc(S["start_ps"], 1)
            pe.wait_ge(S["stf_sb"], 1)
            pe.matmul(MSC[:, M_BC:M_BC + NT], ones[0:1, :], T["stf"][:, :], start=True, stop=True)
            pe.matmul(MSC[0:1, M_FL:M_FL + 1], T["vs"][:, 0:1], ones[:EP, 0:1], start=True, stop=False)
            pe.matmul(MSC[0:1, M_FL:M_FL + 1], T["tot"][:, 1:2], ones[:NT, 0:1], start=False, stop=True)\
                .then_inc(S["flag_ps"], 1)

            for bank in (KA, KS):
                pe.matmul(bank[:, :], fb_z[:, 0:128], fb_z[:, :], start=True, stop=False,
                          skip_group_check=True)
            pe.wait_ge(S["wrest_lo"], 5)

            def kv_transpose(t, k):
                pe.wait_ge(S["xc_ready"], t + 1)
                after(pe, "xT_lo", t - 1)
                for c in range(2):
                    ins = pe.transpose(TRP[k][:, c * P:c * P + P], T["xc"][:, k, 128 * c:128 * c + 128],
                                       ident[:P, :P])
                ins.then_inc(S["tr_ps"], 1)

            def kv_project(t, k):
                pe.wait_ge(S["xT_lo"], t + 1)
                after(pe, "kn_ready", 2 * (t - 1))
                out = KVP[k][:P, :]
                pe.matmul(out, onesr[:, :], bkvs[:, 0, :], start=True, stop=False)
                pe.matmul(out, onesr[:, :], bkvs[:, 1, :], start=False, stop=False)
                for c in range(2):
                    pe.matmul(out, xT[:, k, 0, c, :], wkv[:, 0, c, :], start=False, stop=False)
                    pe.matmul(out, xT[:, k, 0, c, :], wkv[:, 1, c, :], start=False, stop=False)
                    ins = pe.matmul(out, xT[:, k, 1, c, :], wkv[:, 0, c, :], start=False, stop=c == 1)
                ins.then_inc(S["kv_ps"], 1)

            def kv_sum(t, k, rows=P, last=False):
                pe.wait_ge(S["kn_ready"], 2 * t + 2)
                kn, vn = T["kn"], T["vn"]
                for h in range(2):
                    pe.matmul(KA[:, 129 * h:129 * h + 129], kn[:rows, k, 128 * h:128 * h + 128], vn[:rows, k, h, 0:129],
                              start=False, stop=last, skip_group_check=True)
                for h in range(2):
                    ins = pe.matmul(KS[:, 128 * h:128 * h + 128], ones[:rows, :], vn[:rows, k, h, 0:128],
                                    start=False, stop=last, skip_group_check=True)
                ins.then_inc(S["kv_sum"], 1)

            def kv_turn(t, k):
                const = isinstance(t, int)
                if not const or t < NT:
                    kv_transpose(t, k)
                if not const or 1 <= t <= NT:
                    kv_project(t - 1, 1 - k)
                if not const or t >= 2:
                    last = const and t - 2 == NT - 1
                    kv_sum(t - 2, k, LAST if last else P, last)

            kv_turn(0, 0)
            kv_turn(1, 1)
            with pe.Fori(1, NT // 2 - 1) as i:
                kv_turn(i * 2, 0)
                kv_turn(i * 2 + 1, 1)
            for t in range(NT - 2, NT + 2):
                kv_turn(t, t % 2)

            pe.wait_ge(S["flag_sb"], 1)
            needed = pe.value_load(flag[0:1, 0:1], min_val=0, max_val=1)
            with pe.If(needed > 0):
                with pe.Fori(0, NT) as t:
                    pe.wait_ge(S["fb_res"], t)
                    pe.matmul(CNT[:P, :], fb_z[:, 0:P], fb_z[:, :], start=True, stop=False, skip_group_check=True)
                    with pe.Fori(0, EC) as j:
                        q = t * EC + (j + 1)
                        pe.wait_ge(S["fb_gath"], q * 16)
                        pe.wait_ge(S["fb_oh"], q)
                        pe.matmul(CNT[:P, :], fb_o[:, :], fb_g[:, :], start=False, stop=False, skip_group_check=True)\
                            .then_inc(S["fb_mm"], 1)
                    pe.matmul(CNT[:P, :], fb_z[:, 0:P], fb_z[:, :], start=False, stop=True, skip_group_check=True)\
                        .then_inc(S["fb_sum"], 1)

            pe.wait_ge(S["kvs_sb"], 1)
            pe.wait_ge(S["col_in"], 16)
            for h in range(2):
                pe.matmul(TRP[h][:, 0:D], T["kvs"][:, h, :], wsm[:, h, O_WQ:O_WQ + D], start=True, stop=True)
                ins = pe.matmul(MSC[:, M_CM + h:M_CM + h + 1], T["kvs"][:, h, :], T["col"][:, h:h + 1],
                                start=True, stop=True)
            ins.then_inc(S["rT_ps"], 1)
            pe.wait_ge(S["rT_sb"], 3)
            for c in range(2):
                w = slice(128 * c, 128 * c + 128)
                for h in range(2):
                    pe.matmul(KVP[c][:, 0:D], T["rT"][:, h, w], wsm[:, h, O_W1:O_W1 + D], start=h == 0, stop=h == 1)
                for h in range(2):
                    ins = pe.matmul(MSC[:, M_CM + 2 + c:M_CM + 3 + c], wsm[:, h, O_W1 + 128 * c:O_W1 + 128 * c + 128],
                                    T["rb"][:, h:h + 1], start=h == 0, stop=h == 1)
            ins.then_inc(S["wm_ps"], 1)
            pe.wait_ge(S["wm_lo"], 3)
            pe.sem_inc(S["pro_over"], 1)
            pe.wait_ge(S["pro_over"], 3)
            pe.wait_ge(S["bo_in"], 16 * TG)
            pe.wait_ge(S["bn_ready"], 1)

            def three(out, hi, lo, whi_, wlo_):
                return [(whi_, hi), (whi_, lo), (wlo_, hi)]

            def layer1(g, e, after_mlp=False):
                m = g * EXP + e
                if e == 0:
                    pe.wait_ge(S["mt_lo"], g * 9 + 8)
                after(pe, "l1_act", m * 2)
                if after_mlp:
                    pe.wait_ge(S["g_act"], g * 2 + 4)
                for c in range(2):
                    w = slice(128 * c, 128 * c + 128)
                    for k in range(2):
                        pe.matmul(H1P[c][:, 0:GN], whi[:, e, 0, k, w], x2T[:, 0, k, :], start=k == 0, stop=False)
                        pe.matmul(H1P[c][:, 0:GN], whi[:, e, 0, k, w], x2T[:, 1, k, :], start=False, stop=False)
                        ins = pe.matmul(H1P[c][:, 0:GN], wlo[:, e, 0, k, w], x2T[:, 0, k, :], start=False, stop=k == 1)
                    ins.then_inc(S["l1_ps"], 1)

            def layer2(g, e):
                m = g * EXP + e
                after(pe, "l2_act", m * 2)
                pe.wait_ge(S["l1_hi"], m + 1)
                for c in range(2):
                    w = slice(128 * c, 128 * c + 128)
                    for k in range(2):
                        pe.matmul(H2P[c][:, 0:GN], whi[:, e, 1, k, w], h1[:, 0, k, :], start=k == 0, stop=False)
                        pe.matmul(H2P[c][:, 0:GN], wlo[:, e, 1, k, w], h1[:, 0, k, :], start=False, stop=False)
                pe.wait_ge(S["l1_lo"], m + 1)
                for c in range(2):
                    w = slice(128 * c, 128 * c + 128)
                    for k in range(2):
                        ins = pe.matmul(H2P[c][:, 0:GN], whi[:, e, 1, k, w], h1[:, 1, k, :], start=False, stop=k == 1)
                    ins.then_inc(S["l2_ps"], 1)

            def layer3(g, e):
                m = g * EXP + e
                pe.wait_ge(S["l2_hi"], m + 1)
                pe.wait_ge(S["l2_lo"], m + 1)
                for t in range(TG):
                    w = slice(t * P, t * P + P)
                    if e and t % 2 == 0:
                        pe.wait_ge(S["y_used"], m * TG + (t - 2))
                    for k in range(2):
                        pe.matmul(YP[t], h2[:, 0, k, w], whi[:, e, 2, k, :], start=k == 0, stop=False)
                        pe.matmul(YP[t], h2[:, 0, k, w], wlo[:, e, 2, k, :], start=False, stop=False)
                        ins = pe.matmul(YP[t], h2[:, 1, k, w], whi[:, e, 2, k, :], start=False, stop=k == 1)
                    ins.then_inc(S["y_ps"], 1)

            def mlp(q):
                pe.wait_ge(S["xg_in"], q * 16 + 16)
                after(pe, "l1_act", (q - 1) * (2 * EXP) + 2)
                for c in range(2):
                    w = slice(128 * c, 128 * c + 128)
                    for k in range(2):
                        pe.matmul(H1P[c][:, 0:GN], wms[:, 0, k, w], xg[:, :, 0, k, :], start=k == 0, stop=False)
                        pe.matmul(H1P[c][:, 0:GN], wms[:, 0, k, w], xg[:, :, 1, k, :], start=False, stop=False)
                        ins = pe.matmul(H1P[c][:, 0:GN], wms[:, 1, k, w], xg[:, :, 0, k, :], start=False, stop=k == 1)
                    ins.then_inc(S["g_ps"], 1)

            def agg(q, u):
                pe.wait_ge(S[f"gath{u % 2}"], q * (TG * US * 16) + (u // 2 + 1) * (US * 16))
                pe.wait_ge(S["oh_ready"], q * 8 + (u + 1))
                if u % 2 == 0:
                    after(pe, "agg_evac", q * TG + u // 2)
                for s in range(US):
                    ins = pe.matmul(AGG[:P, :], oh[:, u % 2, :, s], G[:, u % 2, s, :],
                                    start=u % 2 == 0 and s == 0, stop=u % 2 == 1 and s == US - 1)
                ins.then_inc(S["unit_done"], 1)

            def small_bank(q, mt, mp):
                after(pe, "mt_lo", q * 9 + mt)
                after(pe, "mp_free", q * 8 + mp)

            def transposes(q, at, src):
                small_bank(q, at, MP_BEFORE[at])
                for c in range(2):
                    ins = pe.transpose(MT[:, c * P:c * P + P], src[:, 128 * c:128 * c + 128], ident[:P, :P])
                ins.then_inc(S["mt_ps"], 1)

            def agg_transpose(q, t):
                pe.wait_ge(S["ag_ready"], q * TG + (t + 1))
                transposes(q, T_AT[t], ag2)

            def x2_transpose(q, t):
                pe.wait_ge(S["xn2_ready"], q * TG + (t + 1))
                transposes(q, X_AT[t], xn2[:, t, :])

            def project(q, t):
                if t == 0:
                    pe.wait_ge(S["g_lo"], q + 1)
                small_bank(q, MT_BEFORE[t], t)
                w = slice(t * P, t * P + P)
                for k in range(2):
                    for i, (lhs, wts) in enumerate(((gT[:, :, k, w], w2s), (aT[:, :, k, :], wgT))):
                        pe.matmul(MP, lhs[:, 0, :], wts[:, 0, k, :], start=k == 0 and i == 0, stop=False)
                        pe.matmul(MP, lhs[:, 0, :], wts[:, 1, k, :], start=False, stop=False)
                        ins = pe.matmul(MP, lhs[:, 1, :], wts[:, 0, k, :], start=False, stop=k == 1 and i == 1)
                ins.then_inc(S["mp_ps"], 1)

            def route(q):
                small_bank(q, 8, 4)
                for t in range(TG):
                    w = slice(t * P, t * P + P)
                    out = ML[:, EXP * t:EXP * t + EXP]
                    for k in range(2):
                        pe.matmul(out, x2T[:, 0, k, w], wrs[:, 0, k, :], start=k == 0, stop=False)
                        pe.matmul(out, x2T[:, 0, k, w], wrs[:, 1, k, :], start=False, stop=False)
                        ins = pe.matmul(out, x2T[:, 1, k, w], wrs[:, 0, k, :], start=False, stop=k == 1)
                ins.then_inc(S["r_ps"], 1)

            def w_transpose(g):
                pe.wait_ge(S["w_ready"], g + 1)
                small_bank(g, 8, 4)
                pe.transpose(MT[0:TG * EXP, 0:P], wn[:, :, :].rearrange("p t e -> p (t e)"), ident[:P, :P])\
                    .then_inc(S["mt_ps"], 1)

            def bias(g, t):
                small_bank(g, 9, 4 + t)
                pe.matmul(MP, wT[:, :], bo4[:, t, :], start=True, stop=True).then_inc(S["mp_ps"], 1)

            mlp(0)
            agg(0, 0)
            agg(0, 1)
            agg_transpose(0, 0)
            agg(0, 2)
            agg(0, 3)
            project(0, 0)
            agg_transpose(0, 1)
            agg(0, 4)
            agg(0, 5)
            project(0, 1)
            agg_transpose(0, 2)
            agg(0, 6)
            agg(0, 7)
            project(0, 2)
            x2_transpose(0, 0)
            x2_transpose(0, 1)
            agg_transpose(0, 3)
            x2_transpose(0, 2)
            project(0, 3)
            x2_transpose(0, 3)
            route(0)
            pe.wait_ge(S["wst_free"], EXP)

            def group(g, prepare):
                q = g + 1
                layer1(g, 0)
                w_transpose(g)
                if prepare:
                    agg(q, 0)
                    mlp(q)
                bias(g, 0)
                layer1(g, 1, prepare)
                bias(g, 1)
                layer2(g, 0)
                bias(g, 2)
                bias(g, 3)
                for e in range(1, EXP):
                    if prepare:
                        agg(q, e)
                    if e < EXP - 1:
                        layer1(g, e + 1)
                    elif prepare:
                        x2_transpose(q, 1)
                    layer2(g, e)
                    if prepare and e in (2, 4, 6):
                        project(q, e // 2 - 1)
                    if prepare and e == 7:
                        agg_transpose(q, 3)
                    layer3(g, e - 1)
                    if prepare:
                        if e in (1, 3, 5):
                            agg_transpose(q, e // 2)
                        if e == 6:
                            x2_transpose(q, 0)
                        if e == 7:
                            x2_transpose(q, 2)
                            project(q, 3)
                layer3(g, EXP - 1)
                if prepare:
                    x2_transpose(q, 3)
                    route(q)

            with pe.Fori(0, NG - 1) as g:
                group(g, True)
            group(NG - 1, False)


def kernel(**inputs):
    import concourse.bacc as _bacc
    from concourse.bass_utils import run_bass_kernel_spmd as _run

    a = {k: np.asarray(v) for k, v in inputs.items()}
    x = np.zeros((NP, D), np.float32)
    x[:N] = a["x"]
    edges = np.ascontiguousarray(np.stack([a["src"], a["dst"]], axis=-1))
    w = np.stack([a["L0_ffn_W1"], a["L0_ffn_W2"], a["L0_ffn_Wo"]], axis=1).reshape(EXP, 3, 2, 128, D)
    wffn = np.ascontiguousarray(w.transpose(3, 0, 1, 2, 4))
    bn = np.stack([np.stack([a[f"L0_ffn_{n}{l}"] for n in ("b", "g", "be", "m", "v")]) for l in (1, 2)])
    bn = np.ascontiguousarray(bn.reshape(2, 5, EXP, 2, 128).transpose(4, 0, 1, 2, 3))
    wq, wk, wv = a["L0_mix_w_qkv"].reshape(D, D // HC, 3, HC).transpose(2, 0, 1, 3).reshape(3, D, D)
    bq, bk, bv = a["L0_mix_b_qkv"].reshape(D // HC, 3, HC).transpose(1, 0, 2).reshape(3, D)
    wsm = np.concatenate([a["L0_gnn_W"].T, wk, wv, a["L0_mix_w1"], a["L0_mix_w2"], a["L0_ffn_Wr"], wq.T], axis=1)
    wsm = np.ascontiguousarray(wsm.reshape(2, 128, SW).transpose(1, 0, 2))
    col = np.ascontiguousarray(np.stack([bq[:128], bq[128:], a["L0_mix_b1"][:128], a["L0_mix_b1"][128:],
                                         np.tile(a["L0_mix_kln_g"], 4), np.tile(a["L0_mix_kln_b"], 4)], axis=1))
    row = np.concatenate([np.tile(a["L0_mix_vln_g"], 4), np.tile(a["L0_mix_vln_b"], 4), a["L0_gnn_b"],
                          a["L0_mix_b2"], a["L0_ffn_br"], a["L0_gnn_alpha"], bk, bv])[None]

    nc = _bacc.Bacc("TRN2", target_bir_lowering=False, num_devices=1)
    arrays = dict(x=x, edges=edges, wffn=wffn, bn=bn, wsm=wsm, col=col, row=row, bo=a["L0_ffn_bo"])
    args = [nc.dram_tensor(n + "_in", v.shape, mybir.dt.from_np(v.dtype), kind="ExternalInput").ap()
            for n, v in arrays.items()]
    out = nc.dram_tensor("out", (NP, D), mybir.dt.float32, kind="ExternalOutput").ap()
    build(nc, *args, out)
    r = _run(nc, [{n + "_in": v for n, v in arrays.items()}], core_ids=[0])
    return r.results[0]["out"][:N]
```

```python
import numpy as np
import concourse.bass as bass
from concourse import mybir
from contextlib import ExitStack

N, D, E = 3125, 256, 53125
P = 112
NT = 28
NP = P * NT
TG = 4
NG = NT // TG
GN = TG * P
LAST = N - (NT - 1) * P
EXP = 8
HC = 32
NH2 = 2 * D // HC
EP, EC = 125, 425
CH = 25
NCH = EC // CH
CA, CB = NP // 64, 64
WIN = 2048
WS = WIN // 128
US = 8
SCALE = 2048.0
LN_EPS, BN_EPS = 1e-5, 1e-3
O_WT, O_KV, O_W1, O_W2, O_WR, O_WQ = 0, 256, 768, 1024, 1280, 1288
SW = 1544
R_VG, R_VB, R_BG, R_B2, R_BR, R_A, R_BKV = 0, 128, 256, 512, 768, 776, 777
RW = R_BKV + 512
M_ST, M_BC, M_FL, M_CM = 0, 64, 100, 128
DVE_LINKS = 4 * 4 + 4


def build(nc, x_d, edges_d, wffn_d, bn_d, wsm_d, col_d, row_d, bo_d, out_d):
    f32, f32r, f16, i32 = mybir.dt.float32, mybir.dt.float32r, mybir.dt.float16, mybir.dt.int32
    ACT = mybir.ActivationFunctionType
    ALU = mybir.AluOpType
    AX = mybir.AxisListType.X
    ds = bass.ds

    table_d = nc.dram_tensor("table_d", [NP, 2 * D], f16).ap()
    base_d = nc.dram_tensor("base_d", [NP, D], f32).ap()
    self_d = nc.dram_tensor("self_d", [NP, D], f32).ap()
    xnT_d = nc.dram_tensor("xnT_d", [NT, 128, 4 * P], f32).ap()
    cnt_d = nc.dram_tensor("cnt_d", [NP], f32).ap()

    ctx = ExitStack()
    with ctx:
        def sb(name, shape, dt, where=ctx):
            return where.enter_context(nc.sbuf_tensor(name, shape, dt))

        def sem(name):
            return ctx.enter_context(nc.semaphore(name))

        G = sb("G", [128, 2, US, 2 * D], f16)
        idx = sb("idx", [128, 2, WS], i32)
        win = sb("win", [128, NT, WS, 2], i32)
        oh = sb("oh", [128, 2, P, US], f16)
        dl = sb("dl", [128, WS], f16)
        iota_rep = sb("iota_rep", [128, P, US], f16)
        ident = sb("ident", [128, 128], f32)
        tbase = sb("tbase", [128, NT], f32)
        wgT = sb("wgT", [128, 2, 2, D], f32r)
        w2s = sb("w2s", [128, 2, 2, D], f32r)
        wms = sb("wms", [128, 2, 2, D], f32r)
        wrs = sb("wrs", [128, 2, 2, EXP], f32r)
        bnsc = sb("bnsc", [128, 2, EXP, 2], f32)
        bnbi = sb("bnbi", [128, 2, EXP, 2], f32)
        cm = sb("cm", [128, 2], f32)
        bo4 = sb("bo4", [32, TG, D], f32)
        rd = sb("rd", [P, NT], f32)
        br_b = sb("br_b", [P, EXP], f32)
        epsc = sb("epsc", [128, 1], f32)
        flag = sb("flag", [1, 1], i32)
        starts = sb("starts", [1, NT], i32)
        stbc = sb("stbc", [128, NT], f32)
        iotaP = sb("iotaP", [128, P], f32)

        pro = ExitStack()
        x_all = sb("x_all", [P, NT, D], f32, pro)
        edg = sb("edg", [EP, EC, 2], i32, pro)
        oneA = sb("oneA", [EP, 2, CA, CH], f16, pro)
        oneB = sb("oneB", [EP, 2, CB, CH], f16, pro)
        xn = sb("xn", [P, NT, D], f32, pro)
        iotaA = sb("iotaA", [EP, CA, CH], f16, pro)
        iotaB = sb("iotaB", [EP, CB, CH], f16, pro)
        ab_i = sb("ab_i", [EP, 2, EC], i32, pro)
        ab_f = sb("ab_f", [EP, 2, EC], f16, pro)
        posn = sb("posn", [EP, EC], f32, pro)
        viol = sb("viol", [EP, EC], f32, pro)
        wsm = sb("wsm", [128, 2, SW], f32, pro)
        pro_small = dict(
            col=[128, 6], rowv=[128, RW], bn=[128, 2, 5, EXP, 2], bntmp=[128, 2, EXP, 2],
            nxt=[EP, 2], vs=[EP, 2], cnt_ab=[CA, CB], cnt_t=[NT, P], tot=[NT, 2], ltri=[NT, NT],
            ones=[128, 128], stf=[1, NT], deg=[P, NT], dinv=[P, NT], dS=[P, NT], sd=[P, NT],
            bst=[P, 7, 6], mv=[P, NT, 2], rstd=[P, NT], nmr=[P, NT], a1=[P, 2], brow=[P, D],
            gm=[128, 2, NH2], gb=[1, NH2], bkv=[1, 512],
            sq=[P, 512], s2=[P, 2, NH2], kn=[P, 2, D], vn=[P, 2, 2, 130], xc=[P, 2, D],
            kvs=[128, 2, 128], kvt=[128, 2, 128], rT=[128, 2, D], rb=[128, 2],
        )
        T = {}
        for k, s in pro_small.items():
            T[k] = sb("p_" + k, s, i32 if k == "nxt" else f32, pro)
        wkv = sb("wkv", [128, 2, 2, 512], f32r, pro)
        bkvs = sb("bkvs", [1, 2, 512], f32r, pro)
        onesr = sb("onesr", [1, P], f32r, pro)
        xT = sb("xT", [128, 2, 2, 2, P], f32r, pro)
        xs32 = sb("xs32", [P, 2, 2, D], f32, pro)
        tb16 = sb("tb16", [P, 2, 2, 2, D], f16, pro)
        sf32 = sb("sf32", [P, 2, 2, D], f32, pro)
        fb_e = sb("fb_e", [EP, 2], i32, pro)
        fb_g = sb("fb_g", [EP, 2 * D], f16, pro)
        fb_o = sb("fb_o", [EP, P], f16, pro)
        fb_s = sb("fb_s", [EP, 8], f32, pro)
        fb_a = sb("fb_a", [P, D], f32, pro)
        fb_z = sb("fb_z", [EP, 512], f16, pro)
        wst = sb("wst", [128, 2, 3, 2, D], f32, pro)
        pro.close()

        whi = sb("whi", [128, EXP, 3, 2, D], f32r)
        with ExitStack() as raw:
            wraw = sb("wraw", [128, EXP, 3, 2, D], f32, raw)
        wlo = sb("wlo", [128, EXP, 3, 2, D], f32r)
        t2 = sb("t2", [128, 2, GN], f32)
        x2T = sb("x2T", [128, 2, 2, GN], f32r)
        gT = sb("gT", [128, 2, 2, GN], f32r)
        xg = sb("xg", [128, TG, 2, 2, P], f32r)
        x1 = sb("x1", [P, TG, D], f32)
        xb = sb("xb", [P, TG, D], f32)
        acc = sb("acc", [P, TG, D], f32)
        bs = sb("bs", [P, 2, 2, D], f32)
        alo = sb("alo", [P, D], f32)
        ag1 = sb("ag1", [P, D], f32)
        ag2 = sb("ag2", [P, D], f32)
        aT = sb("aT", [128, 2, 2, P], f32r)
        bst2 = sb("bst2", [P, 6], f32)
        mv2 = sb("mv2", [P, TG, 2], f32)
        sd2 = sb("sd2", [P, TG], f32)
        rs2 = sb("rs2", [P, TG], f32)
        nm2 = sb("nm2", [P, TG], f32)
        xn2 = sb("xn2", [P, TG, D], f32)
        lg = sb("lg", [P, TG, EXP], f32)
        lg2 = sb("lg2", [P, TG, EXP], f32)
        mx = sb("mx", [P, TG], f32)
        sm = sb("sm", [P, TG], f32)
        wn = sb("wn", [P, TG, EXP], f32)
        wT = sb("wT", [TG * EXP, P], f32)
        t1 = sb("t1", [128, 2, GN], f32)
        h1 = sb("h1", [128, 2, 2, GN], f32r)
        h2 = sb("h2", [128, 2, 2, GN], f32r)

        B = [ctx.enter_context(nc.psum_tensor(f"bank{i}", [128, 512], f32)) for i in range(8)]
        TRP = [B[0], B[1]]
        KVP = [B[2], B[3]]
        KA, KS, CNT, MSC = B[4], B[5], B[6], B[7]
        H1P, H2P = [B[0], B[1]], [B[2], B[3]]
        YP = [B[4][:P, 0:D], B[4][:P, D:2 * D], B[5][:P, 0:D], B[5][:P, D:2 * D]]
        AGG = B[6]
        MP = B[7][:P, 0:D]
        MT = B[7][:, D:D + 2 * P]
        ML = B[7][:P, D + 2 * P:D + 2 * P + TG * EXP]

        S = {n: sem(n) for n in (
            "edges_in nxt_in x_in0 x_in1 x_in2 x_in3 wsm_in col_in row_in bn_in bo_in w_in0 w_in1 w_in2 w_in3 w_in4 w_in5 w_in6 w_in7 "
            "settled consts pool_link dve_link dve_loop_link "
            "ln_var ln_std ln_ready xn_ready one_ready one_free cnt_ps cnt_sb cnt_out cnt_in tot_sb cntT_ps "
            "start_ps starts_sb stf_sb flag_ps flag_sb deg_sb deg_sqrt dinv_sb base_ready base_out "
            "xs_ready xs_hi tb_ready tb_out0 tb_out1 sf_ready sf_out0 sf_out1 win_in idx_ready "
            "wkv_ready wrest_hi wrest_lo w_hi w_lo bn_v bn_sd bn_ready rT_ps rT_sb wm_ps wm_hi wm_lo pro_over "
            "xc_ready tr_ps xT_hi xT_lo xT_out0 xT_out1 kv_ps sq_ready s2_ready sd_ready kn_ready kv_sum kvs_sb "
            "fb_link fb_link2 fb_idx fb_gath fb_oh fb_mm fb_sum fb_res fb_add fb_over "
            "gath0 gath1 dl_ready unit_done oh_ready agg_evac alo_ready ag_ready "
            "mt_ps mt_hi mt_lo mp_ps mp_free st_ready var_ready std_ready rs_ready nmr_ready xn2_ready "
            "g_ps g_act g_hi g_lo r_ps r_lg r_max r_sub r_exp r_sum w_ready xg_in bs_in0 bs_in1 "
            "l1_ps l1_act l1_hi l1_lo l2_ps l2_act l2_hi l2_lo y_ps y_used out_sent"
        ).split()}

        block = ctx.enter_context(nc.Block())

        def after(eng, name, value):
            if not isinstance(value, int) or value > 0:
                eng.wait_ge(S[name], value)

        def settle(eng):
            eng.sem_inc(S["settled"], 1)

        def bc_out(ap, n):
            return ap.rearrange("p (o m) -> p o m", o=1).to_broadcast([ap.shape[0], n, ap.shape[1]])

        def bc_in(ap, m):
            return ap.rearrange("p (n o) -> p n o", o=1).to_broadcast([ap.shape[0], ap.shape[1], m])

        A_AT, X_AT, W_AT = (None, 0, 1, 2), (3, 4, 5, 6), 8
        NORM_AT = {2: 0, 3: 1, 5: 2}
        MP_BEFORE = (1, 2, 3, 4, 4, 4, 4, 4, 4)

        def mt_count(q, at):
            return q * 9 + (1 + at)

        def a0_count(q):
            return 0 if isinstance(q, int) and q == 0 else q * 9 - 1

        @block.sync
        def _(sp):
            e3 = edges_d.rearrange("(p j) two -> p j two", p=EP)
            sp.dma_start(edg[:, :, :], e3).then_inc(S["edges_in"], 16)
            xv = x_d.rearrange("(t p) d -> p t d", p=P)
            for i in range(4):
                sp.dma_start(x_all[:, 7 * i:7 * i + 7, :], xv[:, 7 * i:7 * i + 7, :]).then_inc(S[f"x_in{i}"], 16)
            sp.dma_start(T["nxt"][0:EP - 1, :], e3[1:EP, 0, :]).then_inc(S["nxt_in"], 16)
            sp.dma_start(T["rowv"][:, :], row_d.to_broadcast([128, RW])).then_inc(S["row_in"], 16)
            sp.dma_start(T["bn"][:, :, :, :, :], bn_d).then_inc(S["bn_in"], 16)
            sp.dma_start(T["col"][:, :], col_d).then_inc(S["col_in"], 16)
            sp.dma_start(wsm[:, :, :], wsm_d).then_inc(S["wsm_in"], 16)
            sp.wait_ge(S["consts"], 1)
            for t in range(TG):
                sp.dma_start(bo4[EXP * t:EXP * t + EXP, t, :], bo_d).then_inc(S["bo_in"], 16)
            for e in range(2):
                sp.dma_start(wst[:, e, :, :, :], wffn_d[:, e, :, :, :]).then_inc(S[f"w_in{e}"], 16)
            sp.wait_ge(S["cnt_sb"], 1)
            sp.dma_start(cnt_d.rearrange("(a b) -> a b", b=CB), T["cnt_ab"][:, :]).then_inc(S["cnt_out"], 16)
            sp.wait_ge(S["cnt_out"], 16)
            sp.dma_start(T["cnt_t"][:, :], cnt_d.rearrange("(t p) -> t p", p=P)).then_inc(S["cnt_in"], 16)
            ef = edges_d.rearrange("e two -> (e two)")
            sp.wait_ge(S["starts_sb"], 1)
            with sp.Fori(0, NT) as t:
                v = sp.value_load(starts[0:1, ds(t, 1)], min_val=0, max_val=E - WIN)
                sp.dma_start(win[:, ds(t, 1), :, :].rearrange("p o s two -> p o (s two)"),
                             ef[ds(v * 2, 2 * WIN)].rearrange("(p o k) -> p o k", p=128, o=1))\
                    .then_inc(S["win_in"], 16)
                sp.wait_ge(S["win_in"], (t + 1) * 16)
                settle(sp)

            def load_base(t, k):
                settle(sp)
                sp.dma_start(bs[:, k, 0, :], base_d[ds(t * P, P), :]).then_inc(S[f"bs_in{k}"], 16)
                sp.dma_start(bs[:, k, 1, :], self_d[ds(t * P, P), :]).then_inc(S[f"bs_in{k}"], 16)

            def load_xg(q):
                settle(sp)
                sp.dma_start(xg[:, :, :, :, :].rearrange("p t h c n -> p t (h c n)").bitcast(f32),
                             xnT_d[ds(q * TG, TG), :, :].rearrange("t p n -> p t n")).then_inc(S["xg_in"], 16)

            sp.wait_ge(S["fb_over"], 1)
            sp.wait_ge(S["pro_over"], 3)
            for k in range(2):
                sp.wait_ge(S[f"xT_out{k}"], 16 * (NT // 2))
            load_xg(0)
            for t in range(2):
                load_base(t, t % 2)
            for e in range(2, EXP):
                sp.dma_start(wraw[:, e, :, :, :], wffn_d[:, e, :, :, :]).then_inc(S[f"w_in{e}"], 16)

            def group_loads(q, tiles):
                for t in range(tiles):
                    sp.wait_ge(S["mp_free"], q * 8 + (t + 1))
                    load_base(q * TG + (t + 2), t % 2)

            sp.wait_ge(S["g_ps"], 2)
            load_xg(1)
            group_loads(0, TG)
            ov = out_d.rearrange("(g t p) d -> g p t d", t=TG, p=P)

            def store(g):
                sp.wait_ge(S["y_used"], (g + 1) * (EXP * TG))
                settle(sp)
                sp.dma_start(ov[ds(g, 1)].rearrange("g p t d -> p (g t) d"), acc[:, :, :]).then_inc(S["out_sent"], 16)

            with sp.Fori(0, NG - 2) as g:
                sp.wait_ge(S["g_ps"], g * 2 + 4)
                load_xg(g + 2)
                group_loads(g + 1, TG)
                store(g)
            group_loads(NG - 1, 2)
            store(NG - 2)
            store(NG - 1)
            sp.wait_ge(S["out_sent"], NG * 16)

        @block.gpsimd
        def _(pool):
            n = [0]

            def link(ins):
                n[0] += 1
                ins.then_inc(S["pool_link"], 1)
                pool.wait_ge(S["pool_link"], n[0])

            pool.memset(bo4[:, :, :], 0.0).then_inc(S["consts"], 1)
            for dst, m in ((iotaA, CA), (iotaB, CB), (iota_rep, P)):
                pool.iota(dst[:, :, :], [[1, m], [0, dst.shape[2]]], base=0, channel_multiplier=0,
                          allow_small_or_imprecise_dtypes=True).then_inc(S["consts"], 1)
            pool.iota(tbase[:, :], [[P, NT]], base=0, channel_multiplier=0,
                      allow_small_or_imprecise_dtypes=True).then_inc(S["consts"], 1)
            pool.iota(iotaP[:, :], [[1, P]], base=0, channel_multiplier=0,
                      allow_small_or_imprecise_dtypes=True).then_inc(S["consts"], 1)
            link(pool.memset(ident[:, :], 0.0))
            pool.affine_select(out=ident[:, :], in_=ident[:, :], compare_op=ALU.not_equal, fill=1.0, base=0,
                               pattern=[[-1, 128]], channel_multiplier=1).then_inc(S["consts"], 1)
            link(pool.memset(T["ltri"][:, :], 1.0))
            pool.affine_select(out=T["ltri"][:, :], in_=T["ltri"][:, :], compare_op=ALU.is_gt, fill=0.0, base=0,
                               pattern=[[1, NT]], channel_multiplier=-1).then_inc(S["consts"], 1)
            pool.memset(T["ones"][:, :], 1.0).then_inc(S["consts"], 1)
            pool.memset(T["vn"][:, :, :, :], 1.0).then_inc(S["consts"], 1)
            pool.memset(fb_z[:, :], 0.0).then_inc(S["consts"], 1)
            pool.memset(epsc[:, :], LN_EPS).then_inc(S["consts"], 1)
            pool.memset(T["kvs"][:, :, :], 0.0).then_inc(S["consts"], 1)
            pool.iota(posn[:, :], [[1, EC]], base=0, channel_multiplier=EC,
                      allow_small_or_imprecise_dtypes=True).then_inc(S["consts"], 1)
            pool.wait_ge(S["row_in"], 16)
            link(pool.tensor_scalar(T["a1"][:, 0:1], T["rowv"][:P, R_A:R_A + 1], 1.0, None, ALU.add))
            link(pool.tensor_scalar(T["a1"][:, 1:2], T["rowv"][:P, R_A:R_A + 1], -1.0, 1.0, ALU.mult, ALU.add))
            link(pool.tensor_scalar(T["brow"][:, :], T["rowv"][:P, R_BG:R_BG + D], T["a1"][:, 1:2], None, ALU.mult))
            link(pool.tensor_tensor(T["brow"][:, :], T["brow"][:, :], T["rowv"][:P, R_B2:R_B2 + D], ALU.add))
            pool.tensor_copy(br_b[:, :], T["rowv"][:P, R_BR:R_BR + EXP]).then_inc(S["consts"], 1)
            bv = base_d.rearrange("(t p) d -> p t d", p=P)
            for i in range(4):
                pool.wait_ge(S["xn_ready"], 7 * i + 7)
                q = x_all[:, 7 * i:7 * i + 7, :]
                link(pool.tensor_tensor(q, q, bc_out(T["brow"][:, :], 7), ALU.add))
                for t in range(7 * i, 7 * i + 7):
                    link(pool.tensor_scalar(sf32[:, t % 2, 0, :], xn[:, t, :], T["a1"][:, 0:1], None, ALU.mult))
                    link(pool.tensor_tensor(x_all[:, t, :], x_all[:, t, :], sf32[:, t % 2, 0, :], ALU.add))
                pool.dma_start(bv[:, 7 * i:7 * i + 7, :], q).then_inc(S["base_out"], 16)
            pool.sem_inc(S["base_ready"], 1)

            def gather_unit(u, k):
                settle(pool)
                for s in range(US):
                    pool.indirect_dma_start(
                        G[:, u, s, :], None, table_d,
                        bass.IndirectOffsetOnAxis(ap=idx[:, k, u * US + s:u * US + s + 1], axis=0),
                    ).then_inc(S[f"gath{u}"], 16)

            def tile_index(t, k):
                pool.wait_ge(S["win_in"], (t + 1) * 16)
                pool.tensor_copy(idx[:, k:k + 1, :], win[:, ds(t, 1), :, 0]).then_inc(S["idx_ready"], 1)

            tile_index(0, 0)
            pool.wait_ge(S["tb_out0"], 16 * (NT // 4))
            pool.wait_ge(S["tb_out1"], 16 * (NT // 4))
            pool.wait_ge(S["idx_ready"], 1)
            gather_unit(0, 0)
            tile_index(1, 1)
            gather_unit(1, 0)

            pool.wait_ge(S["sf_out0"], 16 * (NT // 4))
            pool.wait_ge(S["sf_out1"], 16 * (NT // 4))
            pool.wait_ge(S["base_out"], 64)
            pool.wait_ge(S["flag_sb"], 1)
            needed = pool.value_load(flag[0:1, 0:1], min_val=0, max_val=1)
            with pool.If(needed > 0):
                with pool.Fori(0, NT) as t:
                    with pool.Fori(0, EC) as j:
                        pool.wait_ge(S["fb_mm"], t * EC + j)
                        pool.tensor_copy(fb_e[:, :], edg[:, ds(j, 1), :].rearrange("p o two -> p (o two)"))\
                            .then_inc(S["fb_idx"], 1)
                        pool.wait_ge(S["fb_idx"], t * EC + (j + 1))
                        settle(pool)
                        pool.indirect_dma_start(fb_g[:, :], None, table_d,
                                                bass.IndirectOffsetOnAxis(ap=fb_e[:, 0:1], axis=0))\
                            .then_inc(S["fb_gath"], 16)
                    pool.wait_ge(S["fb_res"], t + 1)
                    pool.dma_start(self_d[ds(t * P, P), :], fb_a[:, :], accum_op=ALU.add).then_inc(S["fb_add"], 16)
                    pool.wait_ge(S["fb_add"], (t + 1) * 16)
            pool.sem_inc(S["fb_over"], 1)

            def tile_gathers(t, k, more):
                pool.wait_ge(S["idx_ready"], t + 1)
                pool.wait_ge(S["unit_done"], t * 2 - 1)
                gather_unit(0, k)
                pool.wait_ge(S["unit_done"], t * 2)
                if more:
                    tile_index(t + 1, 1 - k)
                gather_unit(1, k)

            with pool.Fori(0, NT // 2 - 1) as i:
                tile_gathers(i * 2 + 1, 1, True)
                tile_gathers(i * 2 + 2, 0, True)
            tile_gathers(NT - 1, 1, False)

        @block.scalar
        def _(act):
            act.wait_ge(S["consts"], 12)
            for i in range(4):
                act.wait_ge(S["ln_var"], 7 * i + 7)
                act.activation(T["rstd"][:, 7 * i:7 * i + 7], T["mv"][:, 7 * i:7 * i + 7, 1], ACT.Sqrt,
                               bias=epsc[:P, :]).then_inc(S["ln_std"], 1)
                act.wait_ge(S["ln_ready"], i + 1)
                with act.Fori(7 * i, 7 * i + 7) as t:
                    act.activation(xn[:, ds(t, 1), :], x_all[:, ds(t, 1), :], ACT.Identity,
                                   bias=T["nmr"][:, ds(t, 1)], scale=T["rstd"][:, ds(t, 1)])\
                        .then_inc(S["xn_ready"], 1)
            act.wait_ge(S["bn_v"], 1)
            act.activation(T["bntmp"][:, :, :, :], T["bntmp"][:, :, :, :], ACT.Sqrt).then_inc(S["bn_sd"], 1)
            act.wait_ge(S["wkv_ready"], 2)
            act.activation(wkv[:, 0, :, :], wsm[:, :, O_KV:O_KV + 512], ACT.Copy).then_inc(S["wrest_hi"], 1)
            act.activation(bkvs[:, 0, :], T["bkv"][:, :], ACT.Copy).then_inc(S["wrest_hi"], 1)
            act.activation(onesr[:, :], T["ones"][0:1, 0:P], ACT.Copy).then_inc(S["wrest_hi"], 1)
            for w, o, m in ((wgT, O_WT, D), (w2s, O_W2, D), (wrs, O_WR, EXP)):
                act.activation(w[:, 0, :, :], wsm[:, :, o:o + m], ACT.Copy).then_inc(S["wrest_hi"], 1)
            act.wait_ge(S["cnt_ps"], 1)
            act.activation(T["cnt_ab"][:, :], CNT[:CA, 0:CB], ACT.Copy).then_inc(S["cnt_sb"], 1)
            act.wait_ge(S["deg_sb"], 1)
            act.activation(T["deg"][:, :], T["deg"][:, :], ACT.Sqrt).then_inc(S["deg_sqrt"], 1)
            act.wait_ge(S["dinv_sb"], 1)
            act.wait_ge(S["base_ready"], 1)

            def table_pair(i, k):
                act.wait_ge(S["xs_ready"], i * 2 + (k + 1))
                after(act, f"tb_out{k}", i * 16)
                act.activation(tb16[:, k, :, 0, :], xs32[:, k, :, :], ACT.Copy).then_inc(S["xs_hi"], 1)
                after(act, f"sf_out{k}", i * 16)
                for m in range(2):
                    t = i * 4 + (2 * k + m)
                    act.activation(sf32[:, k, m:m + 1, :], xn[:, ds(t, 1), :],
                                   ACT.Copy, scale=T["sd"][:, ds(t, 1)]).then_inc(S["sf_ready"], 1)
                act.wait_ge(S["tb_ready"], i * 2 + (k + 1))
                rows = ds(i * (4 * P) + 2 * k * P, 2 * P)
                act.dma_start(table_d[rows, :].rearrange("(m p) d -> p m d", p=P),
                              tb16[:, k, :, :, :].rearrange("p m h d -> p m (h d)")).then_inc(S[f"tb_out{k}"], 16)
                act.wait_ge(S["sf_ready"], i * 4 + (2 * k + 2))
                act.dma_start(self_d[rows, :].rearrange("(m p) d -> p m d", p=P),
                              sf32[:, k, :, :]).then_inc(S[f"sf_out{k}"], 16)

            with act.Fori(0, NT // 4) as i:
                for k in range(2):
                    table_pair(i, k)

            def kv_copy(t, k):
                after(act, "tr_ps", t - 1)
                act.activation(T["xc"][:, k:k + 1, :], xn[:, ds(t, 1), :], ACT.Copy).then_inc(S["xc_ready"], 1)

            def kv_high(t, k, i):
                act.wait_ge(S["tr_ps"], t + 1)
                after(act, "kv_ps", t - 1)
                after(act, f"xT_out{k}", i * 16)
                act.activation(xT[:, k, 0, :, :], TRP[k][:, 0:2 * P].rearrange("p (c n) -> p c n", c=2), ACT.Copy)\
                    .then_inc(S["xT_hi"], 1)

            def kv_square(t, k):
                act.wait_ge(S["kv_ps"], t + 1)
                after(act, "s2_ready", t)
                act.activation(T["sq"][:, :], KVP[k][:P, :], ACT.Square).then_inc(S["sq_ready"], 1)
                act.wait_ge(S["xT_lo"], t + 1)
                act.dma_start(xnT_d[ds(t, 1), :, :].rearrange("o p n -> p o n"),
                              xT[:, k, :, :, :].rearrange("p (o h) c n -> p o (h c n)", o=1).bitcast(f32))\
                    .then_inc(S[f"xT_out{k}"], 16)
                act.wait_ge(S["s2_ready"], t + 1)
                after(act, "kn_ready", 2 * t)
                act.activation(T["s2"][:, 1, :], T["s2"][:, 0, :], ACT.Sqrt, bias=epsc[:P, :], scale=1.0 / HC)\
                    .then_inc(S["sd_ready"], 1)

            def kv_turn(t, k, i):
                if not isinstance(t, int) or t + 1 < NT:
                    kv_copy(t + 1, 1 - k)
                if not isinstance(t, int) or t < NT:
                    kv_high(t, k, i)
                if not isinstance(t, int) or t >= 1:
                    kv_square(t - 1, 1 - k)

            kv_copy(0, 0)
            kv_turn(0, 0, 0)
            kv_turn(1, 1, 0)
            with act.Fori(1, NT // 2 - 1) as i:
                kv_turn(i * 2, 0, i)
                kv_turn(i * 2 + 1, 1, i)
            for t in range(NT - 2, NT + 1):
                kv_turn(t, t % 2, t // 2)
            act.wait_ge(S["wm_ps"], 1)
            for c in range(2):
                act.activation(wms[:, 0, c, :], KVP[c][:, 0:D], ACT.Copy).then_inc(S["wm_hi"], 1)
            act.sem_inc(S["pro_over"], 1)
            act.wait_ge(S["pro_over"], 3)
            act.wait_ge(S["fb_over"], 1)
            for k in range(2):
                act.wait_ge(S[f"xT_out{k}"], 16 * (NT // 2))

            def weights_high(e):
                act.wait_ge(S[f"w_in{e}"], 16)
                act.activation(whi[:, e, :, :, :], wst[:, e, :, :, :] if e < 2 else wraw[:, e, :, :, :],
                               ACT.Copy).then_inc(S["w_hi"], 1)

            def expert_relu(l, g, e, after_mlp=False):
                name, buf, banks = (("l1", t1, H1P), ("l2", t2, H2P))[l]
                m = g * EXP + e
                after(act, name + "_lo", m)
                if after_mlp:
                    act.wait_ge(S["g_lo"], g + 2)
                for c in range(2):
                    act.wait_ge(S[name + "_ps"], m * 2 + (c + 1))
                    act.activation(buf[:, c, :], banks[c][:, 0:GN], ACT.Relu, bias=bnbi[:, l, e, c:c + 1],
                                   scale=bnsc[:, l, e, c:c + 1]).then_inc(S[name + "_act"], 1)

            def expert_high(l, g, e):
                name, buf, hi = (("l1", t1, h1), ("l2", t2, h2))[l]
                m = g * EXP + e
                act.wait_ge(S[name + "_act"], m * 2 + 2)
                if l:
                    after(act, "y_ps", m * TG)
                act.activation(hi[:, 0, :, :], buf[:, :, :], ACT.Copy).then_inc(S[name + "_hi"], 1)

            def mlp(q):
                after(act, "l2_lo", (q - 1) * EXP)
                for c in range(2):
                    act.wait_ge(S["g_ps"], q * 2 + (c + 1))
                    act.activation(t2[:, c, :], H2P[c][:, 0:GN], ACT.Gelu, bias=cm[:, c:c + 1]).then_inc(S["g_act"], 1)
                act.wait_ge(S["g_act"], q * 2 + 2)
                after(act, "mp_ps", q * 8 - 4)
                act.activation(gT[:, 0, :, :], t2[:, :, :], ACT.Copy).then_inc(S["g_hi"], 1)

            def agg_low(q, t):
                act.wait_ge(S["unit_done"], q * 8 + (2 * t + 2))
                after(act, "agg_evac", q * TG + t)
                act.activation(alo[:, :], AGG[:P, D:2 * D], ACT.Copy,
                               scale=rd[:, ds(q * TG + t, 1)]).then_inc(S["alo_ready"], 1)

            def agg_high(q, t):
                after(act, "mp_ps", q * 8 + t if t else q * 8 - 4)
                act.wait_ge(S["mt_ps"], (mt_count(q, A_AT[t]) if t else a0_count(q)) + 1)
                act.activation(aT[:, 0, :, :], MT[:, :].rearrange("p (c n) -> p c n", c=2), ACT.Copy)\
                    .then_inc(S["mt_hi"], 1)

            def x2_high(q, t):
                after(act, "l1_ps", q * 16)
                act.wait_ge(S["mt_ps"], mt_count(q, X_AT[t]) + 1)
                act.activation(x2T[:, 0, :, t * P:t * P + P], MT[:, :].rearrange("p (c n) -> p c n", c=2), ACT.Copy)\
                    .then_inc(S["mt_hi"], 1)

            def deviation(q, t):
                act.wait_ge(S["var_ready"], q * TG + (t + 1))
                act.activation(sd2[:, t:t + 1], mv2[:, t, 1:2], ACT.Sqrt, bias=epsc[:P, :]).then_inc(S["std_ready"], 1)

            def norm(q, t):
                act.wait_ge(S["nmr_ready"], q * TG + (t + 1))
                act.activation(xn2[:, t, :], x1[:, t, :], ACT.Identity, bias=nm2[:, t:t + 1],
                               scale=rs2[:, t:t + 1]).then_inc(S["xn2_ready"], 1)

            def softmax(q):
                act.wait_ge(S["r_sub"], q + 1)
                act.activation(lg2[:, :, :], lg[:, :, :], ACT.Exp).then_inc(S["r_exp"], 1)

            agg_low(0, 0)
            agg_high(0, 0)
            mlp(0)
            weights_high(0)
            for t in range(TG):
                if t < TG - 1:
                    agg_low(0, t + 1)
                deviation(0, t)
                norm(0, t)
                if t < TG - 1:
                    agg_high(0, t + 1)
                weights_high(t + 1)
            for t in range(TG):
                x2_high(0, t)
                if t < 3:
                    weights_high(t + 5)
            agg_low(1, 0)
            softmax(0)

            expert_relu(0, 0, 0)
            expert_high(0, 0, 0)

            def group(g, prepare, ahead):
                q = g + 1
                if prepare:
                    agg_high(q, 0)
                    mlp(q)
                expert_relu(0, g, 1)
                expert_relu(1, g, 0, prepare)
                expert_high(0, g, 1)
                expert_high(1, g, 0)
                for e in range(1, EXP - 1):
                    if prepare and e in (1, 3, 5):
                        agg_low(q, e // 2 + 1)
                    expert_relu(0, g, e + 1)
                    if prepare and e == 6:
                        deviation(q, 3)
                    expert_relu(1, g, e)
                    if prepare and e in NORM_AT:
                        norm(q, NORM_AT[e])
                    if prepare and e == 6:
                        x2_high(q, 0)
                    expert_high(0, g, e + 1)
                    expert_high(1, g, e)
                    if prepare:
                        if e in (1, 2, 4):
                            deviation(q, e // 2)
                        if e in (1, 3, 5):
                            agg_high(q, e // 2 + 1)
                        if e == 6:
                            x2_high(q, 1)
                if ahead:
                    agg_low(q + 1, 0)
                if prepare:
                    norm(q, 3)
                    x2_high(q, 2)
                expert_relu(1, g, EXP - 1)
                if prepare:
                    x2_high(q, 3)
                expert_high(1, g, EXP - 1)
                if prepare:
                    expert_relu(0, q, 0)
                    expert_high(0, q, 0)
                    softmax(q)

            with act.Fori(0, NG - 2) as g:
                group(g, True, True)
            group(NG - 2, True, False)
            group(NG - 1, False, False)

        @block.vector
        def _(dve):
            n = [0]

            def link(ins):
                n[0] += 1
                ins.then_inc(S["dve_link"], 1)
                dve.wait_ge(S["dve_link"], n[0])

            dve.wait_ge(S["edges_in"], 16)
            dve.wait_ge(S["nxt_in"], 16)
            dst = edg[:, :, 1]
            dve.tensor_scalar(ab_i[:, 0, :], dst, 6, None, ALU.logical_shift_right)
            link(dve.tensor_scalar(ab_i[:, 1, :], dst, 63, None, ALU.bitwise_and))
            dve.tensor_copy(ab_f[:, :, :], ab_i[:, :, :])
            link(dve.memset(viol[:, :], 0.0))
            dve.tensor_tensor(viol[:, 0:EC - 1], edg[:, 0:EC - 1, 1], edg[:, 1:EC, 1], ALU.is_gt)
            link(dve.tensor_tensor(viol[0:EP - 1, EC - 1:EC], edg[0:EP - 1, EC - 1, 1:2], T["nxt"][0:EP - 1, 1:2],
                                   ALU.is_gt))
            link(dve.reduce_sum(T["vs"][:, 0:1], viol[:, :], axis=AX))
            for i in range(4):
                dve.wait_ge(S[f"x_in{i}"], 16)
                after(dve, "ln_var", 7 * i)
                for t in range(7):
                    ins = dve.bn_stats(T["bst"][:, t, :], x_all[:, 7 * i + t, :])
                link(ins)
                for t in range(7):
                    dve.bn_aggr(T["mv"][:, 7 * i + t, :], T["bst"][:, t, :]).then_inc(S["ln_var"], 1)
            for i in range(4):
                w = slice(7 * i, 7 * i + 7)
                dve.wait_ge(S["ln_std"], i + 1)
                link(dve.reciprocal(T["rstd"][:, w], T["rstd"][:, w]))
                dve.scalar_tensor_tensor(out=T["nmr"][:, w], in0=T["mv"][:, w, 0], scalar=-1.0, in1=T["rstd"][:, w],
                                         op0=ALU.mult, op1=ALU.mult).then_inc(S["ln_ready"], 1)
            dve.wait_ge(S["bn_in"], 16)
            bnv = T["bn"]
            dve.tensor_scalar(T["bntmp"][:, :, :, :], bnv[:, :, 4, :, :], BN_EPS, None, ALU.add).then_inc(S["bn_v"], 1)

            def one_hots(c, k):
                after(dve, "one_free", c - 1)
                dve.tensor_tensor(oneA[:, k, :, :], iotaA[:, :, :],
                                  ab_f[:, 0, ds(c * CH, CH)].rearrange("p (o m) -> p o m", o=1)
                                  .to_broadcast([EP, CA, CH]), ALU.is_equal).then_inc(S["one_ready"], 1)
                dve.tensor_tensor(oneB[:, k, :, :], iotaB[:, :, :],
                                  ab_f[:, 1, ds(c * CH, CH)].rearrange("p (o m) -> p o m", o=1)
                                  .to_broadcast([EP, CB, CH]), ALU.is_equal).then_inc(S["one_ready"], 1)

            dve.wait_ge(S["consts"], 15)
            one_hots(0, 0)
            with dve.Fori(0, NCH // 2) as i:
                one_hots(i * 2 + 1, 1)
                one_hots(i * 2 + 2, 0)

            dve.wait_ge(S["bn_sd"], 1)
            link(dve.reciprocal(T["bntmp"][:, :, :, :], T["bntmp"][:, :, :, :]))
            link(dve.tensor_tensor(bnsc[:, :, :, :], T["bntmp"][:, :, :, :], bnv[:, :, 1, :, :], ALU.mult))
            link(dve.tensor_tensor(T["bntmp"][:, :, :, :], bnv[:, :, 0, :, :], bnv[:, :, 3, :, :], ALU.subtract))
            link(dve.tensor_tensor(T["bntmp"][:, :, :, :], T["bntmp"][:, :, :, :], bnsc[:, :, :, :], ALU.mult))
            dve.tensor_tensor(bnbi[:, :, :, :], T["bntmp"][:, :, :, :], bnv[:, :, 2, :, :], ALU.add)\
                .then_inc(S["bn_ready"], 1)
            dve.wait_ge(S["wsm_in"], 16)
            for c in range(2):
                wv = wsm[:, c, O_KV:O_KV + 512].rearrange("p (h d) -> p h d", d=HC)
                link(dve.reduce_sum(T["gm"][:, c, :], wv, axis=AX))
                link(dve.tensor_scalar(T["gm"][:, c, :], T["gm"][:, c, :], -1.0 / HC, None, ALU.mult))
                ins = dve.tensor_tensor(wv, wv, bc_in(T["gm"][:, c, :], HC), ALU.add)
                if c == 0:
                    link(ins)
                else:
                    ins.then_inc(S["wkv_ready"], 1)
            brow_v = T["rowv"][0:1, R_BKV:R_BKV + 512].rearrange("p (h d) -> p h d", d=HC)
            link(dve.reduce_sum(T["gb"][:, :], brow_v, axis=AX))
            link(dve.tensor_scalar(T["gb"][:, :], T["gb"][:, :], -1.0 / HC, None, ALU.mult))
            dve.tensor_tensor(T["bkv"][:, :].rearrange("p (h d) -> p h d", d=HC), brow_v, bc_in(T["gb"][:, :], HC),
                              ALU.add).then_inc(S["wkv_ready"], 1)

            dve.wait_ge(S["cnt_in"], 16)
            link(dve.reduce_sum(T["tot"][:, 0:1], T["cnt_t"][:, :], axis=AX))
            dve.tensor_scalar(T["tot"][:, 1:2], T["tot"][:, 0:1], float(WIN), None, ALU.is_gt).then_inc(S["tot_sb"], 1)
            dve.wait_ge(S["cntT_ps"], 1)
            link(dve.tensor_scalar(T["deg"][:, :], CNT[:P, 128:128 + NT], 1.0, None, ALU.add))
            dve.tensor_scalar(T["deg"][:, :], T["deg"][:, :], 1.0, None, ALU.max).then_inc(S["deg_sb"], 1)
            dve.wait_ge(S["start_ps"], 1)
            dve.tensor_scalar(starts[:, :], MSC[0:1, M_ST:M_ST + NT], float(E - WIN), None, ALU.min)\
                .then_inc(S["starts_sb"], 1)
            dve.tensor_scalar(T["stf"][:, :], MSC[0:1, M_ST:M_ST + NT], float(E - WIN), None, ALU.min)\
                .then_inc(S["stf_sb"], 1)
            dve.wait_ge(S["deg_sqrt"], 1)
            link(dve.reciprocal(T["dinv"][:, :], T["deg"][:, :]))
            link(dve.tensor_scalar(T["dS"][:, :], T["dinv"][:, :], SCALE, None, ALU.mult))
            link(dve.tensor_scalar(T["rstd"][:, :], T["dinv"][:, :], T["a1"][:, 1:2], None, ALU.mult))
            link(dve.tensor_scalar(rd[:, :], T["rstd"][:, :], 1.0 / SCALE, None, ALU.mult))
            dve.tensor_tensor(T["sd"][:, :], T["dinv"][:, :], T["rstd"][:, :], ALU.mult).then_inc(S["dinv_sb"], 1)

            with dve.Fori(0, NT // 4) as i:
                dve.wait_ge(S["tb_ready"], i * 2)
                for k in range(2):
                    for m in range(2):
                        t = i * 4 + (2 * k + m)
                        ins = dve.tensor_scalar(xs32[:, k, m:m + 1, :], xn[:, ds(t, 1), :], T["dS"][:, ds(t, 1)],
                                                None, ALU.mult)
                    ins.then_inc(S["xs_ready"], 1)
                for k in range(2):
                    dve.wait_ge(S["xs_hi"], i * 2 + (k + 1))
                    dve.tensor_tensor(tb16[:, k, :, 1, :], xs32[:, k, :, :], tb16[:, k, :, 0, :], ALU.subtract)\
                        .then_inc(S["tb_ready"], 1)
            dve.wait_ge(S["flag_ps"], 1)
            dve.tensor_copy(stbc[:, :], MSC[:, M_BC:M_BC + NT])
            dve.tensor_scalar(flag[:, :], MSC[0:1, M_FL:M_FL + 1], 0.5, None, ALU.is_gt).then_inc(S["flag_sb"], 1)

            dve.wait_ge(S["wrest_hi"], 6)
            for w, o, m in ((wkv, O_KV, 512), (wgT, O_WT, D), (w2s, O_W2, D), (wrs, O_WR, EXP)):
                dve.tensor_tensor(w[:, 1, :, :], wsm[:, :, o:o + m], w[:, 0, :, :].bitcast(f32), ALU.subtract)\
                    .then_inc(S["wrest_lo"], 1)
            dve.tensor_tensor(bkvs[:, 1, :], T["bkv"][:, :], bkvs[:, 0, :].bitcast(f32), ALU.subtract)\
                .then_inc(S["wrest_lo"], 1)

            def kv_low(t, k):
                dve.wait_ge(S["xT_hi"], t + 1)
                dve.tensor_tensor(xT[:, k, 1, :, :], TRP[k][:, 0:2 * P].rearrange("p (c n) -> p c n", c=2),
                                  xT[:, k, 0, :, :].bitcast(f32), ALU.subtract).then_inc(S["xT_lo"], 1)

            def kv_norm(t, k):
                dve.wait_ge(S["sq_ready"], t + 1)
                dve.reduce_sum(T["s2"][:, 0, :], T["sq"][:, :].rearrange("p (h d) -> p h d", d=HC), axis=AX)\
                    .then_inc(S["s2_ready"], 1)
                dve.wait_ge(S["sd_ready"], t + 1)
                dve.reciprocal(T["s2"][:, 1, :], T["s2"][:, 1, :]).then_inc(S["dve_loop_link"], 1)
                after(dve, "kv_sum", t - 1)
                dve.wait_ge(S["dve_loop_link"], t + 1)
                dve.tensor_tensor(T["kn"][:, k, :].rearrange("p (h d) -> p h d", d=HC),
                                  KVP[k][:P, 0:D].rearrange("p (h d) -> p h d", d=HC),
                                  bc_in(T["s2"][:, 1, 0:8], HC), ALU.mult).then_inc(S["kn_ready"], 1)
                for h in range(2):
                    ins = dve.tensor_tensor(T["vn"][:, k, h, 0:128].rearrange("p (h d) -> p h d", d=HC),
                                            KVP[k][:P, D + 128 * h:D + 128 * h + 128].rearrange("p (h d) -> p h d", d=HC),
                                            bc_in(T["s2"][:, 1, 8 + 4 * h:12 + 4 * h], HC), ALU.mult)
                ins.then_inc(S["kn_ready"], 1)

            def kv_turn(t, k):
                if not isinstance(t, int) or t < NT:
                    kv_low(t, k)
                if not isinstance(t, int) or t >= 1:
                    kv_norm(t - 1, 1 - k)

            kv_turn(0, 0)
            kv_turn(1, 1)
            with dve.Fori(1, NT // 2 - 1) as i:
                kv_turn(i * 2, 0)
                kv_turn(i * 2 + 1, 1)
            for t in range(NT - 2, NT + 1):
                kv_turn(t, t % 2)

            dve.wait_ge(S["flag_sb"], 1)
            needed = dve.value_load(flag[0:1, 0:1], min_val=0, max_val=1)
            with dve.If(needed > 0):
                with dve.Fori(0, NT) as t:
                    with dve.Fori(0, EC) as j:
                        q = t * EC + j
                        rel, lt, off = fb_s[:, 0:1], fb_s[:, 1:2], fb_s[:, 2:3]
                        dve.tensor_scalar(rel, posn[:, ds(j, 1)], stbc[:EP, ds(t, 1)], 0.0, ALU.subtract, ALU.is_ge)
                        dve.tensor_scalar(lt, posn[:, ds(j, 1)], stbc[:EP, ds(t, 1)], float(WIN), ALU.subtract,
                                          ALU.is_lt)
                        dve.tensor_scalar(off, edg[:, ds(j, 1), 1], tbase[:EP, ds(t, 1)], None, ALU.subtract)\
                            .then_inc(S["fb_link"], 1)
                        dve.wait_ge(S["fb_link"], q * 3 + 1)
                        dve.tensor_tensor(rel, rel, lt, ALU.mult).then_inc(S["fb_link"], 1)
                        dve.wait_ge(S["fb_link"], q * 3 + 2)
                        dve.tensor_scalar(lt, rel, -1.0, 1.0, ALU.mult, ALU.add).then_inc(S["fb_link"], 1)
                        dve.wait_ge(S["fb_link"], q * 3 + 3)
                        dve.wait_ge(S["fb_mm"], q)
                        dve.tensor_scalar(fb_o[:, :], iotaP[:EP, :], off, lt, ALU.is_equal, ALU.mult)\
                            .then_inc(S["fb_oh"], 1)
                    dve.wait_ge(S["fb_sum"], t + 1)
                    dve.wait_ge(S["fb_add"], t * 16)
                    dve.tensor_scalar(fb_a[:, :], CNT[:P, D:2 * D], rd[:, ds(t, 1)], None, ALU.mult)\
                        .then_inc(S["fb_link2"], 1)
                    dve.wait_ge(S["fb_link2"], t + 1)
                    dve.scalar_tensor_tensor(out=fb_a[:, :], in0=CNT[:P, 0:D], scalar=rd[:, ds(t, 1)], in1=fb_a[:, :],
                                             op0=ALU.mult, op1=ALU.add).then_inc(S["fb_res"], 1)

            dve.wait_ge(S["kv_sum"], NT)
            vg, vb = T["rowv"][:, R_VG:R_VG + 128], T["rowv"][:, R_VB:R_VB + 128]
            kg, kb = T["col"][:, 4:5], T["col"][:, 5:6]
            for h in range(2):
                A, sk, sv = KA[:, 129 * h:129 * h + 128], KA[:, 129 * h + 128:129 * h + 129], KS[:, 128 * h:128 * h + 128]
                u, v = T["kvt"][:, 0, :], T["kvt"][:, 1, :]
                link(dve.tensor_tensor(u, A, vg, ALU.mult))
                link(dve.tensor_copy(T["rb"][:, 0:1], sk))
                link(dve.scalar_tensor_tensor(out=u, in0=vb, scalar=T["rb"][:, 0:1], in1=u, op0=ALU.mult, op1=ALU.add))
                link(dve.tensor_tensor(v, sv, vg, ALU.mult))
                link(dve.scalar_tensor_tensor(out=v, in0=vb, scalar=float(N), in1=v, op0=ALU.mult, op1=ALU.add))
                link(dve.tensor_scalar(v, v, kb, 1.0 / N, ALU.mult, ALU.mult))
                link(dve.tensor_scalar(u, u, kg, 1.0 / N, ALU.mult, ALU.mult))
                for b in range(4):
                    w = slice(32 * b, 32 * b + 32)
                    ins = dve.tensor_tensor(T["kvs"][w, h, w], T["kvt"][w, 0, w], T["kvt"][w, 1, w], ALU.add)
                if h == 0:
                    link(ins)
                else:
                    ins.then_inc(S["kvs_sb"], 1)
            dve.wait_ge(S["rT_ps"], 1)
            for h in range(2):
                link(dve.tensor_copy(T["rT"][:, h, :], TRP[h][:, 0:D]))
                c = slice(128 * h, 128 * h + 128)
                dve.tensor_tensor(T["rT"][:, h, c], T["rT"][:, h, c], ident[:, :], ALU.add).then_inc(S["rT_sb"], 1)
            dve.tensor_copy(T["rb"][:, :], MSC[:, M_CM:M_CM + 2]).then_inc(S["rT_sb"], 1)
            dve.wait_ge(S["wm_ps"], 1)
            dve.wait_ge(S["wm_hi"], 2)
            for c in range(2):
                dve.tensor_tensor(wms[:, 1, c, :], KVP[c][:, 0:D], wms[:, 0, c, :].bitcast(f32), ALU.subtract)\
                    .then_inc(S["wm_lo"], 1)
            dve.tensor_tensor(cm[:, :], MSC[:, M_CM + 2:M_CM + 4], T["col"][:, 2:4], ALU.add).then_inc(S["wm_lo"], 1)

            dve.sem_inc(S["pro_over"], 1)
            dve.wait_ge(S["pro_over"], 3)
            dve.wait_ge(S["fb_over"], 1)
            for k in range(2):
                dve.wait_ge(S[f"xT_out{k}"], 16 * (NT // 2))

            def weights_low(e):
                dve.wait_ge(S["w_hi"], e + 1)
                dve.tensor_tensor(wlo[:, e, :, :, :], wst[:, e, :, :, :] if e < 2 else wraw[:, e, :, :, :],
                                  whi[:, e, :, :, :].bitcast(f32), ALU.subtract).then_inc(S["w_lo"], 1)

            def one_hot(q, u):
                t = q * TG + u // 2
                if u % 2 == 0:
                    dve.wait_ge(S["win_in"], t * 16 + 16)
                    after(dve, "oh_ready", q * 8 + u)
                    dve.tensor_scalar(dl[:, :], win[:, ds(t, 1), :, 1].rearrange("p o s -> p (o s)"),
                                      tbase[:, ds(t, 1)], None, ALU.subtract).then_inc(S["dl_ready"], 1)
                    dve.wait_ge(S["dl_ready"], t + 1)
                after(dve, "unit_done", q * 8 + (u - 1))
                k = u % 2
                dve.tensor_tensor(oh[:, k, :, :], iota_rep[:, :, :], bc_out(dl[:, k * US:k * US + US], P),
                                  ALU.is_equal).then_inc(S["oh_ready"], 1)

            def cut_low(name, g, e):
                buf, hi = ((t1, h1), (t2, h2))[name == "l2"]
                dve.wait_ge(S[name + "_hi"], g * EXP + (e + 1))
                dve.tensor_tensor(hi[:, 1, :, :], buf[:, :, :], hi[:, 0, :, :].bitcast(f32), ALU.subtract)\
                    .then_inc(S[name + "_lo"], 1)

            def mlp(q):
                dve.wait_ge(S["g_hi"], q + 1)
                dve.tensor_tensor(gT[:, 1, :, :], t2[:, :, :], gT[:, 0, :, :].bitcast(f32), ALU.subtract)\
                    .then_inc(S["g_lo"], 1)

            def agg_add(q, t):
                i = q * TG + t
                if t == 0:
                    after(dve, "mt_ps", mt_count(q - 1, A_AT[3]) + 1)
                else:
                    dve.wait_ge(S["mt_ps"], (mt_count(q, A_AT[t - 1]) if t > 1 else a0_count(q)) + 1)
                dve.wait_ge(S["alo_ready"], i + 1)
                dve.scalar_tensor_tensor(out=ag1[:, :], in0=AGG[:P, 0:D], scalar=rd[:, ds(i, 1)], in1=alo[:, :],
                                         op0=ALU.mult, op1=ALU.add).then_inc(S["agg_evac"], 1)
                dve.wait_ge(S["agg_evac"], i + 1)
                dve.wait_ge(S[f"bs_in{t % 2}"], q * 64 + (t // 2 * 32 + 32))
                dve.tensor_tensor(ag2[:, :], ag1[:, :], bs[:, t % 2, 1, :], ALU.add).then_inc(S["ag_ready"], 1)

            def agg_cut(q, t):
                dve.wait_ge(S["mt_hi"], q * 8 + (t + 1))
                dve.tensor_tensor(aT[:, 1, :, :], MT[:, :].rearrange("p (c n) -> p c n", c=2),
                                  aT[:, 0, :, :].bitcast(f32), ALU.subtract).then_inc(S["mt_lo"], 1)

            def x2_cut(q, t):
                w = slice(t * P, t * P + P)
                dve.wait_ge(S["mt_hi"], q * 8 + (t + 5))
                dve.tensor_tensor(x2T[:, 1, :, w], MT[:, :].rearrange("p (c n) -> p c n", c=2),
                                  x2T[:, 0, :, w].bitcast(f32), ALU.subtract).then_inc(S["mt_lo"], 1)

            def residual(q, t):
                dve.wait_ge(S["mp_ps"], q * 8 + (t + 1))
                dve.tensor_tensor(x1[:, t, :], MP, bs[:, t % 2, 0, :], ALU.add).then_inc(S["mp_free"], 1)
                dve.wait_ge(S["mp_free"], q * 8 + (t + 1))
                dve.bn_stats(bst2[:, :], x1[:, t, :]).then_inc(S["st_ready"], 1)
                dve.wait_ge(S["st_ready"], q * TG + (t + 1))
                settle(dve)
                dve.bn_aggr(mv2[:, t, :], bst2[:, :]).then_inc(S["var_ready"], 1)

            def scales(q, t):
                dve.wait_ge(S["std_ready"], q * TG + (t + 1))
                dve.reciprocal(rs2[:, t:t + 1], sd2[:, t:t + 1]).then_inc(S["rs_ready"], 1)
                dve.wait_ge(S["rs_ready"], q * TG + (t + 1))
                dve.scalar_tensor_tensor(out=nm2[:, t:t + 1], in0=mv2[:, t, 0:1], scalar=-1.0, in1=rs2[:, t:t + 1],
                                         op0=ALU.mult, op1=ALU.mult).then_inc(S["nmr_ready"], 1)

            def softmax(q):
                dve.wait_ge(S["r_ps"], q + 1)
                dve.tensor_tensor(lg[:, :, :], ML.rearrange("p (t e) -> p t e", t=TG), bc_out(br_b[:, :], TG), ALU.add)\
                    .then_inc(S["r_lg"], 1)
                dve.wait_ge(S["r_lg"], q + 1)
                dve.reduce_max(mx[:, :], lg[:, :, :], axis=AX).then_inc(S["r_max"], 1)
                dve.wait_ge(S["r_max"], q + 1)
                dve.tensor_tensor(lg[:, :, :], lg[:, :, :], bc_in(mx[:, :], EXP), ALU.subtract)\
                    .then_inc(S["r_sub"], 1)
                dve.wait_ge(S["r_exp"], q + 1)
                dve.reduce_sum(sm[:, :], lg2[:, :, :], axis=AX).then_inc(S["r_sum"], 1)
                dve.wait_ge(S["r_sum"], q * 2 + 1)
                dve.reciprocal(sm[:, :], sm[:, :]).then_inc(S["r_sum"], 1)

            def router_weights(q):
                dve.wait_ge(S["r_sum"], q * 2 + 2)
                after(dve, "y_used", q * (EXP * TG))
                dve.tensor_tensor(wn[:, :, :], lg2[:, :, :], bc_in(sm[:, :], EXP), ALU.mult).then_inc(S["w_ready"], 1)

            def w_transposed(g, last):
                dve.wait_ge(S["mt_ps"], mt_count(g, W_AT - last) + 1)
                dve.tensor_copy(wT[:, :], MT[0:TG * EXP, 0:P]).then_inc(S["mt_lo"], 1)

            def add_bias(g, t):
                dve.wait_ge(S["mp_ps"], g * 8 + (t + 5))
                dve.tensor_tensor(xb[:, t, :], MP, x1[:, t, :], ALU.add).then_inc(S["mp_free"], 1)

            def add_expert(g, e):
                for t in range(TG):
                    i = g * (EXP * TG) + (e * TG + t)
                    if t % 2 == 0:
                        dve.wait_ge(S["y_ps"], i + 2)
                    if e == 0:
                        dve.wait_ge(S["mp_free"], g * 8 + (t + 5))
                        dve.wait_ge(S["w_ready"], g + 1)
                        after(dve, "out_sent", g * 16)
                    else:
                        dve.wait_ge(S["y_used"], i - 3)
                    dve.scalar_tensor_tensor(out=acc[:, t, :], in0=YP[t], scalar=wn[:, t, e:e + 1],
                                             in1=xb[:, t, :] if e == 0 else acc[:, t, :],
                                             op0=ALU.mult, op1=ALU.add).then_inc(S["y_used"], 1)

            one_hot(0, 0)
            one_hot(0, 1)
            agg_add(0, 0)
            one_hot(0, 2)
            agg_cut(0, 0)
            one_hot(0, 3)
            mlp(0)
            weights_low(0)
            for t in range(TG):
                if t < TG - 1:
                    agg_add(0, t + 1)
                residual(0, t)
                if t < TG - 1:
                    one_hot((t + 2) // 4, (2 * t + 4) % 8)
                scales(0, t)
                if t < TG - 1:
                    agg_cut(0, t + 1)
                    one_hot((t + 2) // 4, (2 * t + 5) % 8)
                weights_low(t + 1)
            for t in range(TG):
                x2_cut(0, t)
                if t < 3:
                    weights_low(t + 5)
            agg_add(1, 0)
            one_hot(1, 2)
            softmax(0)
            router_weights(0)

            cut_low("l1", 0, 0)

            def group(g, prepare, ahead):
                q = g + 1
                if prepare:
                    agg_cut(q, 0)
                w_transposed(g, int(not prepare))
                if prepare:
                    mlp(q)
                add_bias(g, 0)
                if prepare:
                    one_hot(q, 3)
                add_bias(g, 1)
                cut_low("l1", g, 1)
                cut_low("l2", g, 0)
                for e in range(1, EXP - 1):
                    if e == 1:
                        add_bias(g, 2)
                    if prepare and e < 5:
                        one_hot(q, e + 3)
                    if ahead and e >= 5:
                        one_hot(q + 1, e - 5)
                    if prepare and e in NORM_AT:
                        scales(q, NORM_AT[e])
                    if prepare and e in (1, 3, 5):
                        agg_add(q, e // 2 + 1)
                    if e == 1:
                        add_bias(g, 3)
                    if prepare and e == 6:
                        residual(q, 3)
                    cut_low("l1", g, e + 1)
                    if prepare and e == 6:
                        x2_cut(q, 0)
                    if prepare and e in (1, 2, 4):
                        residual(q, e // 2)
                    cut_low("l2", g, e)
                    if prepare and e in (1, 3, 5):
                        agg_cut(q, e // 2 + 1)
                    if prepare and e == 6:
                        scales(q, 3)
                        x2_cut(q, 1)
                    add_expert(g, e - 1)
                if ahead:
                    one_hot(q + 1, 2)
                    agg_add(q + 1, 0)
                if prepare:
                    x2_cut(q, 2)
                    x2_cut(q, 3)
                cut_low("l2", g, EXP - 1)
                add_expert(g, EXP - 2)
                if prepare:
                    cut_low("l1", q, 0)
                    softmax(q)
                add_expert(g, EXP - 1)
                if prepare:
                    router_weights(q)

            with dve.Fori(0, NG - 2) as g:
                group(g, True, True)
            group(NG - 2, True, False)
            group(NG - 1, False, False)

        @block.tensor
        def _(pe):
            def count(c, k, first=False, last=False):
                pe.wait_ge(S["one_ready"], c * 2 + 2)
                for j in range(CH):
                    ins = pe.matmul(CNT[:CA, 0:CB], oneA[:, k, :, j], oneB[:, k, :, j],
                                    start=first and j == 0, stop=last and j == CH - 1, skip_group_check=True)
                ins.then_inc(S["one_free"], 1)

            count(0, 0, first=True)
            with pe.Fori(0, NCH // 2 - 1) as i:
                count(i * 2 + 1, 1)
                count(i * 2 + 2, 0)
            count(NCH - 2, 1)
            count(NCH - 1, 0, last=True)
            pe.wait_ge(S["one_free"], NCH)
            pe.sem_inc(S["cnt_ps"], 1)

            ones = T["ones"]
            pe.wait_ge(S["consts"], 15)
            pe.wait_ge(S["cnt_in"], 16)
            pe.transpose(CNT[:P, 128:128 + NT], T["cnt_t"][:, :], ident[:NT, :NT]).then_inc(S["cntT_ps"], 1)
            pe.wait_ge(S["tot_sb"], 1)
            pe.matmul(MSC[0:1, M_ST:M_ST + NT], T["tot"][:, 0:1], T["ltri"][:, :], start=True, stop=True)\
                .then_inc(S["start_ps"], 1)
            pe.wait_ge(S["stf_sb"], 1)
            pe.matmul(MSC[:, M_BC:M_BC + NT], ones[0:1, :], T["stf"][:, :], start=True, stop=True)
            pe.matmul(MSC[0:1, M_FL:M_FL + 1], T["vs"][:, 0:1], ones[:EP, 0:1], start=True, stop=False)
            pe.matmul(MSC[0:1, M_FL:M_FL + 1], T["tot"][:, 1:2], ones[:NT, 0:1], start=False, stop=True)\
                .then_inc(S["flag_ps"], 1)

            for bank in (KA, KS):
                pe.matmul(bank[:, :], fb_z[:, 0:128], fb_z[:, :], start=True, stop=False,
                          skip_group_check=True)
            pe.wait_ge(S["wrest_lo"], 5)

            def kv_transpose(t, k):
                pe.wait_ge(S["xc_ready"], t + 1)
                after(pe, "xT_lo", t - 1)
                for c in range(2):
                    ins = pe.transpose(TRP[k][:, c * P:c * P + P], T["xc"][:, k, 128 * c:128 * c + 128],
                                       ident[:P, :P])
                ins.then_inc(S["tr_ps"], 1)

            def kv_project(t, k):
                pe.wait_ge(S["xT_lo"], t + 1)
                after(pe, "kn_ready", 2 * (t - 1))
                out = KVP[k][:P, :]
                pe.matmul(out, onesr[:, :], bkvs[:, 0, :], start=True, stop=False)
                pe.matmul(out, onesr[:, :], bkvs[:, 1, :], start=False, stop=False)
                for c in range(2):
                    pe.matmul(out, xT[:, k, 0, c, :], wkv[:, 0, c, :], start=False, stop=False)
                    pe.matmul(out, xT[:, k, 0, c, :], wkv[:, 1, c, :], start=False, stop=False)
                    ins = pe.matmul(out, xT[:, k, 1, c, :], wkv[:, 0, c, :], start=False, stop=c == 1)
                ins.then_inc(S["kv_ps"], 1)

            def kv_sum(t, k, rows=P, last=False):
                pe.wait_ge(S["kn_ready"], 2 * t + 2)
                kn, vn = T["kn"], T["vn"]
                for h in range(2):
                    pe.matmul(KA[:, 129 * h:129 * h + 129], kn[:rows, k, 128 * h:128 * h + 128], vn[:rows, k, h, 0:129],
                              start=False, stop=last, skip_group_check=True)
                for h in range(2):
                    ins = pe.matmul(KS[:, 128 * h:128 * h + 128], ones[:rows, :], vn[:rows, k, h, 0:128],
                                    start=False, stop=last, skip_group_check=True)
                ins.then_inc(S["kv_sum"], 1)

            def kv_turn(t, k):
                const = isinstance(t, int)
                if not const or t < NT:
                    kv_transpose(t, k)
                if not const or 1 <= t <= NT:
                    kv_project(t - 1, 1 - k)
                if not const or t >= 2:
                    last = const and t - 2 == NT - 1
                    kv_sum(t - 2, k, LAST if last else P, last)

            kv_turn(0, 0)
            kv_turn(1, 1)
            with pe.Fori(1, NT // 2 - 1) as i:
                kv_turn(i * 2, 0)
                kv_turn(i * 2 + 1, 1)
            for t in range(NT - 2, NT + 2):
                kv_turn(t, t % 2)

            pe.wait_ge(S["flag_sb"], 1)
            needed = pe.value_load(flag[0:1, 0:1], min_val=0, max_val=1)
            with pe.If(needed > 0):
                with pe.Fori(0, NT) as t:
                    pe.wait_ge(S["fb_res"], t)
                    pe.matmul(CNT[:P, :], fb_z[:, 0:P], fb_z[:, :], start=True, stop=False, skip_group_check=True)
                    with pe.Fori(0, EC) as j:
                        q = t * EC + (j + 1)
                        pe.wait_ge(S["fb_gath"], q * 16)
                        pe.wait_ge(S["fb_oh"], q)
                        pe.matmul(CNT[:P, :], fb_o[:, :], fb_g[:, :], start=False, stop=False, skip_group_check=True)\
                            .then_inc(S["fb_mm"], 1)
                    pe.matmul(CNT[:P, :], fb_z[:, 0:P], fb_z[:, :], start=False, stop=True, skip_group_check=True)\
                        .then_inc(S["fb_sum"], 1)

            pe.wait_ge(S["kvs_sb"], 1)
            pe.wait_ge(S["col_in"], 16)
            for h in range(2):
                pe.matmul(TRP[h][:, 0:D], T["kvs"][:, h, :], wsm[:, h, O_WQ:O_WQ + D], start=True, stop=True)
                ins = pe.matmul(MSC[:, M_CM + h:M_CM + h + 1], T["kvs"][:, h, :], T["col"][:, h:h + 1],
                                start=True, stop=True)
            ins.then_inc(S["rT_ps"], 1)
            pe.wait_ge(S["rT_sb"], 3)
            for c in range(2):
                w = slice(128 * c, 128 * c + 128)
                for h in range(2):
                    pe.matmul(KVP[c][:, 0:D], T["rT"][:, h, w], wsm[:, h, O_W1:O_W1 + D], start=h == 0, stop=h == 1)
                for h in range(2):
                    ins = pe.matmul(MSC[:, M_CM + 2 + c:M_CM + 3 + c], wsm[:, h, O_W1 + 128 * c:O_W1 + 128 * c + 128],
                                    T["rb"][:, h:h + 1], start=h == 0, stop=h == 1)
            ins.then_inc(S["wm_ps"], 1)
            pe.wait_ge(S["wm_lo"], 3)
            pe.sem_inc(S["pro_over"], 1)
            pe.wait_ge(S["pro_over"], 3)
            pe.wait_ge(S["bo_in"], 16 * TG)
            pe.wait_ge(S["bn_ready"], 1)

            def three(out, hi, lo, whi_, wlo_):
                return [(whi_, hi), (whi_, lo), (wlo_, hi)]

            def layer1(g, e):
                m = g * EXP + e
                if e == 0:
                    pe.wait_ge(S["mt_lo"], mt_count(g, X_AT[3]) + 1)
                after(pe, "l1_act", m * 2)
                for c in range(2):
                    w = slice(128 * c, 128 * c + 128)
                    for k in range(2):
                        pe.matmul(H1P[c][:, 0:GN], whi[:, e, 0, k, w], x2T[:, 0, k, :], start=k == 0, stop=False)
                        pe.matmul(H1P[c][:, 0:GN], whi[:, e, 0, k, w], x2T[:, 1, k, :], start=False, stop=False)
                        ins = pe.matmul(H1P[c][:, 0:GN], wlo[:, e, 0, k, w], x2T[:, 0, k, :], start=False, stop=k == 1)
                    ins.then_inc(S["l1_ps"], 1)

            def layer2(g, e, after_mlp=False):
                m = g * EXP + e
                after(pe, "l2_act", m * 2)
                if after_mlp:
                    pe.wait_ge(S["g_act"], g * 2 + 4)
                pe.wait_ge(S["l1_hi"], m + 1)
                for c in range(2):
                    w = slice(128 * c, 128 * c + 128)
                    for k in range(2):
                        pe.matmul(H2P[c][:, 0:GN], whi[:, e, 1, k, w], h1[:, 0, k, :], start=k == 0, stop=False)
                        pe.matmul(H2P[c][:, 0:GN], wlo[:, e, 1, k, w], h1[:, 0, k, :], start=False, stop=False)
                pe.wait_ge(S["l1_lo"], m + 1)
                for c in range(2):
                    w = slice(128 * c, 128 * c + 128)
                    for k in range(2):
                        ins = pe.matmul(H2P[c][:, 0:GN], whi[:, e, 1, k, w], h1[:, 1, k, :], start=False, stop=k == 1)
                    ins.then_inc(S["l2_ps"], 1)

            def layer3(g, e):
                m = g * EXP + e
                pe.wait_ge(S["l2_hi"], m + 1)
                pe.wait_ge(S["l2_lo"], m + 1)
                for t in range(TG):
                    w = slice(t * P, t * P + P)
                    if e and t % 2 == 0:
                        pe.wait_ge(S["y_used"], m * TG + (t - 2))
                    for k in range(2):
                        pe.matmul(YP[t], h2[:, 0, k, w], whi[:, e, 2, k, :], start=k == 0, stop=False)
                        pe.matmul(YP[t], h2[:, 0, k, w], wlo[:, e, 2, k, :], start=False, stop=False)
                        ins = pe.matmul(YP[t], h2[:, 1, k, w], whi[:, e, 2, k, :], start=False, stop=k == 1)
                    ins.then_inc(S["y_ps"], 1)

            def mlp(q):
                pe.wait_ge(S["xg_in"], q * 16 + 16)
                after(pe, "l2_act", (q - 1) * (2 * EXP))
                for c in range(2):
                    w = slice(128 * c, 128 * c + 128)
                    for k in range(2):
                        pe.matmul(H2P[c][:, 0:GN], wms[:, 0, k, w], xg[:, :, 0, k, :], start=k == 0, stop=False)
                        pe.matmul(H2P[c][:, 0:GN], wms[:, 0, k, w], xg[:, :, 1, k, :], start=False, stop=False)
                        ins = pe.matmul(H2P[c][:, 0:GN], wms[:, 1, k, w], xg[:, :, 0, k, :], start=False, stop=k == 1)
                    ins.then_inc(S["g_ps"], 1)

            def agg(q, u):
                pe.wait_ge(S[f"gath{u % 2}"], q * (TG * US * 16) + (u // 2 + 1) * (US * 16))
                pe.wait_ge(S["oh_ready"], q * 8 + (u + 1))
                if u % 2 == 0:
                    after(pe, "agg_evac", q * TG + u // 2)
                for s in range(US):
                    ins = pe.matmul(AGG[:P, :], oh[:, u % 2, :, s], G[:, u % 2, s, :],
                                    start=u % 2 == 0 and s == 0, stop=u % 2 == 1 and s == US - 1)
                ins.then_inc(S["unit_done"], 1)

            def small_bank(mt, mp):
                after(pe, "mt_lo", mt)
                after(pe, "mp_free", mp)

            def transposes(src):
                for c in range(2):
                    ins = pe.transpose(MT[:, c * P:c * P + P], src[:, 128 * c:128 * c + 128], ident[:P, :P])
                ins.then_inc(S["mt_ps"], 1)

            def agg_transpose(q, t):
                pe.wait_ge(S["ag_ready"], q * TG + (t + 1))
                if t:
                    small_bank(mt_count(q, A_AT[t]), q * 8 + MP_BEFORE[A_AT[t]])
                else:
                    small_bank(a0_count(q), q * 8 - 4)
                    after(pe, "r_lg", q)
                transposes(ag2)

            def x2_transpose(q, t):
                pe.wait_ge(S["xn2_ready"], q * TG + (t + 1))
                small_bank(mt_count(q, X_AT[t]), q * 8 + 4)
                transposes(xn2[:, t, :])

            def project(q, t):
                if t == 0:
                    pe.wait_ge(S["g_lo"], q + 1)
                small_bank(mt_count(q, t), q * 8 + t)
                w = slice(t * P, t * P + P)
                for k in range(2):
                    for i, (lhs, wts) in enumerate(((gT[:, :, k, w], w2s), (aT[:, :, k, :], wgT))):
                        pe.matmul(MP, lhs[:, 0, :], wts[:, 0, k, :], start=k == 0 and i == 0, stop=False)
                        pe.matmul(MP, lhs[:, 0, :], wts[:, 1, k, :], start=False, stop=False)
                        ins = pe.matmul(MP, lhs[:, 1, :], wts[:, 0, k, :], start=False, stop=k == 1 and i == 1)
                ins.then_inc(S["mp_ps"], 1)

            def route(q):
                small_bank(mt_count(q, X_AT[3]) + 1, q * 8 + 4)
                for t in range(TG):
                    w = slice(t * P, t * P + P)
                    out = ML[:, EXP * t:EXP * t + EXP]
                    for k in range(2):
                        pe.matmul(out, x2T[:, 0, k, w], wrs[:, 0, k, :], start=k == 0, stop=False)
                        pe.matmul(out, x2T[:, 0, k, w], wrs[:, 1, k, :], start=False, stop=False)
                        ins = pe.matmul(out, x2T[:, 1, k, w], wrs[:, 0, k, :], start=False, stop=k == 1)
                ins.then_inc(S["r_ps"], 1)

            def w_transpose(g, last):
                pe.wait_ge(S["w_ready"], g + 1)
                small_bank(mt_count(g, W_AT - last), g * 8 + 4)
                pe.transpose(MT[0:TG * EXP, 0:P], wn[:, :, :].rearrange("p t e -> p (t e)"), ident[:P, :P])\
                    .then_inc(S["mt_ps"], 1)

            def bias(g, t, last):
                small_bank(mt_count(g, W_AT - last) + 1, g * 8 + (4 + t))
                pe.matmul(MP, wT[:, :], bo4[:, t, :], start=True, stop=True).then_inc(S["mp_ps"], 1)

            agg(0, 0)
            agg(0, 1)
            mlp(0)
            agg_transpose(0, 0)
            for t in range(TG):
                if t < TG - 1:
                    agg(0, 2 * t + 2)
                    agg(0, 2 * t + 3)
                project(0, t)
                if t < TG - 1:
                    agg_transpose(0, t + 1)
            for t in range(TG):
                x2_transpose(0, t)
            route(0)
            agg(1, 0)
            agg(1, 1)
            pe.wait_ge(S["w_lo"], EXP)

            layer1(0, 0)

            def group(g, prepare, ahead):
                q, last = g + 1, int(not prepare)
                if prepare:
                    agg_transpose(q, 0)
                    agg(q, 2)
                    mlp(q)
                w_transpose(g, last)
                layer1(g, 1)
                bias(g, 0, last)
                layer2(g, 0, prepare)
                bias(g, 1, last)
                for e in range(1, EXP - 1):
                    if prepare and e < 6:
                        agg(q, e + 2)
                    if ahead and e == 6:
                        agg(q + 1, 0)
                    if e == 1:
                        bias(g, 2, last)
                    layer1(g, e + 1)
                    if e == 1:
                        bias(g, 3, last)
                    if prepare and e == 6:
                        project(q, 3)
                    layer2(g, e)
                    if prepare and e in (1, 2, 4):
                        project(q, e // 2)
                    if prepare and e == 6:
                        x2_transpose(q, 0)
                    layer3(g, e - 1)
                    if prepare and e in (1, 3, 5):
                        agg_transpose(q, e // 2 + 1)
                    if prepare and e == 6:
                        x2_transpose(q, 1)
                if ahead:
                    agg(q + 1, 1)
                if prepare:
                    x2_transpose(q, 2)
                layer2(g, EXP - 1)
                if prepare:
                    x2_transpose(q, 3)
                layer3(g, EXP - 2)
                if prepare:
                    layer1(q, 0)
                    route(q)
                layer3(g, EXP - 1)

            with pe.Fori(0, NG - 2) as g:
                group(g, True, True)
            group(NG - 2, True, False)
            group(NG - 1, False, False)


def kernel(**inputs):
    import concourse.bacc as _bacc
    from concourse.bass_utils import run_bass_kernel_spmd as _run

    a = {k: np.asarray(v) for k, v in inputs.items()}
    x = np.zeros((NP, D), np.float32)
    x[:N] = a["x"]
    edges = np.ascontiguousarray(np.stack([a["src"], a["dst"]], axis=-1))
    w = np.stack([a["L0_ffn_W1"], a["L0_ffn_W2"], a["L0_ffn_Wo"]], axis=1).reshape(EXP, 3, 2, 128, D)
    wffn = np.ascontiguousarray(w.transpose(3, 0, 1, 2, 4))
    bn = np.stack([np.stack([a[f"L0_ffn_{n}{l}"] for n in ("b", "g", "be", "m", "v")]) for l in (1, 2)])
    bn = np.ascontiguousarray(bn.reshape(2, 5, EXP, 2, 128).transpose(4, 0, 1, 2, 3))
    wq, wk, wv = a["L0_mix_w_qkv"].reshape(D, D // HC, 3, HC).transpose(2, 0, 1, 3).reshape(3, D, D)
    bq, bk, bv = a["L0_mix_b_qkv"].reshape(D // HC, 3, HC).transpose(1, 0, 2).reshape(3, D)
    wsm = np.concatenate([a["L0_gnn_W"].T, wk, wv, a["L0_mix_w1"], a["L0_mix_w2"], a["L0_ffn_Wr"], wq.T], axis=1)
    wsm = np.ascontiguousarray(wsm.reshape(2, 128, SW).transpose(1, 0, 2))
    col = np.ascontiguousarray(np.stack([bq[:128], bq[128:], a["L0_mix_b1"][:128], a["L0_mix_b1"][128:],
                                         np.tile(a["L0_mix_kln_g"], 4), np.tile(a["L0_mix_kln_b"], 4)], axis=1))
    row = np.concatenate([np.tile(a["L0_mix_vln_g"], 4), np.tile(a["L0_mix_vln_b"], 4), a["L0_gnn_b"],
                          a["L0_mix_b2"], a["L0_ffn_br"], a["L0_gnn_alpha"], bk, bv])[None]

    nc = _bacc.Bacc("TRN2", target_bir_lowering=False, num_devices=1)
    arrays = dict(x=x, edges=edges, wffn=wffn, bn=bn, wsm=wsm, col=col, row=row, bo=a["L0_ffn_bo"])
    args = [nc.dram_tensor(n + "_in", v.shape, mybir.dt.from_np(v.dtype), kind="ExternalInput").ap()
            for n, v in arrays.items()]
    out = nc.dram_tensor("out", (NP, D), mybir.dt.float32, kind="ExternalOutput").ap()
    build(nc, *args, out)
    r = _run(nc, [{n + "_in": v for n, v in arrays.items()}], core_ids=[0])
    return r.results[0]["out"][:N]
```

```python
import numpy as np
import concourse.bass as bass
from concourse import mybir
from contextlib import ExitStack

N, D, E = 3125, 256, 53125
P = 112
NT = 28
NP = P * NT
TG = 4
NG = NT // TG
GN = TG * P
LAST = N - (NT - 1) * P
EXP = 8
HC = 32
NH2 = 2 * D // HC
EP, EC = 125, 425
CH = 25
NCH = EC // CH
CA, CB = NP // 64, 64
WIN = 2048
KV_PEEL, KV_BODY, KV_LOOP = 4, 8, 2
KV_REST = KV_PEEL + KV_BODY * KV_LOOP
UNIT_TURNS = (2, 6)
XT = 4
TB_SLOTS = 7
CONSTS = 16
WS = WIN // 128
US = 8
SCALE = 2048.0
LN_EPS, BN_EPS = 1e-5, 1e-3
O_WT, O_KV, O_W1, O_W2, O_WR, O_WQ = 0, 256, 768, 1024, 1280, 1288
SW = 1544
R_VG, R_VB, R_BG, R_B2, R_BR, R_A, R_BKV = 0, 128, 256, 512, 768, 776, 777
RW = R_BKV + 512
M_ST, M_BC, M_FL, M_CM = 0, 64, 100, 128


def build(nc, x_d, edges_d, wffn_d, bn_d, wsm_d, col_d, row_d, bo_d, out_d):
    f32, f32r, f16, i32 = mybir.dt.float32, mybir.dt.float32r, mybir.dt.float16, mybir.dt.int32
    ACT = mybir.ActivationFunctionType
    ALU = mybir.AluOpType
    AX = mybir.AxisListType.X
    ds = bass.ds

    table_d = nc.dram_tensor("table_d", [NP, 2 * D], f16).ap()
    base_d = nc.dram_tensor("base_d", [NP, D], f32).ap()
    self_d = nc.dram_tensor("self_d", [NP, D], f32).ap()
    xnT_d = nc.dram_tensor("xnT_d", [NT, 128, 4 * P], f32).ap()
    cnt_d = nc.dram_tensor("cnt_d", [NP], f32).ap()

    ctx = ExitStack()
    with ctx:
        def sb(name, shape, dt, where=ctx):
            return where.enter_context(nc.sbuf_tensor(name, shape, dt))

        def sem(name):
            return ctx.enter_context(nc.semaphore(name))

        G = sb("G", [128, 2, US, 2 * D], f16)
        idx = sb("idx", [128, 2, WS], i32)
        win = sb("win", [128, NT, WS, 2], i32)
        oh = sb("oh", [128, 2, P, US], f16)
        dl = sb("dl", [128, WS], f16)
        iota_rep = sb("iota_rep", [128, P, US], f16)
        ident = sb("ident", [128, 128], f32)
        tbase = sb("tbase", [128, NT], f32)
        wgT = sb("wgT", [128, 2, 2, D], f32r)
        w2s = sb("w2s", [128, 2, 2, D], f32r)
        wms = sb("wms", [128, 2, 2, D], f32r)
        wrs = sb("wrs", [128, 2, 2, EXP], f32r)
        bnsc = sb("bnsc", [128, 2, EXP, 2], f32)
        bnbi = sb("bnbi", [128, 2, EXP, 2], f32)
        cm = sb("cm", [128, 2], f32)
        bo4 = sb("bo4", [32, TG, D], f32)
        rd = sb("rd", [P, NT], f32)
        ro = sb("ro", [P, NT], f32)
        br_b = sb("br_b", [P, EXP], f32)
        epsc = sb("epsc", [128, 1], f32)
        flag = sb("flag", [1, 1], i32)
        starts = sb("starts", [1, NT], i32)
        stbc = sb("stbc", [128, NT], f32)
        iotaP = sb("iotaP", [128, P], f32)
        alo = sb("alo", [P, D], f32)
        ags = sb("ags", [P, TG, D], f32)

        pro = ExitStack()
        x_all = sb("x_all", [P, NT, D], f32, pro)
        edg = sb("edg", [EP, EC, 2], i32, pro)
        with ExitStack() as counting:
            oneA = sb("oneA", [EP, 2, CA, CH], f16, counting)
            oneB = sb("oneB", [EP, 2, CB, CH], f16, counting)
        xT = sb("xT", [128, XT, 2, 2, P], f32r, pro)
        sb("xT_rest", [128, 2 * (CA + CB) * CH - 2 * XT * 4 * P + 8], f16, pro)
        xn = sb("xn", [P, NT, D], f32, pro)
        iotaA = sb("iotaA", [EP, CA, CH], f16, pro)
        iotaB = sb("iotaB", [EP, CB, CH], f16, pro)
        ab_i = sb("ab_i", [EP, 2, EC], i32, pro)
        ab_f = sb("ab_f", [EP, 2, EC], f16, pro)
        posn = sb("posn", [EP, EC], f32, pro)
        viol = sb("viol", [EP, EC], f32, pro)
        wsm = sb("wsm", [128, 2, SW], f32, pro)
        pro_small = dict(
            col=[128, 6], rowv=[128, RW], bn=[128, 2, 5, EXP, 2], bntmp=[128, 2, EXP, 2],
            nxt=[EP, 2], vs=[EP, 2], cnt_ab=[CA, CB], cnt_t=[NT, P], tot=[NT, 2], ltri=[NT, NT],
            ones=[128, 128], stf=[1, NT], deg=[P, NT], dinv=[P, NT], dS=[P, NT],
            bst=[P, 7, 6], mv=[P, NT, 2], rstd=[P, NT], nmr=[P, NT], a1=[P, 2], brow=[P, D],
            gm=[128, 2, NH2], gb=[33, NH2], bkv=[33, 512], one33=[33, P],
            vsum=[P, D], sq=[P, 512], s2=[P, 2, NH2], kvn=[P, 2, 514], xc=[P, 2, D], bsc=[P, NT], bbi=[P, NT],
            kvs=[128, 2, 128], kvt=[128, 2, 2, 128], rT=[128, 2, D], rb=[128, 2],
        )
        T = {}
        for k, s in pro_small.items():
            T[k] = sb("p_" + k, s, i32 if k == "nxt" else f32, pro)
        wkv = sb("wkv", [128, 2, 2, 512], f32r, pro)
        bkvs = sb("bkvs", [33, 512], f32r, pro)
        onesr = sb("onesr", [33, P], f32r, pro)
        tb16 = sb("tb16", [P, TB_SLOTS, 2, 2, D], f16, pro)
        fb_e = sb("fb_e", [EP, 2], i32, pro)
        fb_g = sb("fb_g", [EP, 2 * D], f16, pro)
        fb_o = sb("fb_o", [EP, P], f16, pro)
        fb_d = sb("fb_d", [EP, 1], f32, pro)
        fb_w = sb("fb_w", [EP, 3, NT], f32, pro)
        fb_z = sb("fb_z", [EP, 512], f16, pro)
        wst = sb("wst", [128, 3, 2, D], f32, pro)
        pro.close()

        xg = sb("xg", [128, TG, 2, 2, P], f32r)
        bs = sb("bs", [P, 2, 2, D], f32)
        t2 = sb("t2", [128, 2, GN], f32)
        x2T = sb("x2T", [128, 2, 2, GN], f32r)
        gT = sb("gT", [128, 2, 2, GN], f32r)
        x1 = sb("x1", [P, TG, D], f32)
        xb = ags
        acc = sb("acc", [P, TG, D], f32)
        ag1 = sb("ag1", [P, D], f32)
        ag2 = sb("ag2", [P, D], f32)
        aT = sb("aT", [128, 2, 2, P], f32r)
        bst2 = sb("bst2", [P, 6], f32)
        mv2 = sb("mv2", [P, TG, 2], f32)
        sd2 = sb("sd2", [P, TG], f32)
        rs2 = sb("rs2", [P, TG], f32)
        nm2 = sb("nm2", [P, TG], f32)
        xn2 = sb("xn2", [P, TG, D], f32)
        lg = sb("lg", [P, TG, EXP], f32)
        lg2 = sb("lg2", [P, TG, EXP], f32)
        mx = sb("mx", [P, TG], f32)
        sm = sb("sm", [P, TG], f32)
        wn = sb("wn", [P, TG, EXP], f32)
        wT = sb("wT", [TG * EXP, P], f32)
        whi = sb("whi", [128, EXP, 3, 2, D], f32r)
        with ExitStack() as raw:
            wraw = sb("wraw", [128, EXP, 3, 2, D], f32, raw)
        wlo = sb("wlo", [128, EXP, 3, 2, D], f32r)
        t1 = sb("t1", [128, 2, GN], f32)
        h1 = sb("h1", [128, 2, 2, GN], f32r)
        h2 = sb("h2", [128, 2, 2, GN], f32r)

        B = [ctx.enter_context(nc.psum_tensor(f"bank{i}", [128, 512], f32)) for i in range(8)]
        TRP = [B[0], B[1]]
        KVP = [B[2], B[3]]
        KA, KS, CNT, MSC = B[4], B[5], B[6], B[7]
        H1P, H2P = [B[0], B[1]], [B[2], B[3]]
        YP = [B[4][:P, 0:D], B[4][:P, D:2 * D], B[5][:P, 0:D], B[5][:P, D:2 * D]]
        AGG = B[6]
        MP = B[7][:P, 0:D]
        MT = B[7][:, D:D + 2 * P]
        ML = B[7][:P, D + 2 * P:D + 2 * P + TG * EXP]

        S = {n: sem(n) for n in (
            "edges_in nxt_in x_in0 x_in1 x_in2 x_in3 wsm_in col_in row_in bn_in bo_in w_in0 w_in1 w_in2 w_in3 w_in4 w_in5 w_in6 w_in7 "
            "settled consts pool_link dve_link dve_loop_link "
            "base_mul bsc_ready ln_var ln_std ln_ready xn_ready one_ready one_free cnt_ps cnt_sb cnt_out cnt_in tot_sb cntT_ps "
            "start_ps starts_sb stf_sb flag_ps flag_sb deg_sb deg_sqrt dinv_sb base_out "
            "xs_hi tb_ready tb_out0 tb_out1 tb_out2 tb_out3 tb_out4 tb_out5 tb_out6 own_out win_in idx_ready "
            "wkv_ready wrest_hi wrest_lo w_hi w_lo bn_v bn_sd bn_ready rT_ps rT_sb wm_ps wm_hi wm_lo pro_over "
            "xc_ready tr_ps xT_hi xT_lo xT_out0 xT_out1 xT_out2 xT_out3 kv_ps sq_ready s2_ready sd_ready kn_ready v_added kv_sum kvs_sb "
            "fb_zero fb_link fb_wt fb_idx fb_gath fb_oh fb_mm fb_sum fb_res fb_scaled fb_add fb_over "
            "gath0 gath1 dl_ready unit_done oh_ready agg_evac alo_ready ag_ready "
            "mt_ps mt_hi mt_lo mp_ps mp_free st_ready var_ready std_ready rs_ready nmr_ready xn2_ready "
            "g_ps g_act g_hi g_lo r_ps r_lg r_max r_sub r_exp r_sum w_ready xg_in bs_in0 bs_in1 "
            "l1_ps l1_act l1_hi l1_lo l2_ps l2_act l2_hi l2_lo y_ps y_used out_sent"
        ).split()}

        block = ctx.enter_context(nc.Block())

        FROM_ONE = ("l1_act", "l1_lo", "l2_act", "l2_lo", "y_ps", "out_sent")

        def after(eng, name, value):
            if not isinstance(value, int) or value > 0:
                eng.wait_ge(S[name], value + 1 if name in FROM_ONE else value)

        def settle(eng):
            eng.sem_inc(S["settled"], 1)

        def bc_out(ap, n):
            return ap.rearrange("p (o m) -> p o m", o=1).to_broadcast([ap.shape[0], n, ap.shape[1]])

        def bc_in(ap, m):
            return ap.rearrange("p (n o) -> p n o", o=1).to_broadcast([ap.shape[0], ap.shape[1], m])

        A_AT, X_AT, W_AT = (None, 0, 1, 2), (3, 4, 5, 6), 8
        NORM_AT = {2: 0, 3: 1, 5: 2}
        MP_BEFORE = (1, 2, 3, 4, 4, 4, 4, 4, 4)

        def alone(q):
            return isinstance(q, int) and q == 0

        def mt_of(q, t):
            return B[t % 2][:, 0:2 * P] if alone(q) else MT

        def mp_of(q, t):
            return B[5][:P, 0:D] if alone(q) and t % 2 else MP

        def mt_count(q, at):
            return q * 9 + (1 + at)

        def a0_count(q):
            return 0 if alone(q) else q * 9 - 1

        @block.sync
        def _(sp):
            e3 = edges_d.rearrange("(p j) two -> p j two", p=EP)
            xv = x_d.rearrange("(t p) d -> p t d", p=P)
            for i in range(4):
                sp.dma_start(x_all[:, 7 * i:7 * i + 7, :], xv[:, 7 * i:7 * i + 7, :]).then_inc(S[f"x_in{i}"], 16)
                if i == 1:
                    sp.dma_start(edg[:, :, :], e3).then_inc(S["edges_in"], 16)
                    sp.dma_start(T["nxt"][0:EP - 1, :], e3[1:EP, 0, :]).then_inc(S["nxt_in"], 16)
            sp.dma_start(T["rowv"][:, :], row_d.to_broadcast([128, RW])).then_inc(S["row_in"], 16)
            sp.dma_start(T["bn"][:, :, :, :, :], bn_d).then_inc(S["bn_in"], 16)
            sp.dma_start(T["col"][:, :], col_d).then_inc(S["col_in"], 16)
            sp.dma_start(wsm[:, :, :], wsm_d).then_inc(S["wsm_in"], 16)
            sp.wait_ge(S["consts"], 1)
            for t in range(TG):
                sp.dma_start(bo4[EXP * t:EXP * t + EXP, t, :], bo_d).then_inc(S["bo_in"], 16)
            sp.dma_start(wst[:, :, :, :], wffn_d[:, 0, :, :, :]).then_inc(S["w_in0"], 16)
            for i in range(4):
                sp.wait_ge(S["xn_ready"], 7 * i + 7)
                sp.dma_start(self_d.rearrange("(t p) d -> p t d", p=P)[:, 7 * i:7 * i + 7, :],
                             xn[:, 7 * i:7 * i + 7, :]).then_inc(S["own_out"], 16)
            sp.wait_ge(S["cnt_sb"], 1)
            sp.dma_start(cnt_d.rearrange("(a b) -> a b", b=CB), T["cnt_ab"][:, :]).then_inc(S["cnt_out"], 16)
            sp.wait_ge(S["cnt_out"], 16)
            sp.dma_start(T["cnt_t"][:, :], cnt_d.rearrange("(t p) -> t p", p=P)).then_inc(S["cnt_in"], 16)
            ef = edges_d.rearrange("e two -> (e two)")
            sp.wait_ge(S["starts_sb"], 1)
            with sp.Fori(0, NT) as t:
                v = sp.value_load(starts[0:1, ds(t, 1)], min_val=0, max_val=E - WIN)
                sp.dma_start(win[:, ds(t, 1), :, :].rearrange("p o s two -> p o (s two)"),
                             ef[ds(v * 2, 2 * WIN)].rearrange("(p o k) -> p o k", p=128, o=1))\
                    .then_inc(S["win_in"], 16)
                sp.wait_ge(S["win_in"], (t + 1) * 16)
                settle(sp)

            def load_base(t, k):
                settle(sp)
                sp.dma_start(bs[:, k, 0, :], base_d[ds(t * P, P), :]).then_inc(S[f"bs_in{k}"], 16)
                sp.dma_start(bs[:, k, 1, :], self_d[ds(t * P, P), :]).then_inc(S[f"bs_in{k}"], 16)

            def load_xg(q):
                settle(sp)
                sp.dma_start(xg[:, :, :, :, :].rearrange("p t h c n -> p t (h c n)").bitcast(f32),
                             xnT_d[ds(q * TG, TG), :, :].rearrange("t p n -> p t n")).then_inc(S["xg_in"], 16)

            sp.sem_inc(S["out_sent"], 1)
            sp.wait_ge(S["base_out"], 64)
            sp.wait_ge(S["own_out"], 64)
            sp.wait_ge(S["fb_over"], 1)
            for k in range(XT):
                sp.wait_ge(S[f"xT_out{k}"], 16 * (NT // XT))
            load_xg(0)
            for t in range(2):
                load_base(t, t % 2)

            def group_loads(q, tiles):
                for t in range(tiles):
                    sp.wait_ge(S["mp_free"], q * 8 + (t + 1))
                    load_base(q * TG + (t + 2), t % 2)

            sp.wait_ge(S["g_ps"], 2)
            load_xg(1)
            group_loads(0, TG)
            ov = out_d.rearrange("(g t p) d -> g p t d", t=TG, p=P)

            def store(g):
                sp.wait_ge(S["y_used"], (g + 1) * (EXP * TG))
                settle(sp)
                sp.dma_start(ov[ds(g, 1)].rearrange("g p t d -> p (g t) d"), acc[:, :, :]).then_inc(S["out_sent"], 16)

            with sp.Fori(0, NG - 2) as g:
                sp.wait_ge(S["g_ps"], g * 2 + 4)
                load_xg(g + 2)
                group_loads(g + 1, TG)
                store(g)
            group_loads(NG - 1, 2)
            store(NG - 2)
            store(NG - 1)
            after(sp, "out_sent", NG * 16)

        @block.gpsimd
        def _(pool):
            n = [0]

            def link(ins):
                n[0] += 1
                ins.then_inc(S["pool_link"], 1)
                pool.wait_ge(S["pool_link"], n[0])

            pool.memset(bo4[:, :, :], 0.0).then_inc(S["consts"], 1)
            pool.memset(epsc[:, :], LN_EPS).then_inc(S["consts"], 1)
            for dst, m in ((iotaA, CA), (iotaB, CB), (iota_rep, P)):
                pool.iota(dst[:, :, :], [[1, m], [0, dst.shape[2]]], base=0, channel_multiplier=0,
                          allow_small_or_imprecise_dtypes=True).then_inc(S["consts"], 1)
            pool.iota(tbase[:, :], [[P, NT]], base=0, channel_multiplier=0,
                      allow_small_or_imprecise_dtypes=True).then_inc(S["consts"], 1)
            pool.iota(iotaP[:, :], [[1, P]], base=0, channel_multiplier=0,
                      allow_small_or_imprecise_dtypes=True).then_inc(S["consts"], 1)
            link(pool.memset(ident[:, :], 0.0))
            pool.affine_select(out=ident[:, :], in_=ident[:, :], compare_op=ALU.not_equal, fill=1.0, base=0,
                               pattern=[[-1, 128]], channel_multiplier=1).then_inc(S["consts"], 1)
            link(pool.memset(T["ltri"][:, :], 1.0))
            pool.affine_select(out=T["ltri"][:, :], in_=T["ltri"][:, :], compare_op=ALU.is_gt, fill=0.0, base=0,
                               pattern=[[1, NT]], channel_multiplier=-1).then_inc(S["consts"], 1)
            pool.memset(T["ones"][:, :], 1.0).then_inc(S["consts"], 1)
            pool.memset(T["vsum"][:, :], 0.0).then_inc(S["consts"], 1)
            pool.memset(T["kvn"][:, :, :], 1.0).then_inc(S["consts"], 1)
            link(pool.memset(T["one33"][:, :], 0.0))
            for row in (0, 32):
                link(pool.memset(T["one33"][row:row + 1, :], 1.0))
            pool.memset(fb_z[:, :], 0.0).then_inc(S["consts"], 1)
            pool.memset(T["kvs"][:, :, :], 0.0).then_inc(S["consts"], 1)
            pool.iota(posn[:, :], [[1, EC]], base=0, channel_multiplier=EC,
                      allow_small_or_imprecise_dtypes=True).then_inc(S["consts"], 1)
            pool.wait_ge(S["row_in"], 16)
            link(pool.tensor_scalar(T["a1"][:, 0:1], T["rowv"][:P, R_A:R_A + 1], 1.0, None, ALU.add))
            link(pool.tensor_scalar(T["a1"][:, 1:2], T["rowv"][:P, R_A:R_A + 1], -1.0, 1.0, ALU.mult, ALU.add))
            link(pool.tensor_scalar(T["brow"][:, :], T["rowv"][:P, R_BG:R_BG + D], T["a1"][:, 1:2], None, ALU.mult))
            link(pool.tensor_tensor(T["brow"][:, :], T["brow"][:, :], T["rowv"][:P, R_B2:R_B2 + D], ALU.add))
            pool.tensor_copy(br_b[:, :], T["rowv"][:P, R_BR:R_BR + EXP]).then_inc(S["consts"], 1)
            bv = base_d.rearrange("(t p) d -> p t d", p=P)
            for i in range(4):
                pool.wait_ge(S["base_mul"], 7 * i + 7)
                q = x_all[:, 7 * i:7 * i + 7, :]
                link(pool.tensor_tensor(q, q, bc_out(T["brow"][:, :], 7), ALU.add))
                pool.dma_start(bv[:, 7 * i:7 * i + 7, :], q).then_inc(S["base_out"], 16)

            def gather_unit(u, k):
                settle(pool)
                for s in range(US):
                    pool.indirect_dma_start(
                        G[:, u, s, :], None, table_d,
                        bass.IndirectOffsetOnAxis(ap=idx[:, k, u * US + s:u * US + s + 1], axis=0),
                    ).then_inc(S[f"gath{u}"], 16)

            def tile_index(t, k):
                pool.wait_ge(S["win_in"], (t + 1) * 16)
                pool.tensor_copy(idx[:, k:k + 1, :], win[:, ds(t, 1), :, 0]).then_inc(S["idx_ready"], 1)

            def tile_gathers(t, k, more=True):
                pool.wait_ge(S["idx_ready"], t + 1)
                after(pool, "unit_done", t * 2 - 1)
                gather_unit(0, k)
                after(pool, "unit_done", t * 2)
                if more:
                    tile_index(t + 1, 1 - k)
                gather_unit(1, k)

            with pool.Fori(0, NT // 2 // TB_SLOTS) as i:
                for slot in range(TB_SLOTS):
                    n_pair = i * TB_SLOTS + slot
                    pool.wait_ge(S["tb_ready"], n_pair + 1)
                    settle(pool)
                    pool.dma_start(table_d[ds(n_pair * (2 * P), 2 * P), :].rearrange("(m p) d -> p m d", p=P),
                                   tb16[:, slot, :, :, :].rearrange("p m h d -> p m (h d)"))\
                        .then_inc(S[f"tb_out{slot}"], 16)
            tile_index(0, 0)
            for slot in range(TB_SLOTS):
                after(pool, f"tb_out{slot}", 16 * (NT // 2 // TB_SLOTS))
            for t in range(TG):
                tile_gathers(t, t % 2)

            pool.wait_ge(S["own_out"], 16 * 4)
            pool.wait_ge(S["base_out"], 64)
            pool.wait_ge(S["flag_sb"], 1)
            needed = pool.value_load(flag[0:1, 0:1], min_val=0, max_val=1)
            with pool.If(needed > 0):
                with pool.Fori(0, EC) as j:
                    pool.wait_ge(S["fb_mm"], j * NT + 1)
                    pool.tensor_copy(fb_e[:, :], edg[:, ds(j, 1), :].rearrange("p o two -> p (o two)"))\
                        .then_inc(S["fb_idx"], 1)
                    pool.wait_ge(S["fb_idx"], j + 1)
                    settle(pool)
                    pool.indirect_dma_start(fb_g[:, :], None, table_d,
                                            bass.IndirectOffsetOnAxis(ap=fb_e[:, 0:1], axis=0))\
                        .then_inc(S["fb_gath"], 16)
                pool.wait_ge(S["fb_scaled"], NT)
                pool.dma_start(self_d.rearrange("(t p) d -> p t d", p=P), x_all[:, :, :], accum_op=ALU.add)\
                    .then_inc(S["fb_add"], 16)
                pool.wait_ge(S["fb_add"], 16)
            pool.sem_inc(S["fb_over"], 1)

            with pool.Fori(TG // 2, NT // 2 - 1) as i:
                tile_gathers(i * 2, 0)
                tile_gathers(i * 2 + 1, 1)
            tile_gathers(NT - 2, 0)
            tile_gathers(NT - 1, 1, False)

        @block.scalar
        def _(act):
            act.wait_ge(S["consts"], 2)
            for i in range(4):
                act.wait_ge(S["ln_var"], 7 * i + 7)
                act.activation(T["rstd"][:, 7 * i:7 * i + 7], T["mv"][:, 7 * i:7 * i + 7, 1], ACT.Sqrt,
                               bias=epsc[:P, :]).then_inc(S["ln_std"], 1)
                act.wait_ge(S["ln_ready"], i + 1)
                with act.Fori(7 * i, 7 * i + 7) as t:
                    act.activation(xn[:, ds(t, 1), :], x_all[:, ds(t, 1), :], ACT.Identity,
                                   bias=T["nmr"][:, ds(t, 1)], scale=T["rstd"][:, ds(t, 1)])\
                        .then_inc(S["xn_ready"], 1)
            act.wait_ge(S["xn_ready"], NT)
            act.wait_ge(S["bsc_ready"], 2)
            with act.Fori(0, NT) as t:
                act.activation(x_all[:, ds(t, 1), :], x_all[:, ds(t, 1), :], ACT.Identity,
                               bias=T["bbi"][:, ds(t, 1)], scale=T["bsc"][:, ds(t, 1)]).then_inc(S["base_mul"], 1)
            act.wait_ge(S["bn_v"], 1)
            act.activation(T["bntmp"][:, :, :, :], T["bntmp"][:, :, :, :], ACT.Sqrt).then_inc(S["bn_sd"], 1)
            act.wait_ge(S["cnt_ps"], 1)
            act.activation(T["cnt_ab"][:, :], CNT[:CA, 0:CB], ACT.Copy).then_inc(S["cnt_sb"], 1)
            act.wait_ge(S["wkv_ready"], 2)
            act.activation(wkv[:, 0, :, :], wsm[:, :, O_KV:O_KV + 512], ACT.Copy).then_inc(S["wrest_hi"], 1)
            act.activation(T["sq"][0:33, :].bitcast(f32r), T["bkv"][:, :], ACT.Copy).then_inc(S["wrest_hi"], 1)
            act.activation(bkvs[0:32, :], T["bkv"][0:32, :], ACT.Copy).then_inc(S["wrest_hi"], 1)
            act.activation(onesr[:, :], T["one33"][:, :], ACT.Copy).then_inc(S["wrest_hi"], 1)
            act.wait_ge(S["deg_sb"], 1)
            act.activation(T["deg"][:, :], T["deg"][:, :], ACT.Sqrt).then_inc(S["deg_sqrt"], 1)
            def table_high(n, slot, used):
                after(act, f"tb_out{slot}", used * 16)
                for m in range(2):
                    t = n * 2 + m
                    ins = act.activation(tb16[:, slot, m:m + 1, 0, :], xn[:, ds(t, 1), :], ACT.Copy,
                                         scale=T["dS"][:, ds(t, 1)])
                ins.then_inc(S["xs_hi"], 1)

            act.wait_ge(S["dinv_sb"], 1)
            for pair in range(NT // 2):
                table_high(pair, pair % TB_SLOTS, pair // TB_SLOTS)

            def kv_copy(t, k):
                after(act, "tr_ps", t - 1)
                act.activation(T["xc"][:, k % 2:k % 2 + 1, :], xn[:, ds(t, 1), :], ACT.Copy).then_inc(S["xc_ready"], 1)

            def kv_high(t, k, i):
                act.wait_ge(S["tr_ps"], t + 1)
                after(act, "kv_ps", t - (XT - 1))
                after(act, f"xT_out{k}", i * 16)
                act.activation(xT[:, k, 0, :, :], TRP[k % 2][:, 0:2 * P].rearrange("p (c n) -> p c n", c=2), ACT.Copy)\
                    .then_inc(S["xT_hi"], 1)

            def kv_square(t, k):
                act.wait_ge(S["kv_ps"], t + 1)
                after(act, "s2_ready", t)
                act.activation(T["sq"][:, :], KVP[k % 2][:P, :], ACT.Square).then_inc(S["sq_ready"], 1)
                act.wait_ge(S["xT_lo"], t + 1)
                act.dma_start(xnT_d[ds(t, 1), :, :].rearrange("o p n -> p o n"),
                              xT[:, k, :, :, :].rearrange("p (o h) c n -> p o (h c n)", o=1).bitcast(f32))\
                    .then_inc(S[f"xT_out{k}"], 16)

            def kv_deviation(t):
                act.wait_ge(S["s2_ready"], t + 1)
                after(act, "kn_ready", t)
                act.activation(T["s2"][:, 1, :], T["s2"][:, 0, :], ACT.Sqrt, bias=epsc[:P, :], scale=1.0 / HC)\
                    .then_inc(S["sd_ready"], 1)

            def kv_turn(t, k, i):
                const = isinstance(t, int)
                if not const or 2 <= t < NT + 2:
                    kv_deviation(t - 2)
                if not const or t + 1 < NT:
                    kv_copy(t + 1, (k + 1) % XT)
                if not const or t < NT:
                    kv_high(t, k, i)
                if not const or 1 <= t < NT + 1:
                    kv_square(t - 1, (k - 1) % XT)

            def agg_low(t):
                act.wait_ge(S["unit_done"], t * 2 + 2)
                act.wait_ge(S["agg_evac"], t + 1)
                act.activation(alo[:, :], AGG[:P, D:2 * D], ACT.Copy, scale=rd[:, ds(t, 1)])\
                    .then_inc(S["alo_ready"], 1)

            kv_copy(0, 0)
            for t in range(KV_PEEL):
                kv_turn(t, t % XT, t // XT)
            with act.Fori(0, KV_LOOP) as j:
                for m in range(KV_BODY):
                    kv_turn(j * KV_BODY + (KV_PEEL + m), (KV_PEEL + m) % XT, j * (KV_BODY // XT) + (KV_PEEL + m) // XT)
                agg_low(j)
            for t in range(KV_REST, NT + 2):
                kv_turn(t, t % XT, t // XT)
                if t == KV_REST + KV_BODY - 1:
                    agg_low(KV_LOOP)
            for w, o, m in ((wgT, O_WT, D), (w2s, O_W2, D), (wrs, O_WR, EXP)):
                act.activation(w[:, 0, :, :], wsm[:, :, o:o + m], ACT.Copy).then_inc(S["wrest_hi"], 1)
            agg_low(KV_LOOP + 1)
            act.wait_ge(S["wm_ps"], 1)
            for c in range(2):
                act.activation(wms[:, 0, c, :], KVP[c][:, 0:D], ACT.Copy).then_inc(S["wm_hi"], 1)
            act.sem_inc(S["pro_over"], 1)
            act.wait_ge(S["pro_over"], 3)
            act.wait_ge(S["fb_over"], 1)
            for k in range(XT):
                act.wait_ge(S[f"xT_out{k}"], 16 * (NT // XT))

            def weights_high(e):
                act.wait_ge(S[f"w_in{e}"], 16)
                act.activation(whi[:, e, :, :, :], wst[:, :, :, :] if e == 0 else wraw[:, e, :, :, :],
                               ACT.Copy).then_inc(S["w_hi"], 1)

            act.sem_inc(S["l1_act"], 1)
            act.sem_inc(S["l2_act"], 1)

            def expert_relu(l, g, e, after_mlp=False):
                name, buf, banks = (("l1", t1, H1P), ("l2", t2, H2P))[l]
                m = g * EXP + e
                after(act, name + "_lo", m)
                if after_mlp:
                    act.wait_ge(S["g_lo"], g + 2)
                for c in range(2):
                    act.wait_ge(S[name + "_ps"], m * 2 + (c + 1))
                    act.activation(buf[:, c, :], banks[c][:, 0:GN], ACT.Relu, bias=bnbi[:, l, e, c:c + 1],
                                   scale=bnsc[:, l, e, c:c + 1]).then_inc(S[name + "_act"], 1)

            def expert_high(l, g, e):
                name, buf, hi = (("l1", t1, h1), ("l2", t2, h2))[l]
                m = g * EXP + e
                after(act, name + "_act", m * 2 + 2)
                if l:
                    after(act, "y_ps", m * TG)
                act.activation(hi[:, 0, :, :], buf[:, :, :], ACT.Copy).then_inc(S[name + "_hi"], 1)

            def mlp(q):
                after(act, "l2_lo", (q - 1) * EXP)
                for c in range(2):
                    act.wait_ge(S["g_ps"], q * 2 + (c + 1))
                    act.activation(t2[:, c, :], H2P[c][:, 0:GN], ACT.Gelu, bias=cm[:, c:c + 1]).then_inc(S["g_act"], 1)
                act.wait_ge(S["g_act"], q * 2 + 2)
                after(act, "mp_ps", q * 8 - 4)
                act.activation(gT[:, 0, :, :], t2[:, :, :], ACT.Copy).then_inc(S["g_hi"], 1)

            def agg_high(q, t):
                after(act, "mp_ps", q * 8 + t if t else q * 8 - 4)
                act.wait_ge(S["mt_ps"], (mt_count(q, A_AT[t]) if t else a0_count(q)) + 1)
                act.activation(aT[:, 0, :, :], mt_of(q, t).rearrange("p (c n) -> p c n", c=2), ACT.Copy)\
                    .then_inc(S["mt_hi"], 1)

            def x2_high(q, t):
                after(act, "l1_ps", q * 16)
                act.wait_ge(S["mt_ps"], mt_count(q, X_AT[t]) + 1)
                act.activation(x2T[:, 0, :, t * P:t * P + P], mt_of(q, t).rearrange("p (c n) -> p c n", c=2), ACT.Copy)\
                    .then_inc(S["mt_hi"], 1)

            def deviation(q, t):
                act.wait_ge(S["var_ready"], q * TG + (t + 1))
                act.activation(sd2[:, t:t + 1], mv2[:, t, 1:2], ACT.Sqrt, bias=epsc[:P, :]).then_inc(S["std_ready"], 1)

            def norm(q, t):
                act.wait_ge(S["nmr_ready"], q * TG + (t + 1))
                act.activation(xn2[:, t, :], x1[:, t, :], ACT.Identity, bias=nm2[:, t:t + 1],
                               scale=rs2[:, t:t + 1]).then_inc(S["xn2_ready"], 1)

            def softmax(q):
                act.wait_ge(S["r_sub"], q + 1)
                act.activation(lg2[:, :, :], lg[:, :, :], ACT.Exp).then_inc(S["r_exp"], 1)

            def load_weights(e):
                act.dma_start(wraw[:, e, :, :, :], wffn_d[:, e, :, :, :]).then_inc(S[f"w_in{e}"], 16)

            load_weights(1)
            load_weights(2)
            weights_high(0)
            agg_high(0, 0)
            mlp(0)
            for t in range(TG):
                if t < TG - 1:
                    agg_high(0, t + 1)
                deviation(0, t)
                norm(0, t)
                load_weights(t + 3)
                for e in ((), (1,), (2,), (3, 4))[t]:
                    weights_high(e)
            load_weights(7)
            for t in range(TG):
                x2_high(0, t)
                if t == 0:
                    agg_low(TG)
            weights_high(5)
            weights_high(6)
            expert_relu(0, 0, 0)
            expert_high(0, 0, 0)
            softmax(0)
            weights_high(7)

            def group(g, prepare, ahead):
                q = g + 1
                if prepare:
                    agg_high(q, 0)
                    mlp(q)
                expert_relu(0, g, 1)
                expert_relu(1, g, 0, prepare)
                expert_high(0, g, 1)
                expert_high(1, g, 0)
                for e in range(1, EXP - 1):
                    if prepare and e in (1, 3, 5):
                        agg_low(q * TG + (e // 2 + 1))
                    expert_relu(0, g, e + 1)
                    if prepare and e == 6:
                        deviation(q, 3)
                    expert_relu(1, g, e)
                    if prepare and e in NORM_AT:
                        norm(q, NORM_AT[e])
                    if prepare and e == 6:
                        x2_high(q, 0)
                    expert_high(0, g, e + 1)
                    if prepare and e == 6:
                        x2_high(q, 1)
                    expert_high(1, g, e)
                    if prepare:
                        if e in (1, 2, 4):
                            deviation(q, e // 2)
                        if e in (1, 3, 5):
                            agg_high(q, e // 2 + 1)
                if prepare:
                    norm(q, 3)
                    x2_high(q, 2)
                if ahead:
                    agg_low(q * TG + TG)
                expert_relu(1, g, EXP - 1)
                if prepare:
                    x2_high(q, 3)
                expert_high(1, g, EXP - 1)
                if prepare:
                    expert_relu(0, q, 0)
                    expert_high(0, q, 0)
                    softmax(q)

            with act.Fori(0, NG - 2) as g:
                group(g, True, True)
            group(NG - 2, True, False)
            group(NG - 1, False, False)

        @block.vector
        def _(dve):
            n = [0]

            def link(ins):
                n[0] += 1
                ins.then_inc(S["dve_link"], 1)
                dve.wait_ge(S["dve_link"], n[0])

            def row_stats(i):
                dve.wait_ge(S[f"x_in{i}"], 16)
                after(dve, "ln_var", 7 * i)
                for t in range(7):
                    ins = dve.bn_stats(T["bst"][:, t, :], x_all[:, 7 * i + t, :])
                link(ins)
                for t in range(7):
                    dve.bn_aggr(T["mv"][:, 7 * i + t, :], T["bst"][:, t, :]).then_inc(S["ln_var"], 1)

            def row_scales(i):
                w = slice(7 * i, 7 * i + 7)
                dve.wait_ge(S["ln_std"], i + 1)
                link(dve.reciprocal(T["rstd"][:, w], T["rstd"][:, w]))
                dve.scalar_tensor_tensor(out=T["nmr"][:, w], in0=T["mv"][:, w, 0], scalar=-1.0, in1=T["rstd"][:, w],
                                         op0=ALU.mult, op1=ALU.mult).then_inc(S["ln_ready"], 1)

            def one_hots(c, k):
                after(dve, "one_free", c - 1)
                dve.tensor_tensor(oneA[:, k, :, :], iotaA[:, :, :],
                                  ab_f[:, 0, ds(c * CH, CH)].rearrange("p (o m) -> p o m", o=1)
                                  .to_broadcast([EP, CA, CH]), ALU.is_equal).then_inc(S["one_ready"], 1)
                dve.tensor_tensor(oneB[:, k, :, :], iotaB[:, :, :],
                                  ab_f[:, 1, ds(c * CH, CH)].rearrange("p (o m) -> p o m", o=1)
                                  .to_broadcast([EP, CB, CH]), ALU.is_equal).then_inc(S["one_ready"], 1)

            row_stats(0)
            row_stats(1)
            row_scales(0)
            dve.wait_ge(S["edges_in"], 16)
            dve.wait_ge(S["nxt_in"], 16)
            dst = edg[:, :, 1]
            dve.tensor_scalar(ab_i[:, 0, :], dst, 6, None, ALU.logical_shift_right)
            link(dve.tensor_scalar(ab_i[:, 1, :], dst, 63, None, ALU.bitwise_and))
            dve.tensor_copy(ab_f[:, :, :], ab_i[:, :, :])
            link(dve.memset(viol[:, :], 0.0))
            row_stats(2)
            row_scales(1)
            row_stats(3)
            dve.wait_ge(S["consts"], 4)
            one_hots(0, 0)
            row_scales(2)
            one_hots(1, 1)
            dve.tensor_tensor(viol[:, 0:EC - 1], edg[:, 0:EC - 1, 1], edg[:, 1:EC, 1], ALU.is_gt)
            link(dve.tensor_tensor(viol[0:EP - 1, EC - 1:EC], edg[0:EP - 1, EC - 1, 1:2], T["nxt"][0:EP - 1, 1:2],
                                   ALU.is_gt))
            link(dve.reduce_sum(T["vs"][:, 0:1], viol[:, :], axis=AX))
            one_hots(2, 0)
            row_scales(3)
            dve.wait_ge(S["ln_ready"], 4)
            dve.wait_ge(S["consts"], CONSTS)
            dve.tensor_scalar(T["bsc"][:, :], T["rstd"][:, :], T["a1"][:, 0:1], 1.0, ALU.mult, ALU.add)\
                .then_inc(S["bsc_ready"], 1)
            dve.tensor_scalar(T["bbi"][:, :], T["nmr"][:, :], T["a1"][:, 0:1], None, ALU.mult)\
                .then_inc(S["bsc_ready"], 1)
            dve.wait_ge(S["bn_in"], 16)
            bnv = T["bn"]
            dve.tensor_scalar(T["bntmp"][:, :, :, :], bnv[:, :, 4, :, :], BN_EPS, None, ALU.add).then_inc(S["bn_v"], 1)

            with dve.Fori(1, NCH // 2) as i:
                one_hots(i * 2 + 1, 1)
                one_hots(i * 2 + 2, 0)

            dve.wait_ge(S["bn_sd"], 1)
            link(dve.reciprocal(T["bntmp"][:, :, :, :], T["bntmp"][:, :, :, :]))
            link(dve.tensor_tensor(bnsc[:, :, :, :], T["bntmp"][:, :, :, :], bnv[:, :, 1, :, :], ALU.mult))
            link(dve.tensor_tensor(T["bntmp"][:, :, :, :], bnv[:, :, 0, :, :], bnv[:, :, 3, :, :], ALU.subtract))
            link(dve.tensor_tensor(T["bntmp"][:, :, :, :], T["bntmp"][:, :, :, :], bnsc[:, :, :, :], ALU.mult))
            dve.tensor_tensor(bnbi[:, :, :, :], T["bntmp"][:, :, :, :], bnv[:, :, 2, :, :], ALU.add)\
                .then_inc(S["bn_ready"], 1)
            dve.wait_ge(S["wsm_in"], 16)
            for c in range(2):
                wv = wsm[:, c, O_KV:O_KV + 512].rearrange("p (h d) -> p h d", d=HC)
                link(dve.reduce_sum(T["gm"][:, c, :], wv, axis=AX))
                link(dve.tensor_scalar(T["gm"][:, c, :], T["gm"][:, c, :], -1.0 / HC, None, ALU.mult))
                ins = dve.tensor_tensor(wv, wv, bc_in(T["gm"][:, c, :], HC), ALU.add)
                if c == 0:
                    link(ins)
                else:
                    ins.then_inc(S["wkv_ready"], 1)
            brow_v = T["rowv"][0:33, R_BKV:R_BKV + 512].rearrange("p (h d) -> p h d", d=HC)
            link(dve.reduce_sum(T["gb"][:, :], brow_v, axis=AX))
            link(dve.tensor_scalar(T["gb"][:, :], T["gb"][:, :], -1.0 / HC, None, ALU.mult))
            dve.tensor_tensor(T["bkv"][:, :].rearrange("p (h d) -> p h d", d=HC), brow_v, bc_in(T["gb"][:, :], HC),
                              ALU.add).then_inc(S["wkv_ready"], 1)

            dve.wait_ge(S["cnt_in"], 16)
            link(dve.reduce_sum(T["tot"][:, 0:1], T["cnt_t"][:, :], axis=AX))
            dve.tensor_scalar(T["tot"][:, 1:2], T["tot"][:, 0:1], float(WIN), None, ALU.is_gt).then_inc(S["tot_sb"], 1)
            dve.wait_ge(S["cntT_ps"], 1)
            link(dve.tensor_scalar(T["deg"][:, :], CNT[:P, 128:128 + NT], 1.0, None, ALU.add))
            dve.tensor_scalar(T["deg"][:, :], T["deg"][:, :], 1.0, None, ALU.max).then_inc(S["deg_sb"], 1)
            dve.wait_ge(S["start_ps"], 1)
            dve.tensor_scalar(starts[:, :], MSC[0:1, M_ST:M_ST + NT], float(E - WIN), None, ALU.min)\
                .then_inc(S["starts_sb"], 1)
            dve.tensor_scalar(T["stf"][:, :], MSC[0:1, M_ST:M_ST + NT], float(E - WIN), None, ALU.min)\
                .then_inc(S["stf_sb"], 1)
            dve.wait_ge(S["deg_sqrt"], 1)
            link(dve.reciprocal(T["dinv"][:, :], T["deg"][:, :]))
            dve.tensor_scalar(T["dS"][:, :], T["dinv"][:, :], SCALE, None, ALU.mult).then_inc(S["dinv_sb"], 1)
            link(dve.tensor_scalar(T["rstd"][:, :], T["dinv"][:, :], T["a1"][:, 1:2], None, ALU.mult))
            dve.tensor_scalar(rd[:, :], T["rstd"][:, :], 1.0 / SCALE, None, ALU.mult)
            dve.tensor_tensor(ro[:, :], T["dinv"][:, :], T["rstd"][:, :], ALU.mult).then_inc(S["dinv_sb"], 1)
            dve.wait_ge(S["dinv_sb"], 1)

            dve.wait_ge(S["wrest_hi"], 4)
            dve.tensor_tensor(wkv[:, 1, :, :], wsm[:, :, O_KV:O_KV + 512], wkv[:, 0, :, :].bitcast(f32), ALU.subtract)\
                .then_inc(S["wrest_lo"], 1)
            dve.tensor_tensor(bkvs[32:33, :], T["bkv"][32:33, :], T["sq"][32:33, :], ALU.subtract)\
                .then_inc(S["wrest_lo"], 1)

            def table_low(n, slot):
                dve.wait_ge(S["xs_hi"], n + 1)
                for m in range(2):
                    t = n * 2 + m
                    ins = dve.scalar_tensor_tensor(out=tb16[:, slot, m:m + 1, 1, :], in0=xn[:, ds(t, 1), :],
                                                   scalar=T["dS"][:, ds(t, 1)], in1=tb16[:, slot, m:m + 1, 0, :],
                                                   op0=ALU.mult, op1=ALU.subtract)
                ins.then_inc(S["tb_ready"], 1)

            with dve.Fori(0, NT // 2 // TB_SLOTS) as i:
                for slot in range(TB_SLOTS):
                    table_low(i * TB_SLOTS + slot, slot)
            dve.wait_ge(S["flag_ps"], 1)
            dve.tensor_copy(stbc[:, :], MSC[:, M_BC:M_BC + NT])
            dve.tensor_scalar(flag[:, :], MSC[0:1, M_FL:M_FL + 1], 0.5, None, ALU.is_gt).then_inc(S["flag_sb"], 1)

            def kv_low(t, k):
                dve.wait_ge(S["xT_hi"], t + 1)
                dve.tensor_tensor(xT[:, k, 1, :, :], TRP[k % 2][:, 0:2 * P].rearrange("p (c n) -> p c n", c=2),
                                  xT[:, k, 0, :, :].bitcast(f32), ALU.subtract).then_inc(S["xT_lo"], 1)

            def kv_squares(t):
                dve.wait_ge(S["sq_ready"], t + 1)
                dve.reduce_sum(T["s2"][:, 0, :], T["sq"][:, :].rearrange("p (h d) -> p h d", d=HC), axis=AX)\
                    .then_inc(S["s2_ready"], 1)

            def kv_norm(t, k):
                dve.wait_ge(S["sd_ready"], t + 1)
                dve.reciprocal(T["s2"][:, 1, :], T["s2"][:, 1, :]).then_inc(S["dve_loop_link"], 1)
                after(dve, "kv_sum", t - 1)
                after(dve, "v_added", t - 1)
                dve.wait_ge(S["dve_loop_link"], t + 1)
                dve.tensor_tensor(T["kvn"][:, k % 2, :].rearrange("p (a m) -> p a m", a=2)[:, :, 0:D]
                                  .rearrange("p a (h d) -> p a h d", d=HC),
                                  KVP[k % 2][:P, :].rearrange("p (a h d) -> p a h d", a=2, d=HC),
                                  T["s2"][:, 1, :].rearrange("p (a h o) -> p a h o", a=2, o=1)
                                  .to_broadcast([P, 2, NH2 // 2, HC]), ALU.mult).then_inc(S["kn_ready"], 1)

            def v_add(t, k, rows=P):
                dve.wait_ge(S["kn_ready"], t + 1)
                after(dve, "v_added", t)
                dve.tensor_tensor(T["vsum"][:rows, :], T["vsum"][:rows, :], T["kvn"][:rows, k % 2, D + 1:2 * D + 1], ALU.add)\
                    .then_inc(S["v_added"], 1)

            def kv_turn(t, k):
                const = isinstance(t, int)
                if not const or 2 <= t < NT + 2:
                    kv_norm(t - 2, k)
                if not const or t < NT:
                    kv_low(t, k)
                if not const or 1 <= t < NT + 1:
                    kv_squares(t - 1)
                if not const or 2 <= t < NT + 2:
                    v_add(t - 2, k, LAST if const and t - 2 == NT - 1 else P)

            def one_hot(t, half):
                if half == 0:
                    dve.wait_ge(S["win_in"], t * 16 + 16)
                    after(dve, "oh_ready", t * 2)
                    dve.tensor_scalar(dl[:, :], win[:, ds(t, 1), :, 1].rearrange("p o s -> p (o s)"),
                                      tbase[:, ds(t, 1)], None, ALU.subtract).then_inc(S["dl_ready"], 1)
                    dve.wait_ge(S["dl_ready"], t + 1)
                after(dve, "unit_done", t * 2 + (half - 1))
                dve.tensor_tensor(oh[:, half, :, :], iota_rep[:, :, :], bc_out(dl[:, half * US:half * US + US], P),
                                  ALU.is_equal).then_inc(S["oh_ready"], 1)

            def agg_sum(t, dst):
                dve.wait_ge(S["alo_ready"], t + 1)
                dve.scalar_tensor_tensor(out=dst, in0=AGG[:P, 0:D], scalar=rd[:, ds(t, 1)], in1=alo[:, :],
                                         op0=ALU.mult, op1=ALU.add).then_inc(S["agg_evac"], 1)

            dve.sem_inc(S["agg_evac"], 1)
            one_hot(0, 0)
            one_hot(0, 1)
            for t in range(KV_PEEL):
                kv_turn(t, t % XT)
            with dve.Fori(0, KV_LOOP) as j:
                for m in range(KV_BODY):
                    kv_turn(j * KV_BODY + (KV_PEEL + m), (KV_PEEL + m) % XT)
                    if m in UNIT_TURNS:
                        one_hot(j + 1, UNIT_TURNS.index(m))
                agg_sum(j, ags[:, ds(j, 1), :].rearrange("p o d -> p (o d)"))
            for t in range(KV_REST, NT + 2):
                kv_turn(t, t % XT)
                if t - KV_REST in UNIT_TURNS:
                    one_hot(KV_LOOP + 1, UNIT_TURNS.index(t - KV_REST))
                if t == KV_REST + KV_BODY - 1:
                    agg_sum(KV_LOOP, ags[:, KV_LOOP, :])
            dve.wait_ge(S["wrest_hi"], 7)
            for w, o, m in ((wgT, O_WT, D), (w2s, O_W2, D), (wrs, O_WR, EXP)):
                dve.tensor_tensor(w[:, 1, :, :], wsm[:, :, o:o + m], w[:, 0, :, :].bitcast(f32), ALU.subtract)\
                    .then_inc(S["wrest_lo"], 1)
            dve.wait_ge(S["kv_sum"], NT + 1)
            vg, vb = T["rowv"][:, R_VG:R_VG + 128], T["rowv"][:, R_VB:R_VB + 128]
            kg, kb = T["col"][:, 4:5], T["col"][:, 5:6]
            halves = lambda ap: ap.rearrange("p (h d) -> p h d", h=2)
            u, v = T["kvt"][:, 0, :, :], T["kvt"][:, 1, :, :]
            dve.tensor_tensor(u, halves(KA[:, 1:257]), bc_out(vg, 2), ALU.mult)
            link(dve.tensor_tensor(v, halves(KS[:, 0:256]), bc_out(vg, 2), ALU.mult))
            for h in range(2):
                dve.scalar_tensor_tensor(out=u[:, h, :], in0=vb, scalar=KA[:, 257 * h:257 * h + 1], in1=u[:, h, :],
                                         op0=ALU.mult, op1=ALU.add)
            link(dve.scalar_tensor_tensor(out=v, in0=bc_out(vb, 2), scalar=float(N), in1=v, op0=ALU.mult, op1=ALU.add))
            dve.tensor_scalar(u, u, kg, 1.0 / N, ALU.mult, ALU.mult)
            link(dve.tensor_scalar(v, v, kb, 1.0 / N, ALU.mult, ALU.mult))
            for b in range(4):
                w = slice(32 * b, 32 * b + 32)
                ins = dve.tensor_tensor(T["kvs"][w, :, w], T["kvt"][w, 0, :, w], T["kvt"][w, 1, :, w], ALU.add)
            ins.then_inc(S["kvs_sb"], 1)
            one_hot(TG, 0)
            one_hot(TG, 1)
            agg_sum(KV_LOOP + 1, ags[:, KV_LOOP + 1, :])

            dve.wait_ge(S["flag_sb"], 1)
            needed = dve.value_load(flag[0:1, 0:1], min_val=0, max_val=1)
            with dve.If(needed > 0):
                dve.wait_ge(S["base_out"], 64)
                dve.memset(x_all[:, :, :], 0.0).then_inc(S["fb_zero"], 1)
                dve.wait_ge(S["fb_zero"], 1)
                with dve.Fori(0, EC) as j:
                    off, ins_, wt = fb_w[:, 0, :], fb_w[:, 1, :], fb_w[:, 2, :]
                    dve.tensor_copy(fb_d[:, :], edg[:, ds(j, 1), 1]).then_inc(S["fb_link"], 1)
                    dve.tensor_scalar(wt, stbc[:EP, :], posn[:, ds(j, 1)], 0.0, ALU.subtract, ALU.is_le)
                    dve.tensor_scalar(ins_, stbc[:EP, :], posn[:, ds(j, 1)], float(-WIN), ALU.subtract, ALU.is_gt)\
                        .then_inc(S["fb_link"], 1)
                    dve.wait_ge(S["fb_link"], j * 3 + 2)
                    dve.tensor_scalar(off, tbase[:EP, :], fb_d[:, 0:1], -1.0, ALU.subtract, ALU.mult)
                    dve.tensor_tensor(ins_, ins_, wt, ALU.mult).then_inc(S["fb_link"], 1)
                    dve.wait_ge(S["fb_link"], j * 3 + 3)
                    dve.tensor_scalar(wt, ins_, -1.0, 1.0, ALU.mult, ALU.add).then_inc(S["fb_wt"], 1)
                    dve.wait_ge(S["fb_wt"], j + 1)
                    settle(dve)
                    with dve.Fori(0, NT) as t:
                        q = j * NT + t
                        dve.tensor_scalar(fb_o[:, :], iotaP[:EP, :], fb_w[:, 0, ds(t, 1)], fb_w[:, 2, ds(t, 1)],
                                          ALU.is_equal, ALU.mult).then_inc(S["fb_oh"], 1)
                        for half in range(2):
                            if half == 0:
                                dve.wait_ge(S["fb_mm"], q + 2)
                            else:
                                dve.wait_ge(S["fb_sum"], q + 1)
                            xs = x_all[:, ds(t, 1), :].rearrange("p o d -> p (o d)")
                            dve.tensor_tensor(xs, xs, CNT[:P, half * D:half * D + D], ALU.add)\
                                .then_inc(S["fb_sum" if half == 0 else "fb_res"], 1)
                        dve.wait_ge(S["fb_res"], q + 1)
                with dve.Fori(0, NT) as t:
                    dve.tensor_scalar(x_all[:, ds(t, 1), :], x_all[:, ds(t, 1), :], T["deg"][:, ds(t, 1)], 1.0 / SCALE,
                                      ALU.mult, ALU.mult).then_inc(S["fb_scaled"], 1)

            dve.wait_ge(S["rT_ps"], 1)
            for h in range(2):
                link(dve.tensor_copy(T["rT"][:, h, :], TRP[h][:, 0:D]))
                c = slice(128 * h, 128 * h + 128)
                dve.tensor_tensor(T["rT"][:, h, c], T["rT"][:, h, c], ident[:, :], ALU.add).then_inc(S["rT_sb"], 1)
            dve.tensor_copy(T["rb"][:, :], MSC[:, M_CM:M_CM + 2]).then_inc(S["rT_sb"], 1)
            dve.wait_ge(S["wm_ps"], 1)
            dve.wait_ge(S["wm_hi"], 2)
            for c in range(2):
                dve.tensor_tensor(wms[:, 1, c, :], KVP[c][:, 0:D], wms[:, 0, c, :].bitcast(f32), ALU.subtract)\
                    .then_inc(S["wm_lo"], 1)
            dve.tensor_tensor(cm[:, :], MSC[:, M_CM + 2:M_CM + 4], T["col"][:, 2:4], ALU.add).then_inc(S["wm_lo"], 1)

            dve.sem_inc(S["pro_over"], 1)
            dve.wait_ge(S["pro_over"], 3)
            dve.wait_ge(S["fb_over"], 1)
            for k in range(XT):
                dve.wait_ge(S[f"xT_out{k}"], 16 * (NT // XT))

            dve.sem_inc(S["l1_lo"], 1)
            dve.sem_inc(S["l2_lo"], 1)

            def weights_low(e):
                dve.wait_ge(S["w_hi"], e + 1)
                dve.tensor_tensor(wlo[:, e, :, :, :], wst[:, :, :, :] if e == 0 else wraw[:, e, :, :, :],
                                  whi[:, e, :, :, :].bitcast(f32), ALU.subtract).then_inc(S["w_lo"], 1)

            def cut_low(name, g, e):
                buf, hi = ((t1, h1), (t2, h2))[name == "l2"]
                dve.wait_ge(S[name + "_hi"], g * EXP + (e + 1))
                dve.tensor_tensor(hi[:, 1, :, :], buf[:, :, :], hi[:, 0, :, :].bitcast(f32), ALU.subtract)\
                    .then_inc(S[name + "_lo"], 1)

            def mlp(q):
                dve.wait_ge(S["g_hi"], q + 1)
                dve.tensor_tensor(gT[:, 1, :, :], t2[:, :, :], gT[:, 0, :, :].bitcast(f32), ALU.subtract)\
                    .then_inc(S["g_lo"], 1)

            def agg_own(q, t, src):
                if t == 0:
                    after(dve, "mt_ps", mt_count(q - 1, A_AT[3]) + 1)
                else:
                    dve.wait_ge(S["mt_ps"], (mt_count(q, A_AT[t - 1]) if t > 1 else a0_count(q)) + 1)
                dve.wait_ge(S[f"bs_in{t % 2}"], q * 64 + (t // 2 * 32 + 32))
                dve.wait_ge(S["agg_evac"], q * TG + (t + 2))
                dve.scalar_tensor_tensor(out=ag2[:, :], in0=bs[:, t % 2, 1, :], scalar=ro[:, ds(q * TG + t, 1)],
                                         in1=src, op0=ALU.mult, op1=ALU.add).then_inc(S["ag_ready"], 1)

            def agg_add(q, t):
                after(dve, "ag_ready", q * TG + t)
                agg_sum(q * TG + t, ag1[:, :])
                agg_own(q, t, ag1[:, :])

            def agg_cut(q, t):
                dve.wait_ge(S["mt_hi"], q * 8 + (t + 1))
                dve.tensor_tensor(aT[:, 1, :, :], mt_of(q, t).rearrange("p (c n) -> p c n", c=2),
                                  aT[:, 0, :, :].bitcast(f32), ALU.subtract).then_inc(S["mt_lo"], 1)

            def x2_cut(q, t):
                w = slice(t * P, t * P + P)
                dve.wait_ge(S["mt_hi"], q * 8 + (t + 5))
                dve.tensor_tensor(x2T[:, 1, :, w], mt_of(q, t).rearrange("p (c n) -> p c n", c=2),
                                  x2T[:, 0, :, w].bitcast(f32), ALU.subtract).then_inc(S["mt_lo"], 1)

            def residual(q, t):
                dve.wait_ge(S["mp_ps"], q * 8 + (t + 1))
                dve.tensor_tensor(x1[:, t, :], mp_of(q, t), bs[:, t % 2, 0, :], ALU.add).then_inc(S["mp_free"], 1)
                dve.wait_ge(S["mp_free"], q * 8 + (t + 1))
                dve.bn_stats(bst2[:, :], x1[:, t, :]).then_inc(S["st_ready"], 1)
                dve.wait_ge(S["st_ready"], q * TG + (t + 1))
                settle(dve)
                dve.bn_aggr(mv2[:, t, :], bst2[:, :]).then_inc(S["var_ready"], 1)

            def scales(q, t):
                dve.wait_ge(S["std_ready"], q * TG + (t + 1))
                dve.reciprocal(rs2[:, t:t + 1], sd2[:, t:t + 1]).then_inc(S["rs_ready"], 1)
                dve.wait_ge(S["rs_ready"], q * TG + (t + 1))
                dve.scalar_tensor_tensor(out=nm2[:, t:t + 1], in0=mv2[:, t, 0:1], scalar=-1.0, in1=rs2[:, t:t + 1],
                                         op0=ALU.mult, op1=ALU.mult).then_inc(S["nmr_ready"], 1)

            def softmax(q):
                dve.wait_ge(S["r_ps"], q + 1)
                dve.tensor_tensor(lg[:, :, :], ML.rearrange("p (t e) -> p t e", t=TG), bc_out(br_b[:, :], TG), ALU.add)\
                    .then_inc(S["r_lg"], 1)
                dve.wait_ge(S["r_lg"], q + 1)
                dve.reduce_max(mx[:, :], lg[:, :, :], axis=AX).then_inc(S["r_max"], 1)
                dve.wait_ge(S["r_max"], q + 1)
                dve.tensor_tensor(lg[:, :, :], lg[:, :, :], bc_in(mx[:, :], EXP), ALU.subtract)\
                    .then_inc(S["r_sub"], 1)
                dve.wait_ge(S["r_exp"], q + 1)
                dve.reduce_sum(sm[:, :], lg2[:, :, :], axis=AX).then_inc(S["r_sum"], 1)
                dve.wait_ge(S["r_sum"], q * 2 + 1)
                dve.reciprocal(sm[:, :], sm[:, :]).then_inc(S["r_sum"], 1)

            def router_weights(q):
                dve.wait_ge(S["r_sum"], q * 2 + 2)
                after(dve, "y_used", q * (EXP * TG))
                dve.tensor_tensor(wn[:, :, :], lg2[:, :, :], bc_in(sm[:, :], EXP), ALU.mult).then_inc(S["w_ready"], 1)

            def w_transposed(g, last):
                dve.wait_ge(S["mt_ps"], mt_count(g, W_AT - last) + 1)
                dve.tensor_copy(wT[:, :], MT[0:TG * EXP, 0:P]).then_inc(S["mt_lo"], 1)

            def add_bias(g, t):
                dve.wait_ge(S["mp_ps"], g * 8 + (t + 5))
                dve.tensor_tensor(xb[:, t, :], MP, x1[:, t, :], ALU.add).then_inc(S["mp_free"], 1)

            def add_expert(g, e):
                for t in range(TG):
                    i = g * (EXP * TG) + (e * TG + t)
                    if t % 2 == 0:
                        after(dve, "y_ps", i + 2)
                    if e == 0:
                        dve.wait_ge(S["mp_free"], g * 8 + (t + 5))
                        dve.wait_ge(S["w_ready"], g + 1)
                        after(dve, "out_sent", g * 16)
                    else:
                        dve.wait_ge(S["y_used"], i - 3)
                    dve.scalar_tensor_tensor(out=acc[:, t, :], in0=YP[t], scalar=wn[:, t, e:e + 1],
                                             in1=xb[:, t, :] if e == 0 else acc[:, t, :],
                                             op0=ALU.mult, op1=ALU.add).then_inc(S["y_used"], 1)

            agg_own(0, 0, ags[:, 0, :])
            agg_cut(0, 0)
            weights_low(0)
            mlp(0)
            for t in range(TG):
                if t < TG - 1:
                    agg_own(0, t + 1, ags[:, t + 1, :])
                residual(0, t)
                if t < TG - 1:
                    agg_cut(0, t + 1)
                scales(0, t)
                for e in ((), (), (1,), (2, 3))[t]:
                    weights_low(e)
            for t in range(TG):
                x2_cut(0, t)
                if t == 0:
                    agg_add(1, 0)
                    one_hot(TG + 1, 0)
            weights_low(4)
            weights_low(5)
            cut_low("l1", 0, 0)
            softmax(0)
            router_weights(0)
            weights_low(6)
            weights_low(7)

            def group(g, prepare, ahead):
                q = g + 1
                if prepare:
                    agg_cut(q, 0)
                w_transposed(g, int(not prepare))
                if prepare:
                    mlp(q)
                add_bias(g, 0)
                if prepare:
                    one_hot(q * TG + 1, 1)
                add_bias(g, 1)
                cut_low("l1", g, 1)
                cut_low("l2", g, 0)
                for e in range(1, EXP - 1):
                    if e == 1:
                        add_bias(g, 2)
                    if prepare and e < 5:
                        one_hot(q * TG + (e + 3) // 2, (e + 1) % 2)
                    if ahead and e >= 5:
                        one_hot(q * TG + TG, e - 5)
                    if prepare and e in NORM_AT:
                        scales(q, NORM_AT[e])
                    if prepare and e in (1, 3, 5):
                        agg_add(q, e // 2 + 1)
                    if e == 1:
                        add_bias(g, 3)
                    if prepare and e == 6:
                        residual(q, 3)
                    if prepare and e == 6:
                        x2_cut(q, 0)
                    cut_low("l1", g, e + 1)
                    if prepare and e in (1, 2, 4):
                        residual(q, e // 2)
                    if prepare and e == 6:
                        scales(q, 3)
                        x2_cut(q, 1)
                    cut_low("l2", g, e)
                    if prepare and e in (1, 3, 5):
                        agg_cut(q, e // 2 + 1)
                    add_expert(g, e - 1)
                if prepare:
                    x2_cut(q, 2)
                if ahead:
                    agg_add(q + 1, 0)
                    one_hot(q * TG + (TG + 1), 0)
                if prepare:
                    x2_cut(q, 3)
                cut_low("l2", g, EXP - 1)
                add_expert(g, EXP - 2)
                if prepare:
                    cut_low("l1", q, 0)
                    softmax(q)
                add_expert(g, EXP - 1)
                if prepare:
                    router_weights(q)

            with dve.Fori(0, NG - 2) as g:
                group(g, True, True)
            group(NG - 2, True, False)
            group(NG - 1, False, False)

        @block.tensor
        def _(pe):
            def count(c, k, first=False, last=False):
                pe.wait_ge(S["one_ready"], c * 2 + 2)
                for j in range(CH):
                    ins = pe.matmul(CNT[:CA, 0:CB], oneA[:, k, :, j], oneB[:, k, :, j],
                                    start=first and j == 0, stop=last and j == CH - 1, skip_group_check=True)
                ins.then_inc(S["one_free"], 1)

            count(0, 0, first=True)
            with pe.Fori(0, NCH // 2 - 1) as i:
                count(i * 2 + 1, 1)
                count(i * 2 + 2, 0)
            count(NCH - 2, 1)
            count(NCH - 1, 0, last=True)
            pe.wait_ge(S["one_free"], NCH)
            pe.sem_inc(S["cnt_ps"], 1)

            ones = T["ones"]
            pe.wait_ge(S["consts"], CONSTS)
            pe.wait_ge(S["cnt_in"], 16)
            pe.transpose(CNT[:P, 128:128 + NT], T["cnt_t"][:, :], ident[:NT, :NT]).then_inc(S["cntT_ps"], 1)
            pe.wait_ge(S["tot_sb"], 1)
            pe.matmul(MSC[0:1, M_ST:M_ST + NT], T["tot"][:, 0:1], T["ltri"][:, :], start=True, stop=True)\
                .then_inc(S["start_ps"], 1)
            pe.wait_ge(S["stf_sb"], 1)
            pe.matmul(MSC[:, M_BC:M_BC + NT], ones[0:1, :], T["stf"][:, :], start=True, stop=True)
            pe.matmul(MSC[0:1, M_FL:M_FL + 1], T["vs"][:, 0:1], ones[:EP, 0:1], start=True, stop=False)
            pe.matmul(MSC[0:1, M_FL:M_FL + 1], T["tot"][:, 1:2], ones[:NT, 0:1], start=False, stop=True)\
                .then_inc(S["flag_ps"], 1)

            pe.matmul(KA[:, :], fb_z[:, 0:128], fb_z[:, :], start=True, stop=False, skip_group_check=True)
            pe.wait_ge(S["wrest_lo"], 2)

            def kv_transpose(t, k):
                pe.wait_ge(S["xc_ready"], t + 1)
                after(pe, "xT_lo", t - 1)
                for c in range(2):
                    ins = pe.transpose(TRP[k % 2][:, c * P:c * P + P], T["xc"][:, k % 2, 128 * c:128 * c + 128],
                                       ident[:P, :P])
                ins.then_inc(S["tr_ps"], 1)

            def kv_project(t, k):
                pe.wait_ge(S["xT_lo"], t + 1)
                after(pe, "kn_ready", t - 1)
                out = KVP[k % 2][:P, :]
                pe.matmul(out, onesr[:, :], bkvs[:, :], start=True, stop=False)
                for c in range(2):
                    pe.matmul(out, xT[:, k, 0, c, :], wkv[:, 0, c, :], start=False, stop=False)
                    pe.matmul(out, xT[:, k, 0, c, :], wkv[:, 1, c, :], start=False, stop=False)
                    ins = pe.matmul(out, xT[:, k, 1, c, :], wkv[:, 0, c, :], start=False, stop=c == 1)
                ins.then_inc(S["kv_ps"], 1)

            def kv_sum(t, k, rows=P, last=False):
                pe.wait_ge(S["kn_ready"], t + 1)
                kvn = T["kvn"]
                for h in range(2):
                    ins = pe.matmul(KA[:, 129 * h:129 * h + 129], kvn[:rows, k % 2, 128 * h:128 * h + 128],
                                    kvn[:rows, k % 2, D + 129 * h:D + 129 * h + 129], start=False, stop=last,
                                    skip_group_check=True)
                ins.then_inc(S["kv_sum"], 1)

            def kv_turn(t, k):
                const = isinstance(t, int)
                if not const or t < NT:
                    kv_transpose(t, k)
                if not const or 1 <= t <= NT:
                    kv_project(t - 1, (k - 1) % XT)
                if not const or t >= 3:
                    last = const and t - 3 == NT - 1
                    kv_sum(t - 3, (k - 3) % XT, LAST if last else P, last)

            def agg(t, half):
                pe.wait_ge(S[f"gath{half}"], (t + 1) * (US * 16))
                pe.wait_ge(S["oh_ready"], t * 2 + (half + 1))
                if half == 0:
                    pe.wait_ge(S["agg_evac"], t + 1)
                for s in range(US):
                    ins = pe.matmul(AGG[:P, :], oh[:, half, :, s], G[:, half, s, :],
                                    start=half == 0 and s == 0, stop=half == 1 and s == US - 1)
                ins.then_inc(S["unit_done"], 1)

            for t in range(KV_PEEL):
                kv_turn(t, t % XT)
            with pe.Fori(0, KV_LOOP) as j:
                for m in range(KV_BODY):
                    kv_turn(j * KV_BODY + (KV_PEEL + m), (KV_PEEL + m) % XT)
                    if m in UNIT_TURNS:
                        agg(j, UNIT_TURNS.index(m))
            for t in range(KV_REST, NT + 3):
                kv_turn(t, t % XT)
                if t - KV_REST in UNIT_TURNS:
                    agg(KV_LOOP, UNIT_TURNS.index(t - KV_REST))
            pe.wait_ge(S["v_added"], NT)
            pe.matmul(KS[:, 0:D], ones[:P, :], T["vsum"][:, :], start=True, stop=True).then_inc(S["kv_sum"], 1)
            agg(KV_LOOP + 1, 0)
            agg(KV_LOOP + 1, 1)

            pe.wait_ge(S["flag_sb"], 1)
            needed = pe.value_load(flag[0:1, 0:1], min_val=0, max_val=1)
            with pe.If(needed > 0):
                pe.wait_ge(S["agg_evac"], TG + 1)
                pe.sem_inc(S["fb_mm"], 1)
                with pe.Fori(0, EC) as j:
                    pe.wait_ge(S["fb_gath"], (j + 1) * 16)
                    settle(pe)
                    with pe.Fori(0, NT) as t:
                        pe.wait_ge(S["fb_oh"], j * NT + (t + 1))
                        pe.matmul(CNT[:P, :], fb_o[:, :], fb_g[:, :], start=True, stop=True).then_inc(S["fb_mm"], 1)

            pe.wait_ge(S["kvs_sb"], 1)
            pe.wait_ge(S["col_in"], 16)
            for h in range(2):
                pe.matmul(TRP[h][:, 0:D], T["kvs"][:, h, :], wsm[:, h, O_WQ:O_WQ + D], start=True, stop=True)
                ins = pe.matmul(MSC[:, M_CM + h:M_CM + h + 1], T["kvs"][:, h, :], T["col"][:, h:h + 1],
                                start=True, stop=True)
            ins.then_inc(S["rT_ps"], 1)
            pe.wait_ge(S["rT_sb"], 3)
            for c in range(2):
                w = slice(128 * c, 128 * c + 128)
                for h in range(2):
                    pe.matmul(KVP[c][:, 0:D], T["rT"][:, h, w], wsm[:, h, O_W1:O_W1 + D], start=h == 0, stop=h == 1)
                for h in range(2):
                    ins = pe.matmul(MSC[:, M_CM + 2 + c:M_CM + 3 + c], wsm[:, h, O_W1 + 128 * c:O_W1 + 128 * c + 128],
                                    T["rb"][:, h:h + 1], start=h == 0, stop=h == 1)
            ins.then_inc(S["wm_ps"], 1)
            pe.wait_ge(S["wm_lo"], 3)
            pe.wait_ge(S["wrest_lo"], 5)
            pe.sem_inc(S["pro_over"], 1)
            pe.wait_ge(S["bo_in"], 16 * TG)
            pe.wait_ge(S["bn_ready"], 1)

            def three(out, hi, lo, whi_, wlo_):
                return [(whi_, hi), (whi_, lo), (wlo_, hi)]

            pe.sem_inc(S["y_ps"], 1)

            def layer1(g, e):
                m = g * EXP + e
                if e == 0:
                    pe.wait_ge(S["mt_lo"], mt_count(g, X_AT[3]) + 1)
                pe.wait_ge(S["w_lo"], e + 1)
                after(pe, "l1_act", m * 2)
                for c in range(2):
                    w = slice(128 * c, 128 * c + 128)
                    for k in range(2):
                        pe.matmul(H1P[c][:, 0:GN], whi[:, e, 0, k, w], x2T[:, 0, k, :], start=k == 0, stop=False)
                        pe.matmul(H1P[c][:, 0:GN], whi[:, e, 0, k, w], x2T[:, 1, k, :], start=False, stop=False)
                        ins = pe.matmul(H1P[c][:, 0:GN], wlo[:, e, 0, k, w], x2T[:, 0, k, :], start=False, stop=k == 1)
                    ins.then_inc(S["l1_ps"], 1)

            def layer2(g, e, after_mlp=False):
                m = g * EXP + e
                after(pe, "l2_act", m * 2)
                if after_mlp:
                    pe.wait_ge(S["g_act"], g * 2 + 4)
                pe.wait_ge(S["l1_hi"], m + 1)
                for c in range(2):
                    w = slice(128 * c, 128 * c + 128)
                    for k in range(2):
                        pe.matmul(H2P[c][:, 0:GN], whi[:, e, 1, k, w], h1[:, 0, k, :], start=k == 0, stop=False)
                        pe.matmul(H2P[c][:, 0:GN], wlo[:, e, 1, k, w], h1[:, 0, k, :], start=False, stop=False)
                after(pe, "l1_lo", m + 1)
                for c in range(2):
                    w = slice(128 * c, 128 * c + 128)
                    for k in range(2):
                        ins = pe.matmul(H2P[c][:, 0:GN], whi[:, e, 1, k, w], h1[:, 1, k, :], start=False, stop=k == 1)
                    ins.then_inc(S["l2_ps"], 1)

            def layer3(g, e):
                m = g * EXP + e
                pe.wait_ge(S["l2_hi"], m + 1)
                after(pe, "l2_lo", m + 1)
                for t in range(TG):
                    w = slice(t * P, t * P + P)
                    if e and t % 2 == 0:
                        pe.wait_ge(S["y_used"], m * TG + (t - 2))
                    for k in range(2):
                        pe.matmul(YP[t], h2[:, 0, k, w], whi[:, e, 2, k, :], start=k == 0, stop=False)
                        pe.matmul(YP[t], h2[:, 0, k, w], wlo[:, e, 2, k, :], start=False, stop=False)
                        ins = pe.matmul(YP[t], h2[:, 1, k, w], whi[:, e, 2, k, :], start=False, stop=k == 1)
                    ins.then_inc(S["y_ps"], 1)

            def mlp(q):
                pe.wait_ge(S["xg_in"], q * 16 + 16)
                after(pe, "l2_act", (q - 1) * (2 * EXP))
                for c in range(2):
                    w = slice(128 * c, 128 * c + 128)
                    for k in range(2):
                        pe.matmul(H2P[c][:, 0:GN], wms[:, 0, k, w], xg[:, :, 0, k, :], start=k == 0, stop=False)
                        pe.matmul(H2P[c][:, 0:GN], wms[:, 0, k, w], xg[:, :, 1, k, :], start=False, stop=False)
                        ins = pe.matmul(H2P[c][:, 0:GN], wms[:, 1, k, w], xg[:, :, 0, k, :], start=False, stop=k == 1)
                    ins.then_inc(S["g_ps"], 1)

            def small_bank(mt, mp):
                after(pe, "mt_lo", mt)
                after(pe, "mp_free", mp)

            def transposes(src, dst):
                for c in range(2):
                    ins = pe.transpose(dst[:, c * P:c * P + P], src[:, 128 * c:128 * c + 128], ident[:P, :P])
                ins.then_inc(S["mt_ps"], 1)

            def agg_transpose(q, t):
                pe.wait_ge(S["ag_ready"], q * TG + (t + 1))
                if alone(q):
                    after(pe, "mt_lo", t - 1)
                elif t:
                    small_bank(mt_count(q, A_AT[t]), q * 8 + MP_BEFORE[A_AT[t]])
                else:
                    small_bank(a0_count(q), q * 8 - 4)
                    after(pe, "r_lg", q)
                transposes(ag2, mt_of(q, t))

            def x2_transpose(q, t):
                pe.wait_ge(S["xn2_ready"], q * TG + (t + 1))
                if alone(q):
                    pe.wait_ge(S["mt_lo"], mt_count(q, X_AT[t]) - 1)
                else:
                    small_bank(mt_count(q, X_AT[t]), q * 8 + 4)
                transposes(xn2[:, t, :], mt_of(q, t))

            def project(q, t):
                if t == 0:
                    pe.wait_ge(S["g_lo"], q + 1)
                if alone(q):
                    after(pe, "mp_free", t - 1)
                else:
                    small_bank(mt_count(q, t), q * 8 + t)
                w, out = slice(t * P, t * P + P), mp_of(q, t)
                for i, (lhs, at, wts) in enumerate(((gT, w, w2s), (aT, slice(0, P), wgT))):
                    if i and alone(q):
                        pe.wait_ge(S["mt_lo"], t + 1)
                    for k in range(2):
                        pe.matmul(out, lhs[:, 0, k, at], wts[:, 0, k, :], start=k == 0 and i == 0, stop=False)
                        pe.matmul(out, lhs[:, 0, k, at], wts[:, 1, k, :], start=False, stop=False)
                        ins = pe.matmul(out, lhs[:, 1, k, at], wts[:, 0, k, :], start=False, stop=k == 1 and i == 1)
                ins.then_inc(S["mp_ps"], 1)

            def route(q):
                small_bank(mt_count(q, X_AT[3]) + 1, q * 8 + 4)
                for t in range(TG):
                    w = slice(t * P, t * P + P)
                    out = ML[:, EXP * t:EXP * t + EXP]
                    for k in range(2):
                        pe.matmul(out, x2T[:, 0, k, w], wrs[:, 0, k, :], start=k == 0, stop=False)
                        pe.matmul(out, x2T[:, 0, k, w], wrs[:, 1, k, :], start=False, stop=False)
                        ins = pe.matmul(out, x2T[:, 1, k, w], wrs[:, 0, k, :], start=False, stop=k == 1)
                ins.then_inc(S["r_ps"], 1)

            def w_transpose(g, last):
                pe.wait_ge(S["w_ready"], g + 1)
                small_bank(mt_count(g, W_AT - last), g * 8 + 4)
                pe.transpose(MT[0:TG * EXP, 0:P], wn[:, :, :].rearrange("p t e -> p (t e)"), ident[:P, :P])\
                    .then_inc(S["mt_ps"], 1)

            def bias(g, t, last):
                small_bank(mt_count(g, W_AT - last) + 1, g * 8 + (4 + t))
                pe.matmul(MP, wT[:, :], bo4[:, t, :], start=True, stop=True).then_inc(S["mp_ps"], 1)

            agg_transpose(0, 0)
            mlp(0)
            agg(TG, 0)
            for t in range(TG):
                project(0, t)
                if t < TG - 1:
                    agg_transpose(0, t + 1)
                if t == 0:
                    agg(TG, 1)
            for t in range(TG):
                x2_transpose(0, t)
            layer1(0, 0)
            route(0)

            def group(g, prepare, ahead):
                q, last = g + 1, int(not prepare)
                if prepare:
                    agg_transpose(q, 0)
                    agg(q * TG + 1, 0)
                    mlp(q)
                w_transpose(g, last)
                layer1(g, 1)
                bias(g, 0, last)
                layer2(g, 0, prepare)
                bias(g, 1, last)
                for e in range(1, EXP - 1):
                    if prepare and e < 6:
                        agg(q * TG + (e + 2) // 2, e % 2)
                    if ahead and e == 6:
                        agg(q * TG + TG, 0)
                    if e == 1:
                        bias(g, 2, last)
                    layer1(g, e + 1)
                    if e == 1:
                        bias(g, 3, last)
                    if prepare and e == 6:
                        project(q, 3)
                    layer2(g, e)
                    if prepare and e in (1, 2, 4):
                        project(q, e // 2)
                    if prepare and e == 6:
                        x2_transpose(q, 0)
                    layer3(g, e - 1)
                    if prepare and e in (1, 3, 5):
                        agg_transpose(q, e // 2 + 1)
                    if prepare and e == 6:
                        x2_transpose(q, 1)
                if ahead:
                    agg(q * TG + TG, 1)
                if prepare:
                    x2_transpose(q, 2)
                layer2(g, EXP - 1)
                if prepare:
                    x2_transpose(q, 3)
                layer3(g, EXP - 2)
                if prepare:
                    layer1(q, 0)
                    route(q)
                layer3(g, EXP - 1)

            with pe.Fori(0, NG - 2) as g:
                group(g, True, True)
            group(NG - 2, True, False)
            group(NG - 1, False, False)


def kernel(**inputs):
    import concourse.bacc as _bacc
    from concourse.bass_utils import run_bass_kernel_spmd as _run

    a = {k: np.asarray(v) for k, v in inputs.items()}
    x = np.zeros((NP, D), np.float32)
    x[:N] = a["x"]
    edges = np.ascontiguousarray(np.stack([a["src"], a["dst"]], axis=-1))
    w = np.stack([a["L0_ffn_W1"], a["L0_ffn_W2"], a["L0_ffn_Wo"]], axis=1).reshape(EXP, 3, 2, 128, D)
    wffn = np.ascontiguousarray(w.transpose(3, 0, 1, 2, 4))
    bn = np.stack([np.stack([a[f"L0_ffn_{n}{l}"] for n in ("b", "g", "be", "m", "v")]) for l in (1, 2)])
    bn = np.ascontiguousarray(bn.reshape(2, 5, EXP, 2, 128).transpose(4, 0, 1, 2, 3))
    wq, wk, wv = a["L0_mix_w_qkv"].reshape(D, D // HC, 3, HC).transpose(2, 0, 1, 3).reshape(3, D, D)
    bq, bk, bv = a["L0_mix_b_qkv"].reshape(D // HC, 3, HC).transpose(1, 0, 2).reshape(3, D)
    wsm = np.concatenate([a["L0_gnn_W"].T, wk, wv, a["L0_mix_w1"], a["L0_mix_w2"], a["L0_ffn_Wr"], wq.T], axis=1)
    wsm = np.ascontiguousarray(wsm.reshape(2, 128, SW).transpose(1, 0, 2))
    col = np.ascontiguousarray(np.stack([bq[:128], bq[128:], a["L0_mix_b1"][:128], a["L0_mix_b1"][128:],
                                         np.tile(a["L0_mix_kln_g"], 4), np.tile(a["L0_mix_kln_b"], 4)], axis=1))
    row = np.concatenate([np.tile(a["L0_mix_vln_g"], 4), np.tile(a["L0_mix_vln_b"], 4), a["L0_gnn_b"],
                          a["L0_mix_b2"], a["L0_ffn_br"], a["L0_gnn_alpha"], bk, bv])[None]

    nc = _bacc.Bacc("TRN2", target_bir_lowering=False, num_devices=1)
    arrays = dict(x=x, edges=edges, wffn=wffn, bn=bn, wsm=wsm, col=col, row=row, bo=a["L0_ffn_bo"])
    args = [nc.dram_tensor(n + "_in", v.shape, mybir.dt.from_np(v.dtype), kind="ExternalInput").ap()
            for n, v in arrays.items()]
    out = nc.dram_tensor("out", (NP, D), mybir.dt.float32, kind="ExternalOutput").ap()
    build(nc, *args, out)
    r = _run(nc, [{n + "_in": v for n, v in arrays.items()}], core_ids=[0])
    return r.results[0]["out"][:N]
```
